# Optimizing a Trainium2 kernel written in Bass

```python
import numpy as np
import jax
import jax.numpy as jnp

def _softmax(x, axis=-1):
    return jax.nn.softmax(x, axis=axis)

def _gelu(x):
    return jax.nn.gelu(x, approximate=True)

def _silu(x):
    return jax.nn.silu(x)

def _sigmoid(x):
    return jax.nn.sigmoid(x)

def _layernorm(x, axis=-1, eps=1e-05):
    m = jnp.mean(x, axis=axis, keepdims=True)
    v = jnp.var(x, axis=axis, keepdims=True)
    return (x - m) / jnp.sqrt(v + eps)

def _scatter_add(tgt, idx, src, axis=0):
    return tgt.at[idx].add(src)

def _segment_sum(src, seg, n):
    return jax.ops.segment_sum(src, seg, n)
kernel_name = 'mk_decoder_postln_d2_seqx_r8_993a19'

def setup_inputs(seed: int=0):
    np.random.seed(seed)
    _w = jnp.asarray

    def _rec_inputs():
        import jax
        import jax.numpy as jnp
        _rk = jax.random.key(seed)
        x = -0.0002928 + 1 * jax.random.normal(jax.random.fold_in(_rk, 1), (4, 512, 128), jnp.float32)
        _lenS = 512 - jax.random.randint(jax.random.fold_in(_rk, 7), (4,), 0, max(1, 512 // 4) + 1, jnp.int32)
        _lenS2 = 32 - jax.random.randint(jax.random.fold_in(_rk, 8), (4,), 0, max(1, 32 // 4) + 1, jnp.int32)
        _ctx_1024P = jax.random.normal(jax.random.fold_in(_rk, 11), (4, 16, 128), jnp.float32)
        _ctx_1024c = jax.random.dirichlet(jax.random.fold_in(_rk, 511), 0.3 * jnp.ones((16,), jnp.float32), (4, 32))
        _ctx_1024t = jnp.einsum('bsk,bkd->bsd', _ctx_1024c, _ctx_1024P)
        _ctx_1024t = _ctx_1024t * jax.lax.rsqrt(jnp.mean(jnp.square(_ctx_1024t)) + 1e-12) * 0.953939
        ctx_1024 = 4.13588e-05 + 0.999923 * (_ctx_1024t + 0.3 * jax.random.normal(jax.random.fold_in(_rk, 611), (4, 32, 128), jnp.float32))
        return (x, ctx_1024)
    x, ctx_1024 = _rec_inputs()

    def _L0_attn_setup():
        import jax, jax.numpy as jnp
        import numpy as np
        from jax import lax
        D_MODEL = 128
        D_STATE = 16
        D_CONV = 4
        EXPAND = 2
        D_INNER = EXPAND * D_MODEL
        DT_RANK = min(D_MODEL // 16, 64)
        EPS = 1e-05

        def _rmsnorm(x, w):
            var = jnp.mean(x * x, axis=-1, keepdims=True)
            return x * lax.rsqrt(var + EPS) * w

        def _selective_scan(u, delta, A, Bm, Cm, Dv):

            def step(h, inp):
                d_t, b_t, c_t, u_t = inp
                dA = jnp.exp(d_t[..., None] * A)
                dBu = d_t[..., None] * b_t[:, None, :] * u_t[..., None]
                h = dA * h + dBu
                y_t = jnp.einsum('bdn,bn->bd', h, c_t)
                return (h, y_t)
            xs = (jnp.swapaxes(delta, 0, 1), jnp.swapaxes(Bm, 0, 1), jnp.swapaxes(Cm, 0, 1), jnp.swapaxes(u, 0, 1))
            h0 = jnp.zeros((u.shape[0], D_INNER, D_STATE), u.dtype)
            _, ys = lax.scan(step, h0, xs)
            return jnp.swapaxes(ys, 0, 1) + u * Dv
        key = jax.random.key(seed)
        ks = jax.random.split(key, 8)

        def init(k, shape, s=0.02):
            return jax.random.normal(k, shape, jnp.float32) * s
        return {'x': jax.random.normal(ks[0], (8, 256, D_MODEL), jnp.float32), 'norm_w': jnp.ones((D_MODEL,), jnp.float32), 'in_proj_w': init(ks[1], (2 * D_INNER, D_MODEL)), 'conv_w': init(ks[2], (D_INNER, 1, D_CONV), 0.1), 'conv_b': jnp.zeros((D_INNER,), jnp.float32), 'x_proj_w': init(ks[3], (DT_RANK + 2 * D_STATE, D_INNER)), 'dt_proj_w': init(ks[4], (D_INNER, DT_RANK), 0.1), 'dt_proj_b': init(ks[5], (D_INNER,), 0.1), 'A_log': jnp.log(jnp.broadcast_to(jnp.arange(1, D_STATE + 1, dtype=jnp.float32), (D_INNER, D_STATE))), 'D': jnp.ones((D_INNER,), jnp.float32), 'out_proj_w': init(ks[6], (D_MODEL, D_INNER))}
    _L0_attn_all = _L0_attn_setup()
    _L0_attn_in = {k: v for k, v in _L0_attn_all.items() if k in ('norm_w', 'in_proj_w', 'conv_w', 'conv_b', 'x_proj_w', 'dt_proj_w', 'dt_proj_b', 'A_log', 'D', 'out_proj_w')}
    del _L0_attn_all

    def _L0_xattn_setup():
        import jax, jax.numpy as jnp
        import numpy as np
        DIM = 128
        NUM_HEADS = 16
        DIM_HEAD = 64
        INNER = NUM_HEADS * DIM_HEAD
        SCALE = DIM_HEAD ** (-0.5)

        def _layernorm(x, gamma, beta, eps=1e-05):
            mu = jnp.mean(x, axis=-1, keepdims=True)
            var = jnp.mean(jnp.square(x - mu), axis=-1, keepdims=True)
            return (x - mu) * jax.lax.rsqrt(var + eps) * gamma + beta
        key = jax.random.key(seed)
        ks = jax.random.split(key, 8)
        B, SQ, SK = (2, 256, 512)
        x = jax.random.normal(ks[0], (B, SQ, DIM), dtype=jnp.float32)
        context = jax.random.normal(ks[1], (B, SK, DIM), dtype=jnp.float32)
        ln_gamma = jnp.ones((DIM,), jnp.float32)
        ln_beta = jnp.zeros((DIM,), jnp.float32)
        w_q = jax.random.normal(ks[2], (DIM, INNER), dtype=jnp.float32) / np.sqrt(DIM)
        w_kv = jax.random.normal(ks[3], (DIM, 2 * INNER), dtype=jnp.float32) / np.sqrt(DIM)
        w_out = jax.random.normal(ks[4], (INNER, DIM), dtype=jnp.float32) / np.sqrt(INNER)
        b_out = jnp.zeros((DIM,), jnp.float32)
        gate = jnp.array([0.5], jnp.float32)
        return {'x': x, 'context': context, 'ln_gamma': ln_gamma, 'ln_beta': ln_beta, 'w_q': w_q, 'w_kv': w_kv, 'w_out': w_out, 'b_out': b_out, 'gate': gate}
    _L0_xattn_all = _L0_xattn_setup()
    _L0_xattn_in = {k: v for k, v in _L0_xattn_all.items() if k in ('ln_gamma', 'ln_beta', 'w_q', 'w_kv', 'w_out', 'b_out', 'gate')}
    del _L0_xattn_all

    def _L0_ffn_setup():
        import jax, jax.numpy as jnp
        import numpy as np
        D_MODEL = 128
        D_FF = 512
        N_EXPERTS = 8
        TOP_K = 2

        def _ffn(x, w1, b1, w2, b2):
            h = jax.nn.gelu(x @ w1.T + b1)
            return h @ w2.T + b2
        key = jax.random.key(seed)
        ks = jax.random.split(key, 12)
        s = 0.02
        x = jax.random.normal(ks[0], (4, 256, D_MODEL), dtype=jnp.float32)
        shared_w1 = jax.random.normal(ks[1], (D_FF, D_MODEL), dtype=jnp.float32) * s
        shared_b1 = jnp.zeros((D_FF,), dtype=jnp.float32)
        shared_w2 = jax.random.normal(ks[2], (D_MODEL, D_FF), dtype=jnp.float32) * s
        shared_b2 = jnp.zeros((D_MODEL,), dtype=jnp.float32)
        router_w = jax.random.normal(ks[3], (N_EXPERTS, D_MODEL), dtype=jnp.float32) * s
        router_b = jnp.zeros((N_EXPERTS,), dtype=jnp.float32)
        spec_w1 = jax.random.normal(ks[4], (N_EXPERTS, D_FF, D_MODEL), dtype=jnp.float32) * s
        spec_b1 = jnp.zeros((N_EXPERTS, D_FF), dtype=jnp.float32)
        spec_w2 = jax.random.normal(ks[5], (N_EXPERTS, D_MODEL, D_FF), dtype=jnp.float32) * s
        spec_b2 = jnp.zeros((N_EXPERTS, D_MODEL), dtype=jnp.float32)
        return dict(x=x, shared_w1=shared_w1, shared_b1=shared_b1, shared_w2=shared_w2, shared_b2=shared_b2, router_w=router_w, router_b=router_b, spec_w1=spec_w1, spec_b1=spec_b1, spec_w2=spec_w2, spec_b2=spec_b2)
    _L0_ffn_all = _L0_ffn_setup()
    _L0_ffn_in = {k: v for k, v in _L0_ffn_all.items() if k in ('shared_w1', 'shared_b1', 'shared_w2', 'shared_b2', 'router_w', 'router_b', 'spec_w1', 'spec_b1', 'spec_w2', 'spec_b2')}
    del _L0_ffn_all

    def _L1_attn_setup():
        import jax, jax.numpy as jnp
        import numpy as np
        D_MODEL = 128
        N_HEADS = 16
        HEAD_DIM = D_MODEL // N_HEADS
        WINDOW = 128
        ROPE_BASE = 10000.0

        def _rope_cos_sin(T, dim, dtype):
            inv_freq = 1.0 / ROPE_BASE ** (jnp.arange(0, dim, 2, dtype=jnp.float32) / dim)
            freqs = jnp.arange(T, dtype=jnp.float32)[:, None] * inv_freq[None, :]
            emb = jnp.concatenate([freqs, freqs], axis=-1)
            return (jnp.cos(emb).astype(dtype), jnp.sin(emb).astype(dtype))

        def _rotate_half(x):
            h = x.shape[-1] // 2
            return jnp.concatenate([-x[..., h:], x[..., :h]], axis=-1)

        def _apply_rotary(x, cos, sin):
            c = cos[None, :, None, :]
            s = sin[None, :, None, :]
            return x * c + _rotate_half(x) * s
        key = jax.random.key(seed)
        ks = jax.random.split(key, 6)
        B, T = (2, 256)
        query = jax.random.normal(ks[0], (B, T, D_MODEL), dtype=jnp.float32)
        scale = 1.0 / np.sqrt(D_MODEL)
        Wq = jax.random.normal(ks[1], (D_MODEL, D_MODEL), dtype=jnp.float32) * scale
        Wk = jax.random.normal(ks[2], (D_MODEL, D_MODEL), dtype=jnp.float32) * scale
        Wv = jax.random.normal(ks[3], (D_MODEL, D_MODEL), dtype=jnp.float32) * scale
        Wo = jax.random.normal(ks[4], (D_MODEL, D_MODEL), dtype=jnp.float32) * scale
        bo = jax.random.normal(ks[5], (D_MODEL,), dtype=jnp.float32) * 0.01
        return {'query': query, 'Wq': Wq, 'Wk': Wk, 'Wv': Wv, 'Wo': Wo, 'bo': bo}
    _L1_attn_all = _L1_attn_setup()
    _L1_attn_in = {k: v for k, v in _L1_attn_all.items() if k in ('Wq', 'Wk', 'Wv', 'Wo', 'bo')}
    del _L1_attn_all

    def _L1_xattn_setup():
        import jax, jax.numpy as jnp
        import numpy as np
        HIDDEN = 128
        NUM_HEADS = 16
        HEAD_DIM = HIDDEN // NUM_HEADS
        key = jax.random.key(seed)
        k1, k2, k3, k4, k5, k6 = jax.random.split(key, 6)
        B, SQ, SKV = (4, 128, 256)
        s = HIDDEN ** (-0.5)
        return {'xq': jax.random.normal(k1, (B, SQ, HIDDEN), jnp.float32), 'xkv': jax.random.normal(k2, (B, SKV, HIDDEN), jnp.float32), 'Wq': jax.random.normal(k3, (HIDDEN, HIDDEN), jnp.float32) * s, 'Wkv': jax.random.normal(k4, (2 * HIDDEN, HIDDEN), jnp.float32) * s, 'Wout': jax.random.normal(k5, (HIDDEN, HIDDEN), jnp.float32) * s, 'bout': jax.random.normal(k6, (HIDDEN,), jnp.float32) * 0.01}
    _L1_xattn_all = _L1_xattn_setup()
    _L1_xattn_in = {k: v for k, v in _L1_xattn_all.items() if k in ('Wq', 'Wkv', 'Wout', 'bout')}
    del _L1_xattn_all

    def _L1_ffn_setup():
        import jax, jax.numpy as jnp
        import numpy as np
        DIM = 128
        DEPTH = 2
        HEADS = 8
        DIM_HEAD = 64
        WINDOW = 64
        INNER = HEADS * DIM_HEAD
        HID = int(DIM * 4 * 2 / 3)
        B, N = (2, 1024)
        QK_SCALE = 8.0

        def shift_token(t):
            t1, t2 = jnp.split(t, 2, axis=-1)
            t2 = jnp.pad(t2, ((0, 0), (1, 0), (0, 0)))[:, :-1]
            return jnp.concatenate([t1, t2], axis=-1)

        def l2norm(t):
            return t / jnp.clip(jnp.linalg.norm(t, axis=-1, keepdims=True), 1e-12)

        def rotate_half(x):
            x1, x2 = jnp.split(x, 2, axis=-1)
            return jnp.concatenate([-x2, x1], axis=-1)

        def rotary_xpos(q, k):
            n = q.shape[-2]
            half_idx = jnp.arange(0, DIM_HEAD, 2, dtype=jnp.float32)
            inv_freq = 1.0 / 10000.0 ** (half_idx / DIM_HEAD)
            t = jnp.arange(n, dtype=jnp.float32)
            freqs = t[:, None] * inv_freq[None, :]
            freqs = jnp.concatenate([freqs, freqs], axis=-1)
            base = (half_idx + 0.4 * DIM_HEAD) / (1.4 * DIM_HEAD)
            power = (t - n // 2) / float(WINDOW // 2)
            scale = base[None, :] ** power[:, None]
            scale = jnp.concatenate([scale, scale], axis=-1)
            cos, sin = (jnp.cos(freqs), jnp.sin(freqs))
            q = q * cos * scale + rotate_half(q) * sin * scale
            k = k * cos / scale + rotate_half(k) * sin / scale
            return (q, k)

        def local_attention(q, k, v):
            b, h, n, d = q.shape
            w = n // WINDOW
            bq = q.reshape(b, h, w, WINDOW, d) * QK_SCALE
            bk = k.reshape(b, h, w, WINDOW, d)
            bv = v.reshape(b, h, w, WINDOW, d)

            def look_around(t):
                p = jnp.pad(t, ((0, 0), (0, 0), (1, 0), (0, 0), (0, 0)))
                return jnp.concatenate([p[:, :, :w], p[:, :, 1:]], axis=3)
            bk, bv = (look_around(bk), look_around(bv))
            bt = jnp.arange(n).reshape(w, WINDOW)
            btp = jnp.pad(bt, ((1, 0), (0, 0)), constant_values=-1)
            btk = jnp.concatenate([btp[:w], btp[1:]], axis=1)
            sim = jnp.einsum('bhwid,bhwjd->bhwij', bq, bk)
            i = bt[:, :, None]
            j = btk[:, None, :]
            mask = (i < j) | (i > j + WINDOW) | (j == -1)
            sim = jnp.where(mask, -jnp.finfo(sim.dtype).max, sim)
            attn = jax.nn.softmax(sim, axis=-1)
            out = jnp.einsum('bhwij,bhwjd->bhwid', attn, bv)
            return out.reshape(b, h, n, d)

        def _layer(x, wqkv, qs, ksc, wo, lg, lb, w1, b1, w2, b2):
            b, n, _ = x.shape
            h = shift_token(x)
            qkv = h @ wqkv
            q, k, v = jnp.split(qkv, 3, axis=-1)
            to_heads = lambda t: t.reshape(b, n, HEADS, DIM_HEAD).transpose(0, 2, 1, 3)
            q, k, v = (to_heads(q), to_heads(k), to_heads(v))
            q = l2norm(q) * qs
            k = l2norm(k) * ksc
            q, k = rotary_xpos(q, k)
            o = local_attention(q, k, v)
            o = o.transpose(0, 2, 1, 3).reshape(b, n, INNER)
            x = x + o @ wo
            h = shift_token(x)
            mu = h.mean(-1, keepdims=True)
            var = h.var(-1, keepdims=True)
            h = (h - mu) / jnp.sqrt(var + 1e-05) * lg + lb
            h = h @ w1 + b1
            a, g = jnp.split(h, 2, axis=-1)
            h = a * jax.nn.gelu(g, approximate=False)
            x = x + h @ w2 + b2
            return x
        key = jax.random.key(seed)
        ks = jax.random.split(key, 6)
        return {'x': jax.random.normal(ks[0], (B, N, DIM), jnp.float32), 'wqkv': jax.random.normal(ks[1], (DEPTH, DIM, 3 * INNER), jnp.float32) * 0.02, 'q_scale': jnp.ones((DEPTH, DIM_HEAD), jnp.float32), 'k_scale': jnp.ones((DEPTH, DIM_HEAD), jnp.float32), 'wo': jax.random.normal(ks[2], (DEPTH, INNER, DIM), jnp.float32) * 0.02, 'ln_g': jnp.ones((DEPTH, DIM), jnp.float32), 'ln_b': jnp.zeros((DEPTH, DIM), jnp.float32), 'w1': jax.random.normal(ks[3], (DEPTH, DIM, 2 * HID), jnp.float32) * 0.02, 'b1': jnp.zeros((DEPTH, 2 * HID), jnp.float32), 'w2': jax.random.normal(ks[4], (DEPTH, HID, DIM), jnp.float32) * 0.02, 'b2': jnp.zeros((DEPTH, DIM), jnp.float32)}
    _L1_ffn_all = _L1_ffn_setup()
    _L1_ffn_in = {k: v for k, v in _L1_ffn_all.items() if k in ('wqkv', 'q_scale', 'k_scale', 'wo', 'ln_g', 'ln_b', 'w1', 'b1', 'w2', 'b2')}
    del _L1_ffn_all
    return {'x': x, 'ctx_1024': ctx_1024, 'L0_attn_norm_w': _L0_attn_in['norm_w'], 'L0_attn_in_proj_w': _L0_attn_in['in_proj_w'], 'L0_attn_conv_w': _L0_attn_in['conv_w'], 'L0_attn_conv_b': _L0_attn_in['conv_b'], 'L0_attn_x_proj_w': _L0_attn_in['x_proj_w'], 'L0_attn_dt_proj_w': _L0_attn_in['dt_proj_w'], 'L0_attn_dt_proj_b': _L0_attn_in['dt_proj_b'], 'L0_attn_A_log': _L0_attn_in['A_log'], 'L0_attn_D': _L0_attn_in['D'], 'L0_attn_out_proj_w': _L0_attn_in['out_proj_w'], 'L0_xattn_ln_gamma': _L0_xattn_in['ln_gamma'], 'L0_xattn_ln_beta': _L0_xattn_in['ln_beta'], 'L0_xattn_w_q': _L0_xattn_in['w_q'], 'L0_xattn_w_kv': _L0_xattn_in['w_kv'], 'L0_xattn_w_out': _L0_xattn_in['w_out'], 'L0_xattn_b_out': _L0_xattn_in['b_out'], 'L0_xattn_gate': _L0_xattn_in['gate'], 'L0_ffn_shared_w1': _L0_ffn_in['shared_w1'], 'L0_ffn_shared_b1': _L0_ffn_in['shared_b1'], 'L0_ffn_shared_w2': _L0_ffn_in['shared_w2'], 'L0_ffn_shared_b2': _L0_ffn_in['shared_b2'], 'L0_ffn_router_w': _L0_ffn_in['router_w'], 'L0_ffn_router_b': _L0_ffn_in['router_b'], 'L0_ffn_spec_w1': _L0_ffn_in['spec_w1'], 'L0_ffn_spec_b1': _L0_ffn_in['spec_b1'], 'L0_ffn_spec_w2': _L0_ffn_in['spec_w2'], 'L0_ffn_spec_b2': _L0_ffn_in['spec_b2'], 'L1_attn_Wq': _L1_attn_in['Wq'], 'L1_attn_Wk': _L1_attn_in['Wk'], 'L1_attn_Wv': _L1_attn_in['Wv'], 'L1_attn_Wo': _L1_attn_in['Wo'], 'L1_attn_bo': _L1_attn_in['bo'], 'L1_xattn_Wq': _L1_xattn_in['Wq'], 'L1_xattn_Wkv': _L1_xattn_in['Wkv'], 'L1_xattn_Wout': _L1_xattn_in['Wout'], 'L1_xattn_bout': _L1_xattn_in['bout'], 'L1_ffn_wqkv': _L1_ffn_in['wqkv'], 'L1_ffn_q_scale': _L1_ffn_in['q_scale'], 'L1_ffn_k_scale': _L1_ffn_in['k_scale'], 'L1_ffn_wo': _L1_ffn_in['wo'], 'L1_ffn_ln_g': _L1_ffn_in['ln_g'], 'L1_ffn_ln_b': _L1_ffn_in['ln_b'], 'L1_ffn_w1': _L1_ffn_in['w1'], 'L1_ffn_b1': _L1_ffn_in['b1'], 'L1_ffn_w2': _L1_ffn_in['w2'], 'L1_ffn_b2': _L1_ffn_in['b2']}

def reference(x, ctx_1024, L0_attn_norm_w, L0_attn_in_proj_w, L0_attn_conv_w, L0_attn_conv_b, L0_attn_x_proj_w, L0_attn_dt_proj_w, L0_attn_dt_proj_b, L0_attn_A_log, L0_attn_D, L0_attn_out_proj_w, L0_xattn_ln_gamma, L0_xattn_ln_beta, L0_xattn_w_q, L0_xattn_w_kv, L0_xattn_w_out, L0_xattn_b_out, L0_xattn_gate, L0_ffn_shared_w1, L0_ffn_shared_b1, L0_ffn_shared_w2, L0_ffn_shared_b2, L0_ffn_router_w, L0_ffn_router_b, L0_ffn_spec_w1, L0_ffn_spec_b1, L0_ffn_spec_w2, L0_ffn_spec_b2, L1_attn_Wq, L1_attn_Wk, L1_attn_Wv, L1_attn_Wo, L1_attn_bo, L1_xattn_Wq, L1_xattn_Wkv, L1_xattn_Wout, L1_xattn_bout, L1_ffn_wqkv, L1_ffn_q_scale, L1_ffn_k_scale, L1_ffn_wo, L1_ffn_ln_g, L1_ffn_ln_b, L1_ffn_w1, L1_ffn_b1, L1_ffn_w2, L1_ffn_b2):
    import jax
    import jax.numpy as jnp

    def _L0_attn_ref(x, norm_w, in_proj_w, conv_w, conv_b, x_proj_w, dt_proj_w, dt_proj_b, A_log, D, out_proj_w):
        import jax, jax.numpy as jnp
        import numpy as np
        from jax import lax
        D_MODEL = 128
        D_STATE = 16
        D_CONV = 4
        EXPAND = 2
        D_INNER = EXPAND * D_MODEL
        DT_RANK = min(D_MODEL // 16, 64)
        EPS = 1e-05

        def _rmsnorm(x, w):
            var = jnp.mean(x * x, axis=-1, keepdims=True)
            return x * lax.rsqrt(var + EPS) * w

        def _selective_scan(u, delta, A, Bm, Cm, Dv):

            def step(h, inp):
                d_t, b_t, c_t, u_t = inp
                dA = jnp.exp(d_t[..., None] * A)
                dBu = d_t[..., None] * b_t[:, None, :] * u_t[..., None]
                h = dA * h + dBu
                y_t = jnp.einsum('bdn,bn->bd', h, c_t)
                return (h, y_t)
            xs = (jnp.swapaxes(delta, 0, 1), jnp.swapaxes(Bm, 0, 1), jnp.swapaxes(Cm, 0, 1), jnp.swapaxes(u, 0, 1))
            h0 = jnp.zeros((u.shape[0], D_INNER, D_STATE), u.dtype)
            _, ys = lax.scan(step, h0, xs)
            return jnp.swapaxes(ys, 0, 1) + u * Dv
        residual = x
        xn = _rmsnorm(x, norm_w)
        xz = xn @ in_proj_w.T
        x_part, z = jnp.split(xz, 2, axis=-1)
        xc = lax.conv_general_dilated(jnp.swapaxes(x_part, 1, 2), conv_w, window_strides=(1,), padding=((D_CONV - 1, 0),), feature_group_count=D_INNER, dimension_numbers=('NCH', 'OIH', 'NCH'))
        xc = jnp.swapaxes(xc + conv_b[None, :, None], 1, 2)
        u = jax.nn.silu(xc)
        x_dbl = u @ x_proj_w.T
        dt, Bm, Cm = jnp.split(x_dbl, [DT_RANK, DT_RANK + D_STATE], axis=-1)
        delta = jax.nn.softplus(dt @ dt_proj_w.T + dt_proj_b)
        A = -jnp.exp(A_log)
        y = _selective_scan(u, delta, A, Bm, Cm, D)
        y = y * jax.nn.silu(z)
        out = y @ out_proj_w.T
        return out + residual

    def _L0_xattn_ref(x, context, ln_gamma, ln_beta, w_q, w_kv, w_out, b_out, gate):
        import jax, jax.numpy as jnp
        import numpy as np
        DIM = 128
        NUM_HEADS = 16
        DIM_HEAD = 64
        INNER = NUM_HEADS * DIM_HEAD
        SCALE = DIM_HEAD ** (-0.5)

        def _layernorm(x, gamma, beta, eps=1e-05):
            mu = jnp.mean(x, axis=-1, keepdims=True)
            var = jnp.mean(jnp.square(x - mu), axis=-1, keepdims=True)
            return (x - mu) * jax.lax.rsqrt(var + eps) * gamma + beta
        B, SQ, _ = x.shape
        SK = context.shape[1]
        xn = _layernorm(x, ln_gamma, ln_beta)
        q = (xn @ w_q).reshape(B, SQ, NUM_HEADS, DIM_HEAD)
        kv = context @ w_kv
        k, v = jnp.split(kv, 2, axis=-1)
        k = k.reshape(B, SK, NUM_HEADS, DIM_HEAD)
        v = v.reshape(B, SK, NUM_HEADS, DIM_HEAD)
        scores = jnp.einsum('bqhd,bkhd->bhqk', q * SCALE, k)
        attn = jax.nn.softmax(scores, axis=-1)
        out = jnp.einsum('bhqk,bkhd->bqhd', attn, v).reshape(B, SQ, INNER)
        out = out @ w_out + b_out
        return out * jnp.tanh(gate[0])

    def _L0_ffn_ref(x, shared_w1, shared_b1, shared_w2, shared_b2, router_w, router_b, spec_w1, spec_b1, spec_w2, spec_b2):
        import jax, jax.numpy as jnp
        import numpy as np
        D_MODEL = 128
        D_FF = 512
        N_EXPERTS = 8
        TOP_K = 2

        def _ffn(x, w1, b1, w2, b2):
            h = jax.nn.gelu(x @ w1.T + b1)
            return h @ w2.T + b2
        B, T, D = x.shape
        xf = x.reshape(-1, D)
        U = xf.shape[0]
        logits = xf @ router_w.T + router_b
        routing = jax.nn.softmax(logits, axis=-1)
        sel_w, sel_idx = jax.lax.top_k(routing, TOP_K)
        sel_w = sel_w / sel_w.sum(axis=-1, keepdims=True)
        comb = jnp.zeros_like(routing).at[jnp.arange(U)[:, None], sel_idx].set(sel_w)
        shared_out = _ffn(xf, shared_w1, shared_b1, shared_w2, shared_b2)

        def body(acc, params):
            w1, b1, w2, b2, we = params
            return (acc + we[:, None] * _ffn(xf, w1, b1, w2, b2), None)
        acc0 = jnp.zeros_like(shared_out)
        acc, _ = jax.lax.scan(body, acc0, (spec_w1, spec_b1, spec_w2, spec_b2, comb.T))
        return (shared_out + acc).reshape(B, T, D)

    def _L1_attn_ref(query, Wq, Wk, Wv, Wo, bo):
        import jax, jax.numpy as jnp
        import numpy as np
        D_MODEL = 128
        N_HEADS = 16
        HEAD_DIM = D_MODEL // N_HEADS
        WINDOW = 128
        ROPE_BASE = 10000.0

        def _rope_cos_sin(T, dim, dtype):
            inv_freq = 1.0 / ROPE_BASE ** (jnp.arange(0, dim, 2, dtype=jnp.float32) / dim)
            freqs = jnp.arange(T, dtype=jnp.float32)[:, None] * inv_freq[None, :]
            emb = jnp.concatenate([freqs, freqs], axis=-1)
            return (jnp.cos(emb).astype(dtype), jnp.sin(emb).astype(dtype))

        def _rotate_half(x):
            h = x.shape[-1] // 2
            return jnp.concatenate([-x[..., h:], x[..., :h]], axis=-1)

        def _apply_rotary(x, cos, sin):
            c = cos[None, :, None, :]
            s = sin[None, :, None, :]
            return x * c + _rotate_half(x) * s
        B, T, D = query.shape
        H, Dh = (N_HEADS, HEAD_DIM)
        sm_scale = Dh ** (-0.5)
        q = (query @ Wq.T).reshape(B, T, H, Dh)
        k = (query @ Wk.T).reshape(B, T, H, Dh)
        v = (query @ Wv.T).reshape(B, T, H, Dh)
        cos, sin = _rope_cos_sin(T, Dh, query.dtype)
        q = _apply_rotary(q, cos, sin)
        k = _apply_rotary(k, cos, sin)
        q = q.transpose(0, 2, 1, 3)
        k = k.transpose(0, 2, 1, 3)
        v = v.transpose(0, 2, 1, 3)
        scores = jnp.einsum('bhqd,bhkd->bhqk', q, k) * sm_scale
        i = jnp.arange(T)[:, None]
        j = jnp.arange(T)[None, :]
        mask = (j > i) | (j < i - (WINDOW - 1))
        scores = jnp.where(mask[None, None], jnp.float32(-jnp.inf), scores)
        attn = jax.nn.softmax(scores, axis=-1)
        out = jnp.einsum('bhqk,bhkd->bhqd', attn, v)
        out = out.transpose(0, 2, 1, 3).reshape(B, T, D)
        return out @ Wo.T + bo

    def _L1_xattn_ref(xq, xkv, Wq, Wkv, Wout, bout):
        import jax, jax.numpy as jnp
        import numpy as np
        HIDDEN = 128
        NUM_HEADS = 16
        HEAD_DIM = HIDDEN // NUM_HEADS
        B, SQ, H = xq.shape
        SKV = xkv.shape[1]
        scale = HEAD_DIM ** (-0.5)
        q = (xq @ Wq.T).reshape(B, SQ, NUM_HEADS, HEAD_DIM)
        kv = (xkv @ Wkv.T).reshape(B, SKV, 2, NUM_HEADS, HEAD_DIM)
        k, v = (kv[:, :, 0], kv[:, :, 1])
        att = jax.nn.softmax(jnp.einsum('bxhd,byhd->bhxy', q, k) * scale, axis=-1)
        x = jnp.einsum('bhxy,byhd->bxhd', att, v).reshape(B, SQ, H)
        return x @ Wout.T + bout

    def _L1_ffn_ref(x, wqkv, q_scale, k_scale, wo, ln_g, ln_b, w1, b1, w2, b2):
        import jax, jax.numpy as jnp
        import numpy as np
        DIM = 128
        DEPTH = 2
        HEADS = 8
        DIM_HEAD = 64
        WINDOW = 64
        INNER = HEADS * DIM_HEAD
        HID = int(DIM * 4 * 2 / 3)
        B, N = (2, 1024)
        QK_SCALE = 8.0

        def shift_token(t):
            t1, t2 = jnp.split(t, 2, axis=-1)
            t2 = jnp.pad(t2, ((0, 0), (1, 0), (0, 0)))[:, :-1]
            return jnp.concatenate([t1, t2], axis=-1)

        def l2norm(t):
            return t / jnp.clip(jnp.linalg.norm(t, axis=-1, keepdims=True), 1e-12)

        def rotate_half(x):
            x1, x2 = jnp.split(x, 2, axis=-1)
            return jnp.concatenate([-x2, x1], axis=-1)

        def rotary_xpos(q, k):
            n = q.shape[-2]
            half_idx = jnp.arange(0, DIM_HEAD, 2, dtype=jnp.float32)
            inv_freq = 1.0 / 10000.0 ** (half_idx / DIM_HEAD)
            t = jnp.arange(n, dtype=jnp.float32)
            freqs = t[:, None] * inv_freq[None, :]
            freqs = jnp.concatenate([freqs, freqs], axis=-1)
            base = (half_idx + 0.4 * DIM_HEAD) / (1.4 * DIM_HEAD)
            power = (t - n // 2) / float(WINDOW // 2)
            scale = base[None, :] ** power[:, None]
            scale = jnp.concatenate([scale, scale], axis=-1)
            cos, sin = (jnp.cos(freqs), jnp.sin(freqs))
            q = q * cos * scale + rotate_half(q) * sin * scale
            k = k * cos / scale + rotate_half(k) * sin / scale
            return (q, k)

        def local_attention(q, k, v):
            b, h, n, d = q.shape
            w = n // WINDOW
            bq = q.reshape(b, h, w, WINDOW, d) * QK_SCALE
            bk = k.reshape(b, h, w, WINDOW, d)
            bv = v.reshape(b, h, w, WINDOW, d)

            def look_around(t):
                p = jnp.pad(t, ((0, 0), (0, 0), (1, 0), (0, 0), (0, 0)))
                return jnp.concatenate([p[:, :, :w], p[:, :, 1:]], axis=3)
            bk, bv = (look_around(bk), look_around(bv))
            bt = jnp.arange(n).reshape(w, WINDOW)
            btp = jnp.pad(bt, ((1, 0), (0, 0)), constant_values=-1)
            btk = jnp.concatenate([btp[:w], btp[1:]], axis=1)
            sim = jnp.einsum('bhwid,bhwjd->bhwij', bq, bk)
            i = bt[:, :, None]
            j = btk[:, None, :]
            mask = (i < j) | (i > j + WINDOW) | (j == -1)
            sim = jnp.where(mask, -jnp.finfo(sim.dtype).max, sim)
            attn = jax.nn.softmax(sim, axis=-1)
            out = jnp.einsum('bhwij,bhwjd->bhwid', attn, bv)
            return out.reshape(b, h, n, d)

        def _layer(x, wqkv, qs, ksc, wo, lg, lb, w1, b1, w2, b2):
            b, n, _ = x.shape
            h = shift_token(x)
            qkv = h @ wqkv
            q, k, v = jnp.split(qkv, 3, axis=-1)
            to_heads = lambda t: t.reshape(b, n, HEADS, DIM_HEAD).transpose(0, 2, 1, 3)
            q, k, v = (to_heads(q), to_heads(k), to_heads(v))
            q = l2norm(q) * qs
            k = l2norm(k) * ksc
            q, k = rotary_xpos(q, k)
            o = local_attention(q, k, v)
            o = o.transpose(0, 2, 1, 3).reshape(b, n, INNER)
            x = x + o @ wo
            h = shift_token(x)
            mu = h.mean(-1, keepdims=True)
            var = h.var(-1, keepdims=True)
            h = (h - mu) / jnp.sqrt(var + 1e-05) * lg + lb
            h = h @ w1 + b1
            a, g = jnp.split(h, 2, axis=-1)
            h = a * jax.nn.gelu(g, approximate=False)
            x = x + h @ w2 + b2
            return x
        for l in range(DEPTH):
            x = _layer(x, wqkv[l], q_scale[l], k_scale[l], wo[l], ln_g[l], ln_b[l], w1[l], b1[l], w2[l], b2[l])
        return x
    x = _layernorm(x + _L0_attn_ref(x, L0_attn_norm_w, L0_attn_in_proj_w, L0_attn_conv_w, L0_attn_conv_b, L0_attn_x_proj_w, L0_attn_dt_proj_w, L0_attn_dt_proj_b, L0_attn_A_log, L0_attn_D, L0_attn_out_proj_w), axis=-1)
    x = _layernorm(x + _L0_xattn_ref(x, ctx_1024, L0_xattn_ln_gamma, L0_xattn_ln_beta, L0_xattn_w_q, L0_xattn_w_kv, L0_xattn_w_out, L0_xattn_b_out, L0_xattn_gate), axis=-1)
    x = _layernorm(x + _L0_ffn_ref(x, L0_ffn_shared_w1, L0_ffn_shared_b1, L0_ffn_shared_w2, L0_ffn_shared_b2, L0_ffn_router_w, L0_ffn_router_b, L0_ffn_spec_w1, L0_ffn_spec_b1, L0_ffn_spec_w2, L0_ffn_spec_b2), axis=-1)
    x = _layernorm(x + _L1_attn_ref(x, L1_attn_Wq, L1_attn_Wk, L1_attn_Wv, L1_attn_Wo, L1_attn_bo), axis=-1)
    x = _layernorm(x + _L1_xattn_ref(x, ctx_1024, L1_xattn_Wq, L1_xattn_Wkv, L1_xattn_Wout, L1_xattn_bout), axis=-1)
    x = _layernorm(x + _L1_ffn_ref(x, L1_ffn_wqkv, L1_ffn_q_scale, L1_ffn_k_scale, L1_ffn_wo, L1_ffn_ln_g, L1_ffn_ln_b, L1_ffn_w1, L1_ffn_b1, L1_ffn_w2, L1_ffn_b2), axis=-1)
    return x

_drawn_inputs = setup_inputs


def setup_inputs(seed=0):
    import zlib

    import numpy as np

    out = dict(_drawn_inputs(seed))
    spreads = {'L0_attn_norm_w': (1.0, 0.6),
     'L0_attn_conv_b': (0.0, 0.8),
     'L0_attn_D': (1.0, 0.6),
     'L0_xattn_ln_gamma': (1.0, 0.6),
     'L0_xattn_ln_beta': (0.0, 0.498),
     'L0_xattn_b_out': (0.0, 0.1),
     'L0_ffn_shared_b1': (0.0, 0.291),
     'L0_ffn_shared_b2': (0.0, 0.1),
     'L0_ffn_router_b': (0.0, 0.1),
     'L0_ffn_spec_b1': (0.0, 0.472),
     'L0_ffn_spec_b2': (0.0, 0.1),
     'L1_ffn_q_scale': (1.0, 0.6),
     'L1_ffn_k_scale': (1.0, 0.6),
     'L1_ffn_ln_g': (1.0, 0.6),
     'L1_ffn_ln_b': (0.0, 0.8),
     'L1_ffn_b1': (0.0, 0.8),
     'L1_ffn_b2': (0.0, 0.674)}
    factors = {'L0_attn_in_proj_w': 8.0,
     'L0_attn_conv_w': 8.0,
     'L0_attn_x_proj_w': 8.0,
     'L0_attn_dt_proj_w': 8.0,
     'L0_attn_dt_proj_b': 8.0,
     'L0_attn_A_log': 8.0,
     'L0_attn_out_proj_w': 8.0,
     'L1_attn_bo': 5.626,
     'L1_xattn_bout': 5.645,
     'L1_ffn_w1': 6.733,
     'L1_ffn_w2': 6.508}
    for name, (base, spread) in spreads.items():
        noise = np.random.default_rng([zlib.crc32(name.encode()), seed]).standard_normal(out[name].shape)
        drawn = base * np.exp(spread * noise) if base else spread * noise
        out[name] = jnp.asarray(drawn.astype(out[name].dtype))
    for name, factor in factors.items():
        out[name] = (out[name] * factor).astype(out[name].dtype)
    return out
```

```python
from contextlib import ExitStack

import numpy as np

import concourse.bass as bass
from concourse import mybir

F32 = mybir.dt.float32
BF16 = mybir.dt.bfloat16
U32 = mybir.dt.uint32
ACT = mybir.ActivationFunctionType
ALU = mybir.AluOpType
X = mybir.AxisListType.X

B, T, D = 4, 512, 128
P = 128
NT = T // P
S = 32
CH, NS, KC, DTR = 256, 16, 4, 8
NB = CH // P
H1, DH1 = 16, 64
E, FF = 8, 512
NF = FF // P
H3, DH3 = 16, 8
H5, DH5 = 8, 64
HID = 341
NH = 3
HC = [min(P, HID - P * c) for c in range(NH)]
DEPTH = 2
EPS = 1e-5
SCRATCH = 15360
NEG = -1e30

GROUPS = {
    "mamba": dict(w_in=512, w_conv=KC * CH, norm_w=1, conv_b=NB, x_bc=NB * 96, x_dt=NB * DTR,
                  w_dt=CH, b_dt=NB, a_log=NB * NS, d_skip=NB, w_out=NB * D),
    "cross0": dict(ctx=B * S, w_qT=8 * P, w_k=1024, w_v=1024, w_o=8 * P, gate=1,
                   w4_q=D, w4_k=D, w4_v=D, w4_o=D,
                   scales=DEPTH * 4 * DH5),
    "rope5": dict(tables=NT * 4 * DH5),
    "experts": dict(w1=(E + 1) * FF, b1=(E + 1) * NF, w2=(E + 1) * NF * D, b2s=1, router=E, b2e=D, gamma=1, beta=1),
    "window": dict(w_qk=4 * D, w_v=D, w_o=D),
    "local": dict(w_qkv=DEPTH * 1536, w_o=DEPTH * 4 * D, ln_g=DEPTH, ln_b=DEPTH,
                  w1=DEPTH * 2 * HID, b1=DEPTH * 2 * NH, w2=DEPTH * NH * D),
    "rows": dict(b_x0=D, b_win=D, b_x1=D, b2_0=D, b2_1=D, router=E, ones=P),
    "const": dict(ident=P, mean=P, rope3=NT * 2 * 2 * DH3,
                  pair=2, head=H3, iota=E, eps=1, ten_ln2=1, one=1),
}
WIDTH = {g: sum(c.values()) for g, c in GROUPS.items()}
ROWS = {"rows": 1}
CB = dict(ident=P, band3=2 * P, band5=2 * P, select=2 * NS)


class Waits:

    def __init__(self, eng, own):
        self.eng, self.own, self.asked, self.steps = eng, own, {}, 0

    def __call__(self, sem, k=1):
        n = self.asked.get(sem.name, 0) + k
        self.asked[sem.name] = n
        if n > 0:
            self.eng.wait_ge(sem, n)

    def step(self, ins):
        self.steps += 1
        ins.then_inc(self.own, 1)
        self.eng.wait_ge(self.own, self.steps)


class Ring:

    def __init__(self, eng, banks, n, filled, freed):
        self.eng, self.banks, self.n, self.filled, self.freed, self.at = eng, banks, n, filled, freed, 0

    def open(self):
        if self.at >= self.n:
            self.eng.wait_ge(self.freed, self.at - self.n + 1)
        self.at += 1
        return self.banks[:, (self.at - 1) % self.n]

    def take(self):
        self.at += 1
        self.eng.wait_ge(self.filled, self.at)
        return self.banks[:, (self.at - 1) % self.n]


class Lane:

    def __init__(self, eng, s, own, ps):
        self.eng, self.w = eng, Waits(eng, s[own] if own else None)
        self.a = Ring(eng, ps[0], 2, s["a_filled"], s["a_freed"])
        self.v = Ring(eng, ps[1], 2, s["v_filled"], s["v_freed"])
        self.s = Ring(eng, ps[2], 3, s["s_filled"], s["s_freed"])
        self.o = Ring(eng, ps[3], 1, s["o_filled"], s["o_freed"])
        self.log = []

    def end(self, stage):
        self.log.append((stage, self.a.at, self.v.at, self.s.at, self.o.at))

    def skip(self, a=0, v=0, s=0, o=0):
        self.a.at += a
        self.v.at += v
        self.s.at += s
        self.o.at += o


def decoder_kernel(nc, x_in, packed, cb_in, out, last=7):
    with ExitStack() as ctx:
        def sb(name, shape, dt=F32):
            return ctx.enter_context(nc.sbuf_tensor(name, shape, dt))

        def sem(name):
            return ctx.enter_context(nc.semaphore(name))

        psA = ctx.enter_context(nc.psum_tensor("psA", [P, 2, 512], F32))
        psV = ctx.enter_context(nc.psum_tensor("psV", [P, 2, 512], F32))
        psS = ctx.enter_context(nc.psum_tensor("psS", [P, 3, 512], F32))
        psO = ctx.enter_context(nc.psum_tensor("psO", [P, 1, 512], F32))

        scr = sb("scratch", [P, SCRATCH])
        used = [0]

        def carve(*shape):
            n = int(np.prod(shape))
            v = scr[:, used[0]:used[0] + n]
            used[0] += n
            assert used[0] <= SCRATCH, used
            names = "abcde"[:len(shape)]
            if len(shape) == 1:
                return v
            return v.rearrange(f"p ({' '.join(names)}) -> p {' '.join(names)}",
                               **dict(zip(names[:-1], shape[:-1])))

        wt, cols = {}, {}
        for g, c in GROUPS.items():
            if g in ("cross0", "rope5"):
                wt[g] = carve(WIDTH[g])
            else:
                wt[g] = sb("w_" + g, [ROWS.get(g, P), WIDTH[g]])
            at = 0
            for n, w in c.items():
                cols[g, n] = (at, at + w)
                at += w

        def W(group, name, **dims):
            a, b = cols[group, name]
            v = wt[group][:, a:b]
            if dims:
                v = v.rearrange(f"p ({' '.join(dims)} z) -> p {' '.join(dims)} z", **dims)
            return v

        cb = sb("cb", [P, sum(CB.values())], BF16)
        cbv, at = {}, 0
        for n, w in CB.items():
            cbv[n] = cb[:, at:at + w]
            at += w
        ident, mean_w, ones = W("const", "ident"), W("const", "mean"), W("rows", "ones")
        eps, ten_ln2, one = W("const", "eps"), W("const", "ten_ln2"), W("const", "one")
        row = lambda n: W("rows", n).rearrange("p (o z) -> p o z", o=1).to_broadcast([1, NT, D])

        w_in = W("mamba", "w_in")
        w_conv = W("mamba", "w_conv", k=KC)
        a_neg = sb("a_neg", [P, NB, NS])
        gate = sb("gate", [P, 1])
        b_x0 = W("rows", "b_x0")
        tab5 = sb("tab5", [P, DEPTH, 4, NT, DH5])
        score0 = sb("score0", [P, B, H1 * S])
        value0 = sb("value0", [P, B, 4, D])
        score1 = sb("score1", [P, B, H3 * S])
        value1 = sb("value1", [P, B, 4, D])

        x = sb("x", [P, NT, D])
        y = sb("y", [P, NT, D])
        xT = sb("xT", [P, T + KC - 1])
        hT = sb("hT", [P, T])
        rowstat = sb("rowstat", [P, NT, 6])
        mv = sb("mv", [P, NT, 2])
        rstd = sb("rstd", [P, NT])
        kbd, vbd = carve(B, 512), carve(B, 512)
        row_x0 = b_x0.rearrange("p (o z) -> p o z", o=1).to_broadcast([1, NT, D])
        used[0] = 0
        u, zs, delta, du = carve(NB, T), carve(NB, T), carve(NB, T), carve(NB, T)
        dA, dBu, hs, hC = carve(4, T), carve(2, T), carve(2, T), carve(4, T)
        sp1, sp2, rest, dtS, yg = carve(NB, T), carve(NB, T), carve(T), carve(T), carve(NB, T)
        mid = carve(T // 2).bitcast(BF16)
        parts = carve(T // 2).bitcast(BF16)
        used[0] = 0
        e1 = carve(2, T)
        pT1 = carve(2, 4, P)
        used[0] = 0
        hid, pickS, acc, tmp = carve(2, NF, T), carve(E, T), carve(T), carve(2, T)
        combT = carve(T)
        used[0] = 0
        qk = carve(2, 1024)
        ra, rb = carve(2, 1024), carve(2, 1024)
        qT, kT = carve(4, T), carve(4, T)
        vv = carve(NT, 512)
        oT = carve(4, T)
        pT = carve(2, 512)
        used[0] = 0
        pr = carve(3, 512)
        used[0] = 0
        hc, sq, rst, gg, uu = carve(T), carve(T), carve(T), carve(NH, T), carve(NH, T)
        qpad = sb("qpad", [P, 2, 512])
        kpad = sb("kpad", [P, 2, 512])
        vpad = sb("vpad", [P, NT, H3, 32])
        small = sb("small", [P, 8, 32])
        mx = sb("mx", [P, 2, 64])
        sums = sb("sums", [P, 2, 64])
        rinv = sb("rinv", [P, 2, 64])
        mx2, sums2, rinv2 = mx[:, 0, :], sums[:, 0, :], rinv[:, 0, :]
        m8 = sb("m8", [P, NT, 8])
        i8 = sb("i8", [P, NT, 8], U32)
        lg, comb, eqt = sb("lg", [P, NT, E]), sb("comb", [P, NT, E]), sb("eqt", [P, NT, E])

        names = ("loaded cb_loaded x_loaded stored act_step dve_step pool_step "
                 "a_filled a_freed v_filled v_freed s_filled s_freed o_filled o_freed "
                 "setup_dve setup_act stats_ready rstd_ready norm_ready xT_ready rms_ready "
                 "silu_ready dt_ready soft_ready delta_ready parts_ready decay_ready decay_used "
                 "states_ready states_used sum_filled sums_read gated_ready "
                 "pad_ready max_ready exp_ready rinv_ready prob_ready prob_used pT_ready pT_used "
                 "diff_ready e_ready sum_ready qk_ready qk_used ss_ready rn_ready qn_ready "
                 "rot_ready rot_used rope_ready qkT_ready v_ready oT_ready hT_ready "
                 "gap_ready ratio_ready comb_ready combT_ready hid_ready hid_used pick_ready "
                 "part_ready part_used acc_ready centred_ready sq_ready rst_ready hn_ready "
                 "gelu_ready u_ready y_ready").split()
        s = {n: sem(n) for n in names}
        sems = range(min(v.num for v in s.values()), max(v.num for v in s.values()) + 1)
        assert len(sems) == len(names)

        ps = (psA, psV, psS, psO)
        lanes = {}

        with nc.Block() as block:
            @block.sync
            def _(sp):
                for g in GROUPS:
                    sp.dma_start(wt[g][:, :], packed[g]).then_inc(s["loaded"], 16)
                sp.dma_start(cb[:, :], cb_in).then_inc(s["cb_loaded"], 16)
                sp.wait_ge(s["cb_loaded"], 16)

            @block.gpsimd
            def _(pool):
                nc.gpsimd.memset(qpad[:, :, :], 0.0)
                nc.gpsimd.memset(kpad[:, :, :], 0.0)
                nc.gpsimd.memset(vpad[:, :, :, :], 0.0)
                nc.gpsimd.memset(xT[:, :], 0.0)
                nc.gpsimd.memset(hT[:, :], 0.0)

            @block.scalar
            def _(act):
                act.wait_ge(s["loaded"], 16 * len(GROUPS))
                act.activation(a_neg[:, :, :], W("mamba", "a_log", b=NB), ACT.Exp).then_inc(s["setup_act"], 1)
                act.activation(gate[:, :], W("cross0", "gate"), ACT.Tanh).then_inc(s["setup_act"], 1)

            @block.vector
            def _(dve):
                t = Lane(dve, s, "dve_step", ps)
                w, v = t.w, t.v
                w(s["loaded"], 16 * len(GROUPS))
                w.step(dve.tensor_scalar(w_in[:, :], W("mamba", "w_in"), W("mamba", "norm_w"), None, ALU.mult))
                wx = w_in[:, 0:CH].rearrange("p (o c) -> p o c", o=1).to_broadcast([P, KC, CH])
                dve.tensor_tensor(w_conv[:, :, :], w_conv, wx, ALU.mult)
                w(s["setup_act"], 2)
                dve.tensor_scalar(a_neg[:, :, :], a_neg[:, :, :], -1.0, None, ALU.mult)
                dve.tensor_scalar(b_x0, b_x0, gate[0:1, :], None, ALU.mult)
                rope = W("rope5", "tables", f=4, t=NT)
                for l in range(DEPTH):
                    sc = W("cross0", "scales", l=DEPTH, f=4)
                    for f in range(4):
                        by = sc[:, l, f, :].rearrange("p (o z) -> p o z", o=1).to_broadcast([P, NT, DH5])
                        dve.tensor_tensor(tab5[:, l, f], rope[:, f], by, ALU.mult)
                pair = W("const", "pair").rearrange("p (a i b) -> p a i b", a=1, b=1).to_broadcast([P, B, 2, S])
                for p in range(8):
                    for dst in (kbd, vbd):
                        src = v.take()[:, 0:B * S].rearrange("p (b o k) -> p b o k", b=B, o=1)
                        dve.tensor_tensor(dst[:, :, p * 2 * S:(p + 1) * 2 * S].rearrange("p b (i k) -> p b i k", i=2),
                                          src.to_broadcast([P, B, 2, S]), pair, ALU.mult).then_inc(s["v_freed"], 1)
                for b in range(B):
                    dve.tensor_copy(score0[:, b], v.take()[:, :]).then_inc(s["v_freed"], 1)
                    dve.tensor_scalar(value0[:, b].rearrange("p j d -> p (j d)"), v.take()[:, :], gate[:, :],
                                      None, ALU.mult).then_inc(s["v_freed"], 1)
                head = W("const", "head").rearrange("p (a i b) -> p a i b", a=1, b=1).to_broadcast([P, B, H3, S])
                for dst in (kbd, vbd):
                    src = v.take()[:, 0:B * S].rearrange("p (b o k) -> p b o k", b=B, o=1)
                    for b in range(B):
                        ins = dve.tensor_tensor(dst[:, b].rearrange("p (i k) -> p i k", i=H3),
                                                src[:, b].to_broadcast([P, H3, S]), head[:, b], ALU.mult)
                    ins.then_inc(s["v_freed"], 1)
                for b in range(B):
                    dve.tensor_copy(score1[:, b], v.take()[:, :]).then_inc(s["v_freed"], 1)
                    dve.tensor_copy(value1[:, b].rearrange("p j d -> p (j d)"), v.take()[:, :]).then_inc(s["v_freed"], 1)

            @block.tensor
            def _(pe):
                t = Lane(pe, s, None, ps)
                w, v = t.w, t.v
                w(s["loaded"], 16 * len(GROUPS))
                ctxT = W("cross0", "ctx")
                for p in range(8):
                    for n in ("w_k", "w_v"):
                        pe.matmul(v.open()[:, 0:B * S], W("cross0", n)[:, p * P:(p + 1) * P], ctxT,
                                  start=True, stop=True).then_inc(s["v_filled"], 1)
                for b in range(B):
                    bank = v.open()
                    if b == 0:
                        pe.wait_ge(s["v_freed"], 16)
                    for p in range(8):
                        ins = pe.matmul(bank[:, p * 64:(p + 1) * 64], W("cross0", "w_qT")[:, p * P:(p + 1) * P],
                                        kbd[:, b, p * 64:(p + 1) * 64], start=(p == 0), stop=(p == 7),
                                        skip_group_check=True)
                    ins.then_inc(s["v_filled"], 1)
                    bank = v.open()
                    for j in range(4):
                        for i in range(2):
                            p = 2 * j + i
                            ins = pe.matmul(bank[64 * i:64 * i + 64, j * D:(j + 1) * D],
                                            vbd[:, b, p * 64:(p + 1) * 64], W("cross0", "w_o")[:, p * P:(p + 1) * P],
                                            start=(j == 0), stop=(j == 3), skip_group_check=True)
                    ins.then_inc(s["v_filled"], 1)
                for n in ("w4_k", "w4_v"):
                    pe.matmul(v.open()[:, 0:B * S], W("cross0", n), ctxT, start=True, stop=True).then_inc(s["v_filled"], 1)
                pe.wait_ge(s["v_freed"], 16 + 2 * B + 2)
                for b in range(B):
                    pe.matmul(v.open()[:, :], W("cross0", "w4_q"), kbd[:, b], start=True, stop=True)\
                        .then_inc(s["v_filled"], 1)
                    bank = v.open()
                    for j in range(4):
                        ins = pe.matmul(bank[:, j * D:(j + 1) * D], vbd[:, b, j * P:(j + 1) * P], W("cross0", "w4_o"),
                                        start=(j == 0), stop=(j == 3), skip_group_check=True)
                    ins.then_inc(s["v_filled"], 1)
        nc.sync.sem_clear(sems)
        nc.all_engine_barrier()


        def tok(v, t):
            return v[:, t * P:(t + 1) * P]

        xTn = xT[:, KC - 1:KC - 1 + T]
        x_flat = x[:, :, :].rearrange("p t d -> p (t d)")
        y_flat = y[:, :, :].rearrange("p t d -> p (t d)")

        def norm_vector(t, dst, src, done):
            for i in range(NT):
                ins = t.eng.bn_stats(rowstat[:, i, :], src[:, i, :])
            t.w.step(ins)
            for i in range(NT):
                ins = t.eng.bn_aggr(mv[:, i, :], rowstat[:, i, :])
            ins.then_inc(s["stats_ready"], 1)
            t.w(s["rstd_ready"])
            for i in range(NT):
                ins = t.eng.tensor_scalar(dst[:, i, :], src[:, i, :], mv[:, i, 0:1], rstd[:, i:i + 1],
                                          ALU.subtract, ALU.mult)
            ins.then_inc(s[done], 1)
            t.w(s[done])

        def norm_scalar(t):
            t.w(s["stats_ready"])
            t.w.step(t.eng.activation(rstd[:, :], mv[:, :, 1], ACT.Ln, bias=eps))
            t.eng.activation(rstd[:, :], rstd[:, :], ACT.Exp, scale=-0.5).then_inc(s["rstd_ready"], 1)

        def turn_tensor(t, src):
            bank = t.a.open()
            for i in range(NT):
                ins = t.eng.transpose(tok(bank, i), src[:, i, :], ident)
            ins.then_inc(s["a_filled"], 1)
            return t.a.at

        def plain_scalar(t):
            t.eng.activation(xTn, t.a.take(), ACT.Copy).then_inc(s["a_freed"], 1)

        def residual_vector(t, dst, times=None):
            t.w(s["o_filled"])
            t.skip(o=1)
            bank = psO[:, 0]
            if times:
                ins = t.eng.scalar_tensor_tensor(dst, x_flat, times, bank, ALU.mult, ALU.add)
            else:
                ins = t.eng.tensor_tensor(dst, bank, x_flat, ALU.add)
            ins.then_inc(s["o_freed"], 1)
            t.eng.wait_ge(s["o_freed"], t.o.at)

        def mamba_tensor(t):
            pe = t.eng
            t.w(s["rms_ready"])
            turn_tensor(t, y)
            pe.wait_ge(s["a_freed"], t.a.at)
            for c in range(NB):
                bank = t.a.open()
                for k in range(KC):
                    ins = pe.matmul(bank, w_conv[:, k, c * P:(c + 1) * P], xT[:, k:k + T],
                                    start=(k == 0), stop=(k == KC - 1))
                ins.then_inc(s["a_filled"], 1)
            u_at = t.a.at
            for c in range(NB):
                pe.matmul(t.a.open(), w_in[:, CH + c * P:CH + (c + 1) * P], xTn, start=True, stop=True)\
                    .then_inc(s["a_filled"], 1)
            pe.wait_ge(s["a_freed"], u_at)
            bank = t.a.open()
            for c in range(NB):
                ins = pe.matmul(bank[0:DTR, :], W("mamba", "x_dt", c=NB)[:, c, :], u[:, c, :],
                                start=(c == 0), stop=(c == NB - 1))
            ins.then_inc(s["a_filled"], 1)
            dt_at = t.a.at
            bank = t.v.open()
            for c in range(NB):
                ins = pe.matmul(bank[0:96, :], W("mamba", "x_bc", c=NB)[:, c, :], u[:, c, :],
                                start=(c == 0), stop=(c == NB - 1))
            ins.then_inc(s["v_filled"], 1)
            pe.wait_ge(s["a_freed"], dt_at)
            for c in range(NB):
                pe.matmul(t.a.open(), W("mamba", "w_dt")[0:DTR, c * P:(c + 1) * P], dtS[0:DTR, :],
                          start=True, stop=True).then_inc(s["a_filled"], 1)
            t.w(s["parts_ready"])
            sums2 = [t.s.open(), t.s.open()]
            for n in range(NS + 1):
                if n < NS:
                    for which in (n, NS + n):
                        pe.matmul(t.v.open(), cbv["select"][0:96, which:which + 1].to_broadcast([96, P]), parts[0:96, :],
                                  start=True, stop=True).then_inc(s["v_filled"], 1)
                if n >= 1:
                    pe.wait_ge(s["v_freed"], t.v.at - (2 if n < NS else 0))
                    for c in range(NB):
                        ins = pe.matmul(sums2[c], ident, hC[:, 2 * ((n - 1) % 2) + c, :],
                                        start=(n == 1), stop=(n == NS))
                        if n == NS:
                            ins.then_inc(s["s_filled"], 1)
                    if n < NS:
                        ins.then_inc(s["states_used"], 1)
            t.w(s["gated_ready"])
            bank = t.o.open()
            for i in range(NT):
                for c in range(NB):
                    ins = pe.matmul(tok(bank, i), tok(yg[:, c, :], i), W("mamba", "w_out", c=NB)[:, c, :],
                                    start=(i == 0 and c == 0), stop=(i == NT - 1 and c == NB - 1),
                                    skip_group_check=True)
            ins.then_inc(s["o_filled"], 1)

        def mamba_scalar(t):
            act = t.eng
            t.w(s["x_loaded"], 16)
            for i in range(NT):
                ins = act.activation(tok(rest, i), x[:, i, :], ACT.Square, accum_out=small[:, 0, i:i + 1])
            t.w.step(ins)
            t.w.step(act.activation(rstd[:, :], small[:, 0, 0:NT], ACT.Ln, scale=1.0 / D, bias=eps))
            act.activation(rstd[:, :], rstd[:, :], ACT.Exp, scale=-0.5).then_inc(s["rstd_ready"], 1)
            plain_scalar(t)
            for c in range(NB):
                act.activation(u[:, c, :], t.a.take(), ACT.Silu, bias=W("mamba", "conv_b")[:, c:c + 1])\
                    .then_inc(s["a_freed"], 1)
            for c in range(NB):
                act.activation(zs[:, c, :], t.a.take(), ACT.Silu).then_inc(s["a_freed"], 1)
            act.activation(dtS[0:DTR, :], t.a.take()[0:DTR, :], ACT.Copy).then_inc(s["a_freed"], 1)
            for c in range(NB):
                bank = t.a.take()
                act.activation(sp1[:, c, :], bank, ACT.Abs, bias=W("mamba", "b_dt")[:, c:c + 1])
                act.activation(sp2[:, c, :], bank, ACT.Relu, bias=W("mamba", "b_dt")[:, c:c + 1])\
                    .then_inc(s["a_freed"], 1)
            act.wait_ge(s["a_freed"], t.a.at)
            act.activation(sp1[:, :, :], sp1[:, :, :], ACT.Exp, scale=-1.0).then_inc(s["soft_ready"], 1)
            act.wait_ge(s["soft_ready"], 1)
            act.activation(delta[:, :, :], sp1[:, :, :], ACT.Ln, bias=one).then_inc(s["soft_ready"], 1)
            t.w(s["delta_ready"])
            for n in range(NS):
                for c in range(NB):
                    i = NB * n + c
                    if i >= 4:
                        t.w(s["decay_used"])
                    act.activation(dA[:, i % 4, :], delta[:, c, :], ACT.Exp, scale=a_neg[:, c, n:n + 1])\
                        .then_inc(s["decay_ready"], 1)
            t.skip(v=1 + 2 * NS, s=2, o=1)

        def mamba_vector(t):
            dve = t.eng
            t.w(s["rstd_ready"])
            for i in range(NT):
                ins = dve.tensor_scalar(y[:, i, :], x[:, i, :], rstd[:, i:i + 1], None, ALU.mult)
            ins.then_inc(s["rms_ready"], 1)
            t.skip(a=8)
            bank = t.v.take()
            t.w.step(dve.tensor_copy(parts[0:96, :], bank[0:96, :]))
            dve.tensor_tensor(rest[0:96, :], bank[0:96, :], parts[0:96, :], ALU.subtract)\
                .then_inc(s["v_freed"], 1)
            dve.wait_ge(s["v_freed"], t.v.at)
            t.w.step(dve.tensor_copy(mid[0:96, :], rest[0:96, :]))
            dve.tensor_copy(parts[32:64, :], mid[32:64, :])
            t.w.step(dve.tensor_tensor(rest[64:96, :], rest[64:96, :], mid[64:96, :], ALU.subtract))
            dve.tensor_copy(parts[64:96, :], rest[64:96, :]).then_inc(s["parts_ready"], 1)
            t.w(s["soft_ready"])
            t.w.step(dve.tensor_scalar(du[:, :, :], sp1[:, :, :], 1.0, 1.0, ALU.add, ALU.subtract))
            t.w.step(dve.tensor_tensor(du[:, :, :], sp1[:, :, :], du[:, :, :], ALU.subtract))
            t.w(s["soft_ready"])
            t.w.step(dve.tensor_tensor(delta[:, :, :], delta[:, :, :], du[:, :, :], ALU.add))
            t.w.step(dve.tensor_tensor(delta[:, :, :], delta[:, :, :], sp2[:, :, :], ALU.add))
            dve.tensor_tensor(du[:, :, :], delta[:, :, :], u[:, :, :], ALU.mult).then_inc(s["delta_ready"], 1)
            t.w(s["delta_ready"])
            for n in range(NS):
                bank = t.v.take().rearrange("p (o z) -> p o z", o=1).to_broadcast([P, NB, T])
                dve.tensor_tensor(dBu[:, :, :], du[:, :, :], bank, ALU.mult).then_inc(s["v_freed"], 1)
                dve.wait_ge(s["v_freed"], t.v.at)
                for c in range(NB):
                    i = NB * n + c
                    t.w(s["decay_ready"])
                    dve.tensor_tensor_scan(hs[:, c, :], dA[:, i % 4, :], dBu[:, c, :], 0.0, ALU.mult, ALU.add)\
                        .then_inc(s["decay_used"], 1)
                bank = t.v.take().rearrange("p (o z) -> p o z", o=1).to_broadcast([P, NB, T])
                if n >= 2:
                    t.w(s["states_used"])
                dve.wait_ge(s["decay_used"], NB * (n + 1))
                dve.tensor_tensor(hC[:, 2 * (n % 2):2 * (n % 2) + 2, :], hs[:, :, :], bank, ALU.mult)\
                    .then_inc(s["v_freed"], 1)
            for c in range(NB):
                bank = t.s.take()
                dve.scalar_tensor_tensor(yg[:, c, :], u[:, c, :], W("mamba", "d_skip")[:, c:c + 1], bank,
                                         ALU.mult, ALU.add).then_inc(s["s_freed"], 1)
            dve.wait_ge(s["s_freed"], t.s.at)
            dve.tensor_tensor(yg[:, :, :], yg[:, :, :], zs[:, :, :], ALU.mult).then_inc(s["gated_ready"], 1)
            residual_vector(t, y_flat, 2.0)
            norm_vector(t, x, y, "norm_ready")

        def cross_tensor(t, b, src, score, value, bias):
            pe = t.eng
            t.w(s["norm_ready"], 2 if src is y else 1)
            turn_tensor(t, src)
            pe.wait_ge(s["a_freed"], t.a.at)
            out_bank = t.o.open()
            pe.matmul(out_bank, ones[0:1, :], bias, start=True, stop=False, skip_group_check=True)
            for i in range(NT + 2):
                if i < NT:
                    pe.matmul(t.v.open(), tok(xTn, i), score[:, b], start=True, stop=True)\
                        .then_inc(s["v_filled"], 1)
                if 1 <= i <= NT:
                    t.w(s["prob_ready"])
                    bank = t.a.open()
                    for j in range(4):
                        ins = pe.transpose(tok(bank, j), tok(e1[:, (i - 1) % 2, :], j), ident)
                    ins.then_inc(s["a_filled"], 1)
                if i >= 2:
                    pe.wait_ge(s["a_freed"], t.a.at - (1 if i <= NT else 0))
                    for j in range(4):
                        ins = pe.matmul(tok(out_bank, i - 2), pT1[:, i % 2, j, :], value[:, b, j, :],
                                        start=False, stop=(i == NT + 1 and j == 3), skip_group_check=True)
                    ins.then_inc(s["o_filled"] if i == NT + 1 else s["pT_used"], 1)

        def cross_scalar(t, scale, inner):
            act = t.eng
            if inner:
                norm_scalar(t)
                act.activation(xTn, t.a.take(), ACT.Identity, scale=W("experts", "gamma"),
                               bias=W("experts", "beta")).then_inc(s["a_freed"], 1)
            else:
                plain_scalar(t)
            for i in range(NT + 1):
                if i < NT:
                    t.skip(v=1)
                    act.wait_ge(s["v_freed"], t.v.at)
                    act.activation(e1[:, i % 2, :], e1[:, i % 2, :], ACT.Exp, scale=scale)\
                        .then_inc(s["e_ready"], 1)
                if i >= 1:
                    if i >= 3:
                        t.w(s["pT_used"])
                    act.activation(pT1[:, (i - 1) % 2].rearrange("p j z -> p (j z)"), t.a.take(), ACT.Copy)\
                        .then_inc(s["a_freed"], 1)
            if not inner:
                pass
            t.w(s["pT_used"], 1)
            t.skip(o=1)

        def cross_vector(t, inner):
            dve = t.eng
            if inner:
                norm_vector(t, y, x, "norm_ready")
            t.skip(a=1)
            heads = lambda v: v.rearrange("p (h k) -> p h k", h=H1)
            wide = lambda v: v.rearrange("p (h o) -> p h o", o=1).to_broadcast([P, H1, S])
            for i in range(NT + 1):
                if i < NT:
                    if i >= 2:
                        dve.wait_ge(s["a_freed"], t.a.at - 0)
                    bank = t.v.take()
                    t.w.step(dve.tensor_reduce(mx[:, i % 2, 0:H1], heads(bank), X, ALU.max, negate=True))
                    dve.tensor_tensor(heads(e1[:, i % 2, :]), heads(bank), wide(mx[:, i % 2, 0:H1]), ALU.add)\
                        .then_inc(s["v_freed"], 1)
                if i >= 1:
                    j = (i - 1) % 2
                    t.w(s["e_ready"])
                    t.w.step(dve.tensor_reduce(sums[:, j, 0:H1], heads(e1[:, j, :]), X, ALU.add))
                    dve.reciprocal(rinv[:, j, 0:H1], sums[:, j, 0:H1]).then_inc(s["rinv_ready"], 1)
                    t.skip(a=1)
            residual_vector(t, y_flat)
            norm_vector(t, x, y, "norm_ready")

        def cross_pool(t):
            for i in range(NT):
                t.w(s["rinv_ready"])
                by = rinv[:, i % 2, 0:H1].rearrange("p (h o) -> p h o", o=1).to_broadcast([P, H1, S])
                v = e1[:, i % 2, :].rearrange("p (h k) -> p h k", h=H1)
                t.eng.tensor_tensor(v, v, by, ALU.mult).then_inc(s["prob_ready"], 1)
            t.skip(a=1 + NT, v=NT, o=1)

        def experts_tensor(t):
            pe = t.eng
            t.w(s["norm_ready"])
            turn_tensor(t, x)
            pe.wait_ge(s["a_freed"], t.a.at)
            bank = t.v.open()
            pe.matmul(bank[:, 0:NT * E], ones[0:1, :],
                      W("rows", "router").rearrange("p (o z) -> p o z", o=1).to_broadcast([1, NT, E]),
                      start=True, stop=False, skip_group_check=True)
            for i in range(NT):
                ins = pe.matmul(bank[:, i * E:(i + 1) * E], tok(xTn, i), W("experts", "router"), start=False,
                                stop=(i == NT - 1), skip_group_check=True)
            ins.then_inc(s["v_filled"], 1)
            hid_at = {}
            for k in range(E + 2):
                if 1 <= k <= E:
                    pe.matmul(t.a.open(), ident[0:E, k - 1:k].to_broadcast([E, P]), combT[0:E, :],
                              start=True, stop=True).then_inc(s["a_filled"], 1)
                if k <= E:
                    for f in range(NF):
                        c = k * NF + f
                        pe.matmul(t.a.open(), W("experts", "w1")[:, c * P:(c + 1) * P], xTn, start=True, stop=True)\
                            .then_inc(s["a_filled"], 1)
                    hid_at[k] = t.a.at
                if k == 0:
                    t.w(s["comb_ready"])
                    bank = t.a.open()
                    for i in range(NT):
                        ins = pe.transpose(tok(bank, i)[0:E, :], comb[:, i, :], ident)
                    ins.then_inc(s["a_filled"], 1)
                    pe.wait_ge(s["a_freed"], t.a.at)
                if k >= 1:
                    pe.wait_ge(s["a_freed"], hid_at[k - 1])
                    bank = t.v.open()
                    if k == 1:
                        pe.matmul(bank, W("experts", "b2e")[0:E, :], combT[0:E, :], start=True, stop=False)
                    for f in range(NF):
                        c = (k - 1) * NF + f
                        ins = pe.matmul(bank, W("experts", "w2")[:, c * P:(c + 1) * P], hid[:, (k - 1) % 2, f, :],
                                        start=(k > 1 and f == 0), stop=(f == NF - 1))
                    ins.then_inc(s["v_filled"], 1)
            t.w(s["acc_ready"], E)
            bank = t.v.open()
            for i in range(NT):
                ins = pe.transpose(tok(bank, i), tok(acc, i), ident)
            ins.then_inc(s["v_filled"], 1)

        def experts_scalar(t):
            act = t.eng
            plain_scalar(t)
            t.skip(v=1)
            t.w(s["gap_ready"])
            act.activation(small[:, 1, 0:NT], small[:, 0, 0:NT], ACT.Exp).then_inc(s["ratio_ready"], 1)
            for k in range(E + 1):
                if k >= 1:
                    act.activation(pickS[:, k - 1, :], t.a.take(), ACT.Copy).then_inc(s["a_freed"], 1)
                for f in range(NF):
                    if k >= 2 and f == 0:
                        act.wait_ge(s["v_filled"], t.v.at)
                    c = k * NF + f
                    act.activation(hid[:, k % 2, f, :], t.a.take(), ACT.Gelu_apprx_tanh,
                                   bias=W("experts", "b1")[:, c:c + 1]).then_inc(s["a_freed"], 1)
                if k == 0:
                    act.activation(combT[0:E, :], t.a.take()[0:E, :], ACT.Copy).then_inc(s["a_freed"], 1)
                if k >= 1:
                    t.skip(v=1)
            t.skip(v=2)

        def experts_vector(t):
            dve = t.eng
            bank = t.v.take()
            dve.tensor_copy(lg[:, :, :].rearrange("p t e -> p (t e)"), bank[:, 0:NT * E]).then_inc(s["v_freed"], 1)
            dve.wait_ge(s["v_freed"], t.v.at)
            for i in range(NT):
                ins = dve.max(m8[:, i, :], lg[:, i, :])
            t.w.step(ins)
            dve.tensor_tensor(small[:, 0, 0:NT], m8[:, :, 1], m8[:, :, 0], ALU.subtract).then_inc(s["gap_ready"], 1)
            for i in range(NT):
                ins = dve.max_index(i8[:, i, :], m8[:, i, :], lg[:, i, :])
            t.w.step(ins)
            top = small[:, 2, 0:2 * NT].rearrange("p (t e) -> p t e", e=2)
            dve.tensor_copy(top, i8[:, :, 0:2])
            t.w(s["ratio_ready"])
            t.w.step(dve.tensor_scalar(small[:, 3, 0:NT], small[:, 1, 0:NT], 1.0, None, ALU.add))
            t.w.step(dve.reciprocal(small[:, 4, 0:NT], small[:, 3, 0:NT]))
            t.w.step(dve.tensor_tensor(small[:, 5, 0:NT], small[:, 4, 0:NT], small[:, 1, 0:NT], ALU.mult))
            wide = lambda v: v.rearrange("p (t o) -> p t o", o=1).to_broadcast([P, NT, E])
            iota = W("const", "iota").rearrange("p (o e) -> p o e", o=1).to_broadcast([P, NT, E])
            for n, dst in ((0, comb), (1, eqt)):
                t.w.step(dve.tensor_tensor(dst[:, :, :], iota, top[:, :, n:n + 1].to_broadcast([P, NT, E]), ALU.is_equal))
                t.w.step(dve.tensor_tensor(dst[:, :, :], dst[:, :, :], wide(small[:, 4 + n, 0:NT]), ALU.mult))
            dve.tensor_tensor(comb[:, :, :], comb[:, :, :], eqt[:, :, :], ALU.add).then_inc(s["comb_ready"], 1)
            for k in range(E + 1):
                bank = t.v.take()
                if k == 0:
                    dve.tensor_scalar(acc, bank, W("experts", "b2s"), None, ALU.add).then_inc(s["v_freed"], 1)
                else:
                    if k >= 3:
                        t.w(s["acc_ready"])
                    dve.tensor_tensor(tmp[:, k % 2, :], bank, pickS[:, k - 1, :], ALU.mult).then_inc(s["v_freed"], 1)
            t.w(s["acc_ready"], 2)
            dve.tensor_tensor(y_flat, t.v.take(), x_flat, ALU.add).then_inc(s["v_freed"], 1)
            dve.wait_ge(s["v_freed"], t.v.at)
            t.skip(a=2 + E + (E + 1) * NF)
            norm_vector(t, x, y, "norm_ready")

        def experts_pool(t):
            t.skip(v=2, a=2 + E + (E + 1) * NF)
            for k in range(1, E + 1):
                t.skip(v=1)
                t.eng.wait_ge(s["v_freed"], t.v.at)
                t.eng.tensor_tensor(acc, acc, tmp[:, k % 2, :], ALU.add).then_inc(s["acc_ready"], 1)
                t.w(s["acc_ready"])
            t.skip(v=1)

        class Band:

            def __init__(self, heads, mask, wide_values):
                self.heads, self.mask, self.wide = heads, mask, wide_values
                self.rows = 32 if wide_values == 32 else 64
                self.per = P // self.rows
                self.units = []
                for j in range(NT):
                    nk = 1 if j == 0 else 2
                    for i in range(self.per):
                        for g in range(0, heads // self.per, 4 // nk):
                            hh = [self.per * (g + a) + i for a in range(4 // nk)]
                            self.units.append((j, nk, hh))
                self.per_tile = [sum(1 for u in self.units if u[0] == j) for j in range(NT)]

            def last_of_tile(self, n):
                return n + 1 == len(self.units) or self.units[n + 1][0] != self.units[n][0]

            def cols(self, n):
                return sum(len(hh) for _, _, hh in self.units[:n]), len(self.units[n][2])

        def band_tensor(t, band):
            pe, at = t.eng, {}
            pairs = lambda v, n, z: v.rearrange("p (o z) -> p o z", o=1).to_broadcast([P, n, z])
            U = len(band.units)
            for n in range(U + 3):
                if n < U:
                    j, nk, hh = band.units[n]
                    bank = t.s.open()
                    mask = cbv[band.mask][:, (2 - nk) * P:2 * P]
                    pe.matmul(bank, cbv["ident"], pairs(mask, len(hh), nk * P), start=True, stop=False,
                              skip_group_check=True)
                    for a, h in enumerate(hh):
                        g, r = h // band.per, band.rows * (h % band.per)
                        ins = pe.matmul(bank[:, a * nk * P:(a + 1) * nk * P],
                                        qT[r:r + band.rows, g, j * P:(j + 1) * P],
                                        kT[r:r + band.rows, g, (j + 1 - nk) * P:(j + 1) * P],
                                        start=False, stop=(a == len(hh) - 1), skip_group_check=True)
                    ins.then_inc(s["s_filled"], 1)
                if 2 <= n < U + 2:
                    t.w(s["prob_ready"])
                    bank = t.v.open()
                    for c in range(4):
                        ins = pe.transpose(tok(bank, c), tok(pr[:, (n - 2) % 3, :], c), ident)
                    ins.then_inc(s["v_filled"], 1)
                    at[n - 2] = t.v.at
                if n >= 3:
                    m = n - 3
                    j, nk, hh = band.units[m]
                    pe.wait_ge(s["v_freed"], at[m])
                    if hh[0] == 0:
                        heads_bank = t.o.open()
                    for a, h in enumerate(hh):
                        g, r = h // band.per, band.rows * (h % band.per)
                        for c in range(nk):
                            tile = j + 1 - nk + c
                            if band.wide == 32:
                                v, o = vpad[:, tile, h, :], heads_bank[r:r + 32, 0:P]
                            else:
                                v, o = vv[:, tile, h * 64:(h + 1) * 64], tok(heads_bank, g)[r:r + 64, :]
                            ins = pe.matmul(o, v, pT[:, m % 2, (a * nk + c) * P:(a * nk + c + 1) * P],
                                            start=(g == 0 and c == 0),
                                            stop=(h >= band.heads - band.per and c == nk - 1),
                                            skip_group_check=True)
                    ins.then_inc(s["pT_used"], 1)

        def band_scalar(t, band):
            act = t.eng
            U = len(band.units)
            v0 = t.v.at
            for n in range(U + 3):
                if n < U:
                    j, nk, hh = band.units[n]
                    c0, k = band.cols(n)
                    t.skip(s=1)
                    bank = psS[:, (t.s.at - 1) % 3]
                    t.w(s["max_ready"])
                    if n >= 3:
                        act.wait_ge(s["v_filled"], v0 + n - 2)
                    for a in range(k):
                        z = slice(a * nk * P, (a + 1) * nk * P)
                        ins = act.activation(pr[:, n % 3, z], bank[:, z], ACT.Exp, bias=mx2[:, c0 + a:c0 + a + 1],
                                             accum_out=sums2[:, c0 + a:c0 + a + 1])
                    ins.then_inc(s["s_freed"], 1)
                if 2 <= n < U + 2:
                    t.skip(v=1)
                if n >= 3 and band.last_of_tile(n - 3):
                    j = band.units[n - 3][0]
                    t.w(s["pT_used"], band.per_tile[j])
                    t.skip(o=1)
                    if band.wide == 32:
                        act.activation(tok(oT[:, 0, :], j), psO[:, 0, 0:P], ACT.Copy).then_inc(s["o_freed"], 1)
                    else:
                        act.activation(oT[:, :, j * P:(j + 1) * P], psO[:, 0].rearrange("p (g z) -> p g z", g=4),
                                       ACT.Copy).then_inc(s["o_freed"], 1)

        def band_vector(t, band):
            dve = t.eng
            U = len(band.units)
            s0 = t.s.at
            for n in range(U + 3):
                if n < U:
                    j, nk, hh = band.units[n]
                    c0, k = band.cols(n)
                    bank = t.s.take()
                    dve.tensor_reduce(mx2[:, c0:c0 + k], bank.rearrange("p (a z) -> p a z", a=k), X, ALU.max,
                                      negate=True).then_inc(s["max_ready"], 1)
                if 1 <= n <= U:
                    c0, k = band.cols(n - 1)
                    dve.wait_ge(s["s_freed"], s0 + n)
                    dve.reciprocal(rinv2[:, c0:c0 + k], sums2[:, c0:c0 + k]).then_inc(s["rinv_ready"], 1)
                if 2 <= n < U + 2:
                    if n >= 4:
                        t.w(s["pT_used"])
                    dve.tensor_copy(pT[:, n % 2, :], t.v.take()).then_inc(s["v_freed"], 1)
            t.w(s["pT_used"], 2)
            t.skip(o=NT)

        def band_pool(t, band):
            for n in range(len(band.units)):
                j, nk, hh = band.units[n]
                c0, k = band.cols(n)
                t.w(s["rinv_ready"])
                for a in range(k):
                    z = pr[:, n % 3, a * nk * P:(a + 1) * nk * P]
                    ins = t.eng.tensor_scalar(z, z, rinv2[:, c0 + a:c0 + a + 1], None, ALU.mult)
                ins.then_inc(s["prob_ready"], 1)
            t.skip(s=len(band.units), v=len(band.units), o=NT)

        window, local = Band(H3, "band3", 32), Band(H5, "band5", 64)

        def turn_qk(t, q, k):
            for src in (q, k):
                bank = t.a.open()
                for g in range(4):
                    ins = t.eng.transpose(tok(bank, g), tok(src, g), ident)
                ins.then_inc(s["a_filled"], 1)

        def take_qk(t, i):
            for dst in (qT, kT):
                t.eng.activation(dst[:, :, i * P:(i + 1) * P], t.a.take().rearrange("p (g z) -> p g z", g=4),
                                 ACT.Copy).then_inc(s["a_freed"], 1)

        def window_tensor(t):
            pe = t.eng
            t.w(s["norm_ready"])
            turn_tensor(t, x)
            pe.wait_ge(s["a_freed"], t.a.at)
            bank = t.v.open()
            for i in range(NT):
                ins = pe.matmul(tok(bank, i), tok(xTn, i), W("window", "w_v"), start=(i == 0), stop=(i == NT - 1),
                                skip_group_check=True)
            ins.then_inc(s["v_filled"], 1)
            for i in range(NT + 1):
                if i < NT:
                    pe.matmul(t.v.open(), tok(xTn, i), W("window", "w_qk"), start=True, stop=True)\
                        .then_inc(s["v_filled"], 1)
                if i >= 1:
                    t.w(s["rope_ready"])
                    turn_qk(t, qpad[:, (i - 1) % 2, :], kpad[:, (i - 1) % 2, :])
            pe.wait_ge(s["a_freed"], t.a.at)
            band_tensor(t, window)
            pe.wait_ge(s["o_freed"], t.o.at)
            bank = t.o.open()
            pe.matmul(bank, ones[0:1, :], row("b_win"), start=True, stop=False, skip_group_check=True)
            for i in range(NT):
                ins = pe.matmul(tok(bank, i), tok(oT[:, 0, :], i), W("window", "w_o"), start=False,
                                stop=(i == NT - 1), skip_group_check=True)
            ins.then_inc(s["o_filled"], 1)

        def window_scalar(t):
            plain_scalar(t)
            for i in range(NT):
                take_qk(t, i)
            t.skip(v=1 + NT)
            band_scalar(t, window)
            t.skip(o=1)

        def window_vector(t):
            dve = t.eng
            t.skip(a=1)
            bank = t.v.take().rearrange("p (t h d) -> p t h d", t=NT, h=H3)
            for g in range(4):
                for i in range(NT):
                    ins = dve.tensor_copy(vpad[:, i, 4 * g:4 * g + 4, 8 * g:8 * g + 8],
                                          bank[:, i, 4 * g:4 * g + 4, :])
            ins.then_inc(s["v_freed"], 1)
            rope = W("const", "rope3", t=NT, f=2, q=2)
            for i in range(NT):
                bank = t.v.take().rearrange("p (f q h d) -> p f q h d", f=2, q=2, h=H3)
                for f, dst in ((0, ra), (1, rb)):
                    for q in range(2):
                        by = rope[:, i, f, q:q + 1, :].to_broadcast([P, H3, DH3])
                        ins = dve.tensor_tensor(dst[:, i % 2, q * P:(q + 1) * P].rearrange("p (h d) -> p h d", h=H3),
                                                bank[:, f, q], by, ALU.mult)
                ins.then_inc(s["v_freed"], 1)
                dve.wait_ge(s["v_freed"], t.v.at)
                if i >= 2:
                    dve.wait_ge(s["a_freed"], t.a.at - 2)
                for q, dst in ((0, qpad), (1, kpad)):
                    h = lambda v: v[:, i % 2, q * P:(q + 1) * P].rearrange("p (h d) -> p h d", h=H3)
                    ins = dve.tensor_tensor(dst[:, i % 2, :].rearrange("p (h z) -> p h z", h=H3)[:, :, 0:DH3],
                                            h(ra), h(rb), ALU.add)
                ins.then_inc(s["rope_ready"], 1)
                t.skip(a=2)
            band_vector(t, window)
            residual_vector(t, y_flat)
            norm_vector(t, x, y, "norm_ready")

        def window_pool(t):
            t.skip(a=1 + 2 * NT, v=1 + NT)
            band_pool(t, window)
            t.skip(o=1)

        def shift_scalar(t):
            bank = t.a.take()
            t.eng.activation(hT[0:64, :], bank[0:64, :], ACT.Copy)
            t.eng.activation(hT[64:P, 1:T], bank[64:P, 0:T - 1], ACT.Copy).then_inc(s["a_freed"], 1)

        def local_tensor(t, l):
            pe = t.eng
            w_qkv = W("local", "w_qkv", l=DEPTH)[:, l]
            if l == 0:
                t.w(s["norm_ready"])
            else:
                pe.wait_ge(s["o_freed"], t.o.at)
            turn_tensor(t, x)
            pe.wait_ge(s["a_freed"], t.a.at)
            for i in range(NT + 1):
                if i < NT:
                    for c, ring, sig in ((0, t.a, "a_filled"), (1, t.a, "a_filled"), (2, t.v, "v_filled")):
                        pe.matmul(ring.open(), tok(hT, i), w_qkv[:, c * 512:(c + 1) * 512],
                                  start=True, stop=True).then_inc(s[sig], 1)
                if i >= 1:
                    t.w(s["rope_ready"])
                    turn_qk(t, ra[:, (i - 1) % 2, 0:512], ra[:, (i - 1) % 2, 512:1024])
            pe.wait_ge(s["a_freed"], t.a.at)
            band_tensor(t, local)
            pe.wait_ge(s["o_freed"], t.o.at)
            bank = t.o.open()
            w_o = W("local", "w_o", l=DEPTH, g=4)
            for i in range(NT):
                for g in range(4):
                    ins = pe.matmul(tok(bank, i), tok(oT[:, g, :], i), w_o[:, l, g, :],
                                    start=(i == 0 and g == 0), stop=(i == NT - 1 and g == 3), skip_group_check=True)
            ins.then_inc(s["o_filled"], 1)
            pe.wait_ge(s["o_freed"], t.o.at)
            turn_tensor(t, x)
            pe.wait_ge(s["a_freed"], t.a.at)
            pe.matmul(t.v.open(), mean_w, hT[:, :], start=True, stop=True).then_inc(s["v_filled"], 1)
            t.w(s["sq_ready"])
            pe.matmul(t.a.open(), mean_w, sq, start=True, stop=True).then_inc(s["a_filled"], 1)
            t.w(s["hn_ready"])
            w1 = W("local", "w1", l=DEPTH)[:, l]
            for c in range(NH):
                m = HC[c]
                pe.matmul(t.a.open()[0:m, :], w1[:, HID + c * P:HID + c * P + m], hc, start=True, stop=True)\
                    .then_inc(s["a_filled"], 1)
                pe.matmul(t.v.open()[0:m, :], w1[:, c * P:c * P + m], hc, start=True, stop=True)\
                    .then_inc(s["v_filled"], 1)
            bank = t.o.open()
            pe.matmul(bank, ones[0:1, :], row(f"b2_{l}"), start=True, stop=False, skip_group_check=True)
            w2 = W("local", "w2", l=DEPTH, c=NH)
            pe.wait_ge(s["v_freed"], t.v.at)
            for c in range(NH):
                for i in range(NT):
                    ins = pe.matmul(tok(bank, i), tok(uu[0:HC[c], c, :], i), w2[0:HC[c], l, c, :], start=False,
                                    stop=(i == NT - 1 and c == NH - 1), skip_group_check=True)
            ins.then_inc(s["o_filled"], 1)

        def local_scalar(t, l):
            act = t.eng
            shift_scalar(t)
            for i in range(NT + 1):
                if i < NT:
                    if i >= 2:
                        t.w(s["rope_ready"])
                    for c in range(2):
                        bank, z = t.a.take(), slice(512 * c, 512 * c + 512)
                        act.activation(rb[:, i % 2, z], bank, ACT.Square)
                        act.activation(qk[:, i % 2, z], bank, ACT.Copy).then_inc(s["a_freed"], 1)
                    t.skip(v=1)
                    t.w(s["ss_ready"])
                    z = small[:, 2 * (i % 2), 0:16]
                    t.w.step(act.activation(z, z, ACT.Ln, scale=2.0 ** 20))
                    act.activation(small[:, 2 * (i % 2) + 1, 0:16], z, ACT.Exp, scale=-0.5, bias=ten_ln2)\
                        .then_inc(s["rn_ready"], 1)
                if i >= 1:
                    take_qk(t, i - 1)
            t.w(s["rope_ready"], 2)
            band_scalar(t, local)
            t.skip(o=1)
            shift_scalar(t)
            t.skip(v=1)
            act.wait_ge(s["v_freed"], t.v.at)
            act.activation(sq, hc, ACT.Square).then_inc(s["sq_ready"], 1)
            act.activation(rst, t.a.take(), ACT.Ln, bias=eps).then_inc(s["a_freed"], 1)
            act.wait_ge(s["a_freed"], t.a.at)
            act.activation(rst, rst, ACT.Exp, scale=-0.5).then_inc(s["rst_ready"], 1)
            b1 = W("local", "b1", l=DEPTH, f=2)
            for c in range(NH):
                m = HC[c]
                act.activation(gg[0:m, c, :], t.a.take()[0:m, :], ACT.Gelu, bias=b1[0:m, l, 1, c:c + 1])\
                    .then_inc(s["a_freed"], 1)
            t.skip(v=NH, o=1)

        def local_vector(t, l):
            dve = t.eng
            t.skip(a=1)
            if l == 0:
                t.w.step(dve.tensor_copy(y_flat, x_flat))
            by = tab5[:, l].rearrange("p (q f) t d -> p f t q d", q=2)
            for i in range(NT):
                j = i % 2
                t.skip(a=2)
                dve.tensor_copy(vv[:, i, :], t.v.take()).then_inc(s["v_freed"], 1)
                dve.wait_ge(s["a_freed"], t.a.at)
                ss = small[:, 2 * j, 0:16]
                h = lambda v: v[:, j, :].rearrange("p (h d) -> p h d", h=2 * H5)
                t.w.step(dve.tensor_reduce(ss, h(rb), X, ALU.add))
                dve.tensor_scalar(ss, ss, 1e-24, None, ALU.max).then_inc(s["ss_ready"], 1)
                t.w(s["rn_ready"])
                rn = small[:, 2 * j + 1, 0:16].rearrange("p (h o) -> p h o", o=1).to_broadcast([P, 2 * H5, DH5])
                dve.tensor_tensor(h(qk), h(qk), rn, ALU.mult).then_inc(s["qn_ready"], 1)
                dve.wait_ge(s["qn_ready"], l * NT + i + 1)
                if i >= 2:
                    dve.wait_ge(s["a_freed"], ra_at)
                for q in range(2):
                    z = lambda v: v[:, j, q * 512:(q + 1) * 512].rearrange("p (h d) -> p h d", h=H5)
                    ins = dve.tensor_tensor(z(ra), z(qk), tab5[:, l, 2 * q, i:i + 1, :].to_broadcast([P, H5, DH5]), ALU.mult)
                t.w.step(ins)
                t.w(s["rot_ready"])
                dve.tensor_tensor(ra[:, j, :], ra[:, j, :], rb[:, j, :], ALU.add).then_inc(s["rope_ready"], 1)
                if i >= 1:
                    t.skip(a=2)
                ra_at = t.a.at
            t.skip(a=2)
            band_vector(t, local)
            residual_vector(t, x_flat)
            t.skip(a=1)
            dve.tensor_tensor(hc, hT[:, :], t.v.take(), ALU.subtract).then_inc(s["v_freed"], 1)
            t.skip(a=1)
            t.w(s["rst_ready"])
            t.w.step(dve.tensor_tensor(hc, hc, rst, ALU.mult))
            dve.tensor_scalar(hc, hc, W("local", "ln_g")[:, l:l + 1], W("local", "ln_b")[:, l:l + 1],
                              ALU.mult, ALU.add).then_inc(s["hn_ready"], 1)
            b1 = W("local", "b1", l=DEPTH, f=2)
            for c in range(NH):
                m = HC[c]
                t.skip(a=1)
                bank = t.v.take()
                dve.wait_ge(s["a_freed"], t.a.at)
                dve.scalar_tensor_tensor(uu[0:m, c, :], bank[0:m, :], b1[0:m, l, 0, c:c + 1], gg[0:m, c, :],
                                         ALU.add, ALU.mult).then_inc(s["v_freed"], 1)
            residual_vector(t, x_flat)
            if l == DEPTH - 1:
                t.w.step(dve.tensor_tensor(y_flat, y_flat, x_flat, ALU.add))
                norm_vector(t, x, y, "y_ready")

        def local_pool(t, l):
            for i in range(NT):
                t.w(s["qn_ready"])
                for q in range(2):
                    z = lambda v: v[:, i % 2, q * 512:(q + 1) * 512].rearrange("p (h a d) -> p h a d", h=H5, a=2)
                    for a in range(2):
                        by = tab5[:, l, 2 * q + 1, i:i + 1, 32 * a:32 * a + 32].to_broadcast([P, H5, 32])
                        ins = t.eng.tensor_tensor(z(rb)[:, :, a, :], z(qk)[:, :, 1 - a, :], by, ALU.mult)
                ins.then_inc(s["rot_ready"], 1)
            t.skip(a=1 + 4 * NT, v=NT)
            band_pool(t, local)
            t.skip(a=2 + NH, v=1 + NH, o=2)

        with nc.Fori(0, B) as b:
            with nc.Block() as block:
                @block.sync
                def _(sp):
                    sp.dma_start(x[:, :, :], x_in[b].rearrange("(t p) d -> p t d", p=P)).then_inc(s["x_loaded"], 16)
                    if last == 7:
                        sp.wait_ge(s["y_ready"], 1)
                    else:
                        sp.wait_ge(s["norm_ready"], [0, 1, 3, 4, 5, 6][last])
                    sp.dma_start(out[b].rearrange("(t p) d -> p t d", p=P), x[:, :, :]).then_inc(s["stored"], 16)
                    sp.wait_ge(s["stored"], 16)

                @block.gpsimd
                def _(pool):
                    t = lanes["pool"] = Lane(pool, s, "pool_step", ps)
                    t.skip(a=8, v=1 + 2 * NS, s=2, o=1)
                    t.end(0)
                    if last > 1:
                        cross_pool(t)
                        t.end(1)
                    if last > 2:
                        experts_pool(t)
                        t.end(2)
                    if last > 3:
                        window_pool(t)
                        t.end(3)
                    if last > 4:
                        cross_pool(t)
                        t.end(4)
                    if last > 5:
                        for l in range(DEPTH):
                            local_pool(t, l)
                            t.end(5 + l)

                @block.scalar
                def _(act):
                    t = lanes["act"] = Lane(act, s, "act_step", ps)
                    mamba_scalar(t)
                    t.end(0)
                    norm_scalar(t)
                    if last > 1:
                        cross_scalar(t, DH1 ** -0.5, True)
                        t.end(1)
                        norm_scalar(t)
                    if last > 2:
                        experts_scalar(t)
                        t.end(2)
                        norm_scalar(t)
                    if last > 3:
                        window_scalar(t)
                        t.end(3)
                        norm_scalar(t)
                    if last > 4:
                        cross_scalar(t, DH3 ** -0.5, False)
                        t.end(4)
                        norm_scalar(t)
                    if last > 5:
                        for l in range(DEPTH):
                            local_scalar(t, l)
                            t.end(5 + l)
                        norm_scalar(t)

                @block.vector
                def _(dve):
                    t = lanes["dve"] = Lane(dve, s, "dve_step", ps)
                    mamba_vector(t)
                    t.end(0)
                    if last > 1:
                        cross_vector(t, True)
                        t.end(1)
                    if last > 2:
                        experts_vector(t)
                        t.end(2)
                    if last > 3:
                        window_vector(t)
                        t.end(3)
                    if last > 4:
                        cross_vector(t, False)
                        t.end(4)
                    if last > 5:
                        for l in range(DEPTH):
                            local_vector(t, l)
                            t.end(5 + l)

                @block.tensor
                def _(pe):
                    t = lanes["pe"] = Lane(pe, s, None, ps)
                    mamba_tensor(t)
                    t.end(0)
                    if last > 1:
                        cross_tensor(t, b, y, score0, value0, row_x0)
                        t.end(1)
                    if last > 2:
                        experts_tensor(t)
                        t.end(2)
                    if last > 3:
                        window_tensor(t)
                        t.end(3)
                    if last > 4:
                        cross_tensor(t, b, x, score1, value1, row("b_x1"))
                        t.end(4)
                    if last > 5:
                        for l in range(DEPTH):
                            local_tensor(t, l)
                            t.end(5 + l)
            nc.sync.sem_clear(sems)
            nc.all_engine_barrier()
        for n, t in lanes.items():
            for got, want in zip(t.log, lanes["pe"].log):
                assert got == want, f"{n} counts the rings otherwise: {got} for {want}"


def shape_constants(group):
    c, f = {}, np.float32
    c["ident"] = np.eye(P, dtype=f)
    c["mean"] = np.full((P, P), 1.0 / P, f)
    t = np.arange(T, dtype=np.float64)
    inv = 1.0 / 10000.0 ** (np.arange(0, DH3, 2) / DH3)
    ang = (t[:, None] * inv[None]).astype(f).astype(np.float64)
    cos, sin = np.tile(np.cos(ang), 2), np.tile(np.sin(ang), 2)
    sin[:, :DH3 // 2] *= -1
    r = np.stack([np.stack([cos * DH3 ** -0.5, cos], 1), np.stack([sin * DH3 ** -0.5, sin], 1)], 1)
    c["rope3"] = r.reshape(NT, P, 2 * 2 * DH3).transpose(1, 0, 2).reshape(P, -1)
    half = np.arange(0, DH5, 2)
    inv = 1.0 / 10000.0 ** (half / DH5)
    ang = (t[:, None] * inv[None]).astype(f).astype(np.float64)
    cos, sin = np.tile(np.cos(ang), 2), np.tile(np.sin(ang), 2)
    sin[:, :DH5 // 2] *= -1
    base = (half + 0.4 * DH5) / (1.4 * DH5)
    scale = np.tile(base[None] ** ((t - T // 2) / 32.0)[:, None], 2)
    r = np.stack([cos * scale * 8.0, sin * scale * 8.0, cos / scale, sin / scale])
    c["tables"] = r.reshape(4, NT, P, DH5).transpose(2, 0, 1, 3).reshape(P, -1)
    p = np.arange(P)
    c["pair"] = (p[:, None] // 64 == np.arange(2)[None]).astype(f)
    c["head"] = (p[:, None] // DH3 == np.arange(H3)[None]).astype(f)
    c["iota"] = np.tile(np.arange(E, dtype=f), (P, 1))
    c["eps"] = np.full((P, 1), EPS, f)
    c["ten_ln2"] = np.full((P, 1), 10 * np.log(2.0), f)
    c["one"] = np.ones((P, 1), f)
    return np.concatenate([np.asarray(c[n], f) for n in GROUPS[group]], axis=1)


def bf16_constants(bf16):
    q, k = np.arange(P)[:, None], np.arange(P)[None]
    band = lambda prev, cur: np.where(np.concatenate([prev, cur], 1), 0.0, NEG)
    sel = (np.arange(P)[:, None] % 32 == np.arange(2 * NS)[None]).astype(np.float32)
    parts = [np.eye(P), band(k >= q + 1, k <= q), band(k >= q + 64, (k <= q) & (q - k <= 64)), sel]
    return np.concatenate(parts, axis=1).astype(bf16)


def blocks(a, rows=P):
    n = a.shape[0] // rows
    return a.reshape(n, rows, -1).transpose(1, 0, 2).reshape(rows, -1)


def fill(a, rows=P):
    out = np.zeros((rows,) + a.shape[1:], a.dtype)
    out[:a.shape[0]] = a
    return out


def col(a):
    return np.asarray(a).reshape(-1, P).T


def spread(a):
    return np.broadcast_to(np.asarray(a).reshape(1, -1), (P, a.size))


def pack(w):
    g = {n: {} for n in GROUPS}
    m = g["mamba"]
    m["w_in"] = w["L0_attn_in_proj_w"].T
    m["w_conv"] = spread(np.ascontiguousarray(w["L0_attn_conv_w"][:, 0, :].T))
    m["norm_w"] = w["L0_attn_norm_w"][:, None]
    m["conv_b"] = col(w["L0_attn_conv_b"])
    xp = w["L0_attn_x_proj_w"]
    bc = xp[DTR:]
    m["x_bc"] = blocks(np.ascontiguousarray(np.concatenate([bc, bc, bc], 0).T))
    m["x_dt"] = blocks(np.ascontiguousarray(xp[:DTR].T))
    m["w_dt"] = fill(w["L0_attn_dt_proj_w"].T)
    m["b_dt"] = col(w["L0_attn_dt_proj_b"])
    m["a_log"] = blocks(w["L0_attn_A_log"])
    m["d_skip"] = col(w["L0_attn_D"])
    m["w_out"] = blocks(np.ascontiguousarray(w["L0_attn_out_proj_w"].T))
    c = g["cross0"]
    c["ctx"] = w["ctx_1024"].reshape(B * S, D).T
    c["w_qT"] = blocks(np.ascontiguousarray(w["L0_xattn_w_q"].T))
    c["w_k"] = w["L0_xattn_w_kv"][:, :1024]
    c["w_v"] = w["L0_xattn_w_kv"][:, 1024:]
    c["w_o"] = blocks(w["L0_xattn_w_out"])
    g["experts"]["gamma"] = col(w["L0_xattn_ln_gamma"])
    g["experts"]["beta"] = col(w["L0_xattn_ln_beta"])
    c["gate"] = spread(w["L0_xattn_gate"])
    c["w4_q"] = w["L1_xattn_Wq"]
    c["w4_k"] = w["L1_xattn_Wkv"][:D].T
    c["w4_v"] = w["L1_xattn_Wkv"][D:].T
    c["w4_o"] = w["L1_xattn_Wout"].T
    e = g["experts"]
    w1 = np.concatenate([w["L0_ffn_shared_w1"][None], w["L0_ffn_spec_w1"]], 0)
    e["w1"] = w1.reshape(-1, D).T
    b1 = np.concatenate([w["L0_ffn_shared_b1"][None], w["L0_ffn_spec_b1"]], 0)
    e["b1"] = col(b1)
    w2 = np.concatenate([w["L0_ffn_shared_w2"][None], w["L0_ffn_spec_w2"]], 0)
    e["w2"] = w2.reshape(E + 1, D, NF, P).transpose(3, 0, 2, 1).reshape(P, -1)
    e["b2s"] = col(w["L0_ffn_shared_b2"])
    e["router"] = w["L0_ffn_router_w"].T
    e["b2e"] = fill(w["L0_ffn_spec_b2"])
    h = DH3 // 2
    turned = lambda a: np.concatenate([a.reshape(H3, 2, h, D)[:, 1:], a.reshape(H3, 2, h, D)[:, :1]], 1).reshape(D, D)
    wq, wk = w["L1_attn_Wq"], w["L1_attn_Wk"]
    g["window"]["w_qk"] = np.concatenate([wq, wk, turned(wq), turned(wk)], 0).T
    g["window"]["w_v"] = w["L1_attn_Wv"].T
    g["window"]["w_o"] = w["L1_attn_Wo"].T.reshape(4, 4, DH3, D).transpose(1, 0, 2, 3).reshape(D, D)
    f = g["local"]
    f["w_qkv"] = w["L1_ffn_wqkv"].transpose(1, 0, 2).reshape(P, -1)
    qs, ks = w["L1_ffn_q_scale"], w["L1_ffn_k_scale"]
    swap = lambda a: np.concatenate([a[:, 32:], a[:, :32]], 1)
    c["scales"] = spread(np.stack([qs, swap(qs), ks, swap(ks)], 1))
    f["w_o"] = w["L1_ffn_wo"].reshape(DEPTH, 4, P, D).transpose(2, 0, 1, 3).reshape(P, -1)
    f["ln_g"], f["ln_b"] = w["L1_ffn_ln_g"].T, w["L1_ffn_ln_b"].T
    f["w1"] = w["L1_ffn_w1"].transpose(1, 0, 2).reshape(P, -1)
    b1 = np.zeros((DEPTH, 2, NH * P), np.float32)
    b1[:, :, :HID] = w["L1_ffn_b1"].reshape(DEPTH, 2, HID)
    f["b1"] = b1.reshape(DEPTH * 2 * NH, P).T
    w2 = np.zeros((DEPTH, NH * P, D), np.float32)
    w2[:, :HID] = w["L1_ffn_w2"]
    f["w2"] = w2.reshape(DEPTH * NH, P, D).transpose(1, 0, 2).reshape(P, -1)
    r = g["rows"]
    r["b_x0"], r["b_win"], r["b_x1"] = w["L0_xattn_b_out"][None], w["L1_attn_bo"][None], w["L1_xattn_bout"][None]
    r["b2_0"], r["b2_1"] = w["L1_ffn_b2"][0:1], w["L1_ffn_b2"][1:2]
    r["ones"] = np.ones((1, P), np.float32)
    r["router"] = w["L0_ffn_router_b"][None]
    out = {}
    for n, cols in GROUPS.items():
        if n in ("const", "rope5"):
            out[n] = shape_constants(n)
            continue
        for k, width in cols.items():
            assert g[n][k].shape == (ROWS.get(n, P), width), (n, k, g[n][k].shape, width)
        out[n] = np.ascontiguousarray(np.concatenate([g[n][k] for k in cols], axis=1))
    return out


LAST = 7


def kernel(**inputs):
    import concourse.bacc as bacc
    from concourse.bass_utils import run_bass_kernel_spmd

    w = {n: np.asarray(v) for n, v in inputs.items()}
    arrays = {"in_" + n: v for n, v in pack(w).items()}
    arrays["in_x"] = np.ascontiguousarray(w["x"])
    arrays["in_bf16"] = bf16_constants(mybir.dt.np(BF16))
    nc = bacc.Bacc("TRN2", target_bir_lowering=False, num_devices=1)
    aps = {n: nc.dram_tensor(n, a.shape, mybir.dt.from_np(a.dtype), kind="ExternalInput").ap()
           for n, a in arrays.items()}
    out = nc.dram_tensor("out", (B, T, D), F32, kind="ExternalOutput").ap()
    decoder_kernel(nc, aps["in_x"], {g: aps["in_" + g] for g in GROUPS}, aps["in_bf16"], out, LAST)
    r = run_bass_kernel_spmd(nc, [arrays], core_ids=[0])
    return r.results[0]["out"]
```

```python
from contextlib import ExitStack

import numpy as np

import concourse.bass as bass
from concourse import mybir

F32 = mybir.dt.float32
BF16 = mybir.dt.bfloat16
U32 = mybir.dt.uint32
ACT = mybir.ActivationFunctionType
ALU = mybir.AluOpType
X = mybir.AxisListType.X

B, T, D = 4, 512, 128
P = 128
NT = T // P
S = 32
CH, NS, KC, DTR = 256, 16, 4, 8
NB = CH // P
H1, DH1 = 16, 64
E, FF = 8, 512
NF = FF // P
H3, DH3 = 16, 8
H5, DH5 = 8, 64
HID = 341
NH = 3
HC = [min(P, HID - P * c) for c in range(NH)]
DEPTH = 2
EPS = 1e-5
SCRATCH = 12288
NEG = -1e30

GROUPS = {
    "mamba": dict(w_in=512, w_conv=KC * CH, norm_w=1, conv_b=NB, x_bc=NB * 96, x_dt=NB * DTR,
                  w_dt=CH, b_dt=NB, a_log=NB * NS, d_skip=NB, w_out=NB * D),
    "cross0": dict(ctx=B * S, w_qT=8 * P, w_k=1024, w_v=1024, w_o=8 * P, gate=1,
                   w4_q=D, w4_k=D, w4_v=D, w4_o=D,
                   scales=DEPTH * 4 * DH5),
    "rope5": dict(tables=NT * 4 * DH5),
    "experts": dict(b1=(E + 1) * NF, b2s=1, router=E, b2e=D, gamma=1, beta=1),
    "window": dict(w_qk=4 * D, w_v=D, w_o=D),
    "local": dict(w_qkv=DEPTH * 1536, w_o=DEPTH * 4 * D, ln_g=DEPTH, ln_b=DEPTH,
                  w1=DEPTH * 2 * HID, b1=DEPTH * 2 * NH, w2=DEPTH * NH * D),
    "rows": dict(b_x0=D, b_win=D, b_x1=D, b2_0=D, b2_1=D, router=E, ones=P),
    "const": dict(ident=P, mean=P, rope3=NT * 2 * 2 * DH3,
                  pair=2, head=H3, iota=E, eps=1, neg_half=1, one=1),
}
WIDTH = {g: sum(c.values()) for g, c in GROUPS.items()}
ROWS = {"rows": 1}
CB = dict(ident=P, band3=2 * P, band5=2 * P, select=2 * NS)


STATES_AT, STATE_STEP = 40, 4
CROSS_STEP, EXPERT_STEP, ROPE_STEP, QKV_STEP, WINDOW_STEP, LOCAL_STEP, GEGLU = 5, 8, 4, 9, 3.5, 3.5, 40
LAG = 2
MAMBA_END = STATES_AT + STATE_STEP * 16 + 16
CROSS_END = 12 + CROSS_STEP * 6 + 8
EXPERTS_END = 10 + EXPERT_STEP * 9 + 28


class Waits:

    def __init__(self, eng, own):
        self.eng, self.own, self.asked, self.steps = eng, own, {}, 0

    def __call__(self, sem, k=1):
        n = self.asked.get(sem.name, 0) + k
        self.asked[sem.name] = n
        if n > 0:
            self.eng.wait_ge(sem, n)

    def step(self, ins):
        self.steps += 1
        ins.then_inc(self.own, 1)
        self.eng.wait_ge(self.own, self.steps)


class Ring:

    def __init__(self, eng, banks, filled, freed):
        self.eng, self.banks, self.n, self.filled, self.freed, self.at = eng, banks, len(banks), filled, freed, 0

    def use(self, n):
        self.n = n

    def bank(self):
        return self.banks[(self.at - 1) % self.n]

    def open(self):
        if self.at >= self.n:
            self.eng.wait_ge(self.freed, self.at - self.n + 1)
        self.at += 1
        return self.bank()

    def take(self):
        self.at += 1
        self.eng.wait_ge(self.filled, self.at)
        return self.bank()


class Lane:

    def __init__(self, eng, s, own, ps, m=None):
        self.eng, self.s, self.m, self.w = eng, s, m, Waits(eng, s[own] if own else None)
        self.a = Ring(eng, ps["a"], s["a_filled"], s["a_freed"])
        self.v = Ring(eng, ps["v"], s["v_filled"], s["v_freed"])
        self.o = Ring(eng, ps["o"], s["o_filled"], s["o_freed"])
        self.s_ = Ring(eng, ps["s"], s["s_filled"], s["s_freed"])
        self.at_s = 0
        self.log = []

    def counts(self):
        return self.a.at, self.v.at, self.o.at, self.s_.at

    def skip(self, a=0, v=0, s=0, o=0):
        self.a.at += a
        self.v.at += v
        self.o.at += o
        self.s_.at += s


class Row:
    pass


def run(lane, stages):
    for start, stage in stages:
        for at in stage:
            yield start + at
        lane.log.append(lane.counts())


def interleave(first, second):
    now = [next(first, None), next(second, None)]
    while now[0] is not None or now[1] is not None:
        if now[1] is None or (now[0] is not None and now[0] <= now[1]):
            now[0] = next(first, None)
        else:
            now[1] = next(second, None)


def decoder_kernel(nc, x_in, packed, cb_in, experts_in, folded_dram, out):
    with ExitStack() as ctx:
        def sb(name, shape, dt=F32):
            return ctx.enter_context(nc.sbuf_tensor(name, shape, dt))

        def sem(name):
            return ctx.enter_context(nc.semaphore(name))

        psum = ctx.enter_context(nc.psum_tensor("psum", [P, 8, 512], F32))
        bank = [psum[:, i] for i in range(8)]
        ps = [dict(a=bank[i:i + 2], s=bank[i:i + 2], v=bank[i + 2:i + 4], o=bank[i + 3:i + 4]) for i in (0, 4)]

        scratch = [sb("scratch_0", [P, SCRATCH]), sb("scratch_1", [P, SCRATCH])]
        used = [0, 0]

        def carve(of, *shape):
            n = int(np.prod(shape))
            v = scratch[of][:, used[of]:used[of] + n]
            used[of] += n
            assert used[of] <= SCRATCH, used
            names = "abcde"[:len(shape)]
            if len(shape) == 1:
                return v
            return v.rearrange(f"p ({' '.join(names)}) -> p {' '.join(names)}",
                               **dict(zip(names[:-1], shape[:-1])))

        def again(of, at=0):
            used[of] = at

        wt, cols = {}, {}
        for g, c in GROUPS.items():
            if g in ("cross0", "rope5"):
                wt[g] = carve(1, WIDTH[g])
            else:
                wt[g] = sb("w_" + g, [ROWS.get(g, P), WIDTH[g]])
            at = 0
            for n, w in c.items():
                cols[g, n] = (at, at + w)
                at += w

        def W(group, name, **dims):
            a, b = cols[group, name]
            v = wt[group][:, a:b]
            if dims:
                v = v.rearrange(f"p ({' '.join(dims)} z) -> p {' '.join(dims)} z", **dims)
            return v

        cb = sb("cb", [P, sum(CB.values())], BF16)
        cbv, at = {}, 0
        for n, w in CB.items():
            cbv[n] = cb[:, at:at + w]
            at += w
        ident, mean_w, ones = W("const", "ident"), W("const", "mean"), W("rows", "ones")
        eps, one = W("const", "eps"), W("const", "one")
        row = lambda n: W("rows", n).rearrange("p (o z) -> p o z", o=1).to_broadcast([1, NT, D])

        w_in = W("mamba", "w_in")
        w_conv = W("mamba", "w_conv", k=KC)
        a_neg = sb("a_neg", [P, NB, NS])
        gate = sb("gate", [P, 1])
        b_x0 = W("rows", "b_x0")
        tab5 = sb("tab5", [P, DEPTH, 4, NT, DH5])

        NE = 3
        we = sb("expert_weights", [P, NE, 2 * FF])

        kbd, vbd = carve(0, B, 512), carve(0, B, 512)
        folded = carve(0, 2, 1024)
        row_x0 = b_x0.rearrange("p (o z) -> p o z", o=1).to_broadcast([1, NT, D])

        def row_buffers(i):
            m = Row()
            own = lambda name, shape, dt=F32: sb(f"{name}_{i}", shape, dt)
            m.x = own("x", [P, NT, D])
            m.y = own("y", [P, NT, D])
            m.xT = own("xT", [P, T + KC - 1])
            m.xTn = m.xT[:, KC - 1:KC - 1 + T]
            m.x_flat = m.x[:, :, :].rearrange("p t d -> p (t d)")
            m.y_flat = m.y[:, :, :].rearrange("p t d -> p (t d)")
            m.hT = own("hT", [P, T])
            m.rowstat = own("rowstat", [P, NT, 6])
            m.mv, m.rstd = own("mv", [P, NT, 2]), own("rstd", [P, NT])
            m.small = own("small", [P, 6, 16])
            m.mx, m.sums, m.rinv = (own(n, [P, 2, H1]) for n in ("mx", "sums", "rinv"))
            m.mx2, m.sums2, m.rinv2 = (own(n, [P, 64]) for n in ("mx2", "sums2", "rinv2"))
            m.m8, m.i8 = own("m8", [P, NT, 8]), own("i8", [P, NT, 8], U32)
            m.lg, m.comb, m.eqt = (own(n, [P, NT, E]) for n in ("lg", "comb", "eqt"))
            m.folded = own("folded", [P, 1024])
            m.score = m.folded[:, 0:512]
            m.value = m.folded[:, 512:1024].rearrange("p (j d) -> p j d", j=4)
            again(i)
            m.u, m.zs, m.delta, m.du = (carve(i, NB, T) for _ in range(4))
            m.dA = carve(i, 4, T)
            early = used[i]
            m.dBu, m.hs, m.hC = carve(i, 2, T), carve(i, 2, T), carve(i, 4, T)
            m.mid = carve(i, T // 2).bitcast(BF16)
            m.parts = carve(i, T // 2).bitcast(BF16)
            again(i, early)
            m.rest, m.dtS = carve(i, T), carve(i, T)
            again(i, early + 4 * T)
            m.sp1, m.sp2 = carve(i, NB, T), carve(i, NB, T)
            m.yg = m.delta
            again(i)
            m.e1, m.pT1 = carve(i, 2, T), carve(i, 2, 4, P)
            again(i)
            m.hid, m.pickS, m.acc, m.tmp = carve(i, 2, NF, T), carve(i, E, T), carve(i, T), carve(i, 2, T)
            m.combT = carve(i, T)
            again(i)
            m.qk, m.ra, m.rb = carve(i, 2, 1024), carve(i, 2, 1024), carve(i, 2, 1024)
            after = used[i]
            m.qT, m.kT, m.vv = carve(i, 4, T), carve(i, 4, T), carve(i, NT, 512)
            again(i)
            m.pr, m.pT, m.oT = carve(i, 3, 512), carve(i, 2, 512), carve(i, 4, T)
            assert used[i] <= after
            again(i, used[i] - 3 * T)
            m.qpad, m.kpad = carve(i, 2, 512), carve(i, 2, 512)
            m.ra3, m.rb3 = carve(i, 2, 256), carve(i, 2, 256)
            assert used[i] <= after
            again(i, SCRATCH - NT * H3 * 32)
            m.vpad = carve(i, NT, H3, 32)
            again(i)
            m.hc, m.sq, m.rst, m.gg, m.uu = carve(i, T), carve(i, T), carve(i, T), carve(i, NH, T), carve(i, NH, T)
            return m

        rows = [row_buffers(0), row_buffers(1)]

        own_names = ("act_step dve_step pool_step a_filled a_freed v_filled v_freed o_filled o_freed s_filled s_freed "
                     "stats_ready rstd_ready norm_ready score_loaded e_ready rinv_ready prob_ready pT_used x_loaded "
                     "squares_ready rms_ready soft_ready delta_ready parts_ready decay_ready decay_used states_used "
                     "sum_filled sums_read gated_ready gap_ready ratio_ready comb_ready acc_ready pads_ready "
                     "max_ready ss_ready rn_ready qn_ready rot_ready rope_ready sq_ready rst_ready hn_ready "
                     "y_ready stored ")
        shared_names = ("loaded cb_loaded setup_act slot0_stored slot1_stored "
                        "expert0_loaded expert1_loaded expert2_loaded ")
        shared = {n: sem(n) for n in shared_names.split()}
        sems_of = [dict(shared, **{n: sem(f"row{i}_{n}") for n in own_names.split()}) for i in (0, 1)]
        s = sems_of[0]
        every = {v.num for d in sems_of for v in d.values()}
        sems = range(min(every), max(every) + 1)
        assert len(sems) == len(every)

        with nc.Block() as block:
            @block.sync
            def _(sp):
                for g in GROUPS:
                    sp.dma_start(wt[g][:, :], packed[g]).then_inc(s["loaded"], 16)
                sp.dma_start(cb[:, :], cb_in).then_inc(s["cb_loaded"], 16)
                sp.wait_ge(s["cb_loaded"], 16)
                for i in range(2 * B):
                    sp.wait_ge(s["v_freed"], 16 + 2 * (i + 1) + (2 if i >= B else 0))
                    sp.dma_start(folded_dram[i], folded[:, i % 2, :]).then_inc(s[f"slot{i % 2}_stored"], 16)
                sp.wait_ge(s["slot0_stored"], 16 * B)
                sp.wait_ge(s["slot1_stored"], 16 * B)

            @block.gpsimd
            def _(pool):
                for m in rows:
                    nc.gpsimd.memset(m.xT[:, :], 0.0)
                    nc.gpsimd.memset(m.hT[:, :], 0.0)

            @block.scalar
            def _(act):
                act.wait_ge(s["loaded"], 16 * len(GROUPS))
                act.activation(a_neg[:, :, :], W("mamba", "a_log", b=NB), ACT.Exp).then_inc(s["setup_act"], 1)
                act.activation(gate[:, :], W("cross0", "gate"), ACT.Tanh).then_inc(s["setup_act"], 1)

            @block.vector
            def _(dve):
                t = Lane(dve, s, "dve_step", ps[0])
                w, v = t.w, t.v
                w(s["loaded"], 16 * len(GROUPS))
                w.step(dve.tensor_scalar(w_in[:, :], W("mamba", "w_in"), W("mamba", "norm_w"), None, ALU.mult))
                wx = w_in[:, 0:CH].rearrange("p (o c) -> p o c", o=1).to_broadcast([P, KC, CH])
                dve.tensor_tensor(w_conv[:, :, :], w_conv, wx, ALU.mult)
                w(s["setup_act"], 2)
                dve.tensor_scalar(a_neg[:, :, :], a_neg[:, :, :], -1.0, None, ALU.mult)
                dve.tensor_scalar(b_x0, b_x0, gate[0:1, :], None, ALU.mult)
                rope = W("rope5", "tables", f=4, t=NT)
                for l in range(DEPTH):
                    sc = W("cross0", "scales", l=DEPTH, f=4)
                    for f in range(4):
                        by = sc[:, l, f, :].rearrange("p (o z) -> p o z", o=1).to_broadcast([P, NT, DH5])
                        dve.tensor_tensor(tab5[:, l, f], rope[:, f], by, ALU.mult)
                pair = W("const", "pair").rearrange("p (a i b) -> p a i b", a=1, b=1).to_broadcast([P, B, 2, S])
                for p in range(8):
                    for dst in (kbd, vbd):
                        src = v.take()[:, 0:B * S].rearrange("p (b o k) -> p b o k", b=B, o=1)
                        dve.tensor_tensor(dst[:, :, p * 2 * S:(p + 1) * 2 * S].rearrange("p b (i k) -> p b i k", i=2),
                                          src.to_broadcast([P, B, 2, S]), pair, ALU.mult).then_inc(s["v_freed"], 1)
                for b in range(B):
                    if b >= 2:
                        t.w(s[f"slot{b % 2}_stored"], 16)
                    dve.tensor_copy(folded[:, b % 2, 0:512], v.take()).then_inc(s["v_freed"], 1)
                    dve.tensor_scalar(folded[:, b % 2, 512:1024], v.take(), gate[:, :],
                                      None, ALU.mult).then_inc(s["v_freed"], 1)
                head = W("const", "head").rearrange("p (a i b) -> p a i b", a=1, b=1).to_broadcast([P, B, H3, S])
                for dst in (kbd, vbd):
                    src = v.take()[:, 0:B * S].rearrange("p (b o k) -> p b o k", b=B, o=1)
                    for b in range(B):
                        ins = dve.tensor_tensor(dst[:, b].rearrange("p (i k) -> p i k", i=H3),
                                                src[:, b].to_broadcast([P, H3, S]), head[:, b], ALU.mult)
                    ins.then_inc(s["v_freed"], 1)
                for b in range(B):
                    t.w(s[f"slot{b % 2}_stored"], 16)
                    dve.tensor_copy(folded[:, b % 2, 0:512], v.take()).then_inc(s["v_freed"], 1)
                    dve.tensor_copy(folded[:, b % 2, 512:1024], v.take()).then_inc(s["v_freed"], 1)

            @block.tensor
            def _(pe):
                t = Lane(pe, s, None, ps[0])
                w, v = t.w, t.v
                w(s["loaded"], 16 * len(GROUPS))
                ctxT = W("cross0", "ctx")
                for p in range(8):
                    for n in ("w_k", "w_v"):
                        pe.matmul(v.open()[:, 0:B * S], W("cross0", n)[:, p * P:(p + 1) * P], ctxT,
                                  start=True, stop=True).then_inc(s["v_filled"], 1)
                for b in range(B):
                    bank = v.open()
                    if b == 0:
                        pe.wait_ge(s["v_freed"], 16)
                    for p in range(8):
                        ins = pe.matmul(bank[:, p * 64:(p + 1) * 64], W("cross0", "w_qT")[:, p * P:(p + 1) * P],
                                        kbd[:, b, p * 64:(p + 1) * 64], start=(p == 0), stop=(p == 7),
                                        skip_group_check=True)
                    ins.then_inc(s["v_filled"], 1)
                    bank = v.open()
                    for j in range(4):
                        for i in range(2):
                            p = 2 * j + i
                            ins = pe.matmul(bank[64 * i:64 * i + 64, j * D:(j + 1) * D],
                                            vbd[:, b, p * 64:(p + 1) * 64], W("cross0", "w_o")[:, p * P:(p + 1) * P],
                                            start=(j == 0), stop=(j == 3), skip_group_check=True)
                    ins.then_inc(s["v_filled"], 1)
                for n in ("w4_k", "w4_v"):
                    pe.matmul(v.open()[:, 0:B * S], W("cross0", n), ctxT, start=True, stop=True).then_inc(s["v_filled"], 1)
                pe.wait_ge(s["v_freed"], 16 + 2 * B + 2)
                for b in range(B):
                    pe.matmul(v.open()[:, :], W("cross0", "w4_q"), kbd[:, b], start=True, stop=True)\
                        .then_inc(s["v_filled"], 1)
                    bank = v.open()
                    for j in range(4):
                        ins = pe.matmul(bank[:, j * D:(j + 1) * D], vbd[:, b, j * P:(j + 1) * P], W("cross0", "w4_o"),
                                        start=(j == 0), stop=(j == 3), skip_group_check=True)
                    ins.then_inc(s["v_filled"], 1)
        nc.sync.sem_clear(sems)
        nc.all_engine_barrier()

        def tok(v, t):
            return v[:, t * P:(t + 1) * P]


        def norm_vector(t, dst, src, done):
            for i in range(NT):
                ins = t.eng.bn_stats(t.m.rowstat[:, i, :], src[:, i, :])
            t.w.step(ins)
            for i in range(NT):
                ins = t.eng.bn_aggr(t.m.mv[:, i, :], t.m.rowstat[:, i, :])
            ins.then_inc(t.s["stats_ready"], 1)
            t.w(t.s["rstd_ready"])
            for i in range(NT):
                ins = t.eng.tensor_scalar(dst[:, i, :], src[:, i, :], t.m.mv[:, i, 0:1], t.m.rstd[:, i:i + 1],
                                          ALU.subtract, ALU.mult)
            ins.then_inc(t.s[done], 1)
            t.w(t.s[done])

        def inverse_root(t, dst, src, op, by, done):
            t.w.step(t.eng.tensor_scalar(dst, src, by, None, op))
            t.eng.tensor_tensor(dst, dst, W("const", "neg_half").to_broadcast([P, dst.shape[1]]), ALU.pow)\
                .then_inc(t.s[done], 1)

        def norm_pool(t):
            t.w(t.s["stats_ready"])
            inverse_root(t, t.m.rstd[:, :], t.m.mv[:, :, 1], ALU.add, EPS, "rstd_ready")

        def turn_tensor(t, src):
            bank = t.a.open()
            for i in range(NT):
                ins = t.eng.transpose(tok(bank, i), src[:, i, :], ident)
            ins.then_inc(t.s["a_filled"], 1)
            return t.a.at

        def plain_scalar(t):
            t.eng.activation(t.m.xTn, t.a.take(), ACT.Copy).then_inc(t.s["a_freed"], 1)

        def residual_vector(t, dst, times=None):
            t.w(t.s["o_filled"])
            t.skip(o=1)
            bank = t.o.bank()
            if times:
                ins = t.eng.scalar_tensor_tensor(dst, t.m.x_flat, times, bank, ALU.mult, ALU.add)
            else:
                ins = t.eng.tensor_tensor(dst, bank, t.m.x_flat, ALU.add)
            ins.then_inc(t.s["o_freed"], 1)
            t.eng.wait_ge(t.s["o_freed"], t.o.at)

        def mamba_tensor(t):
            pe = t.eng
            yield 2
            t.w(t.s["rms_ready"])
            turn_tensor(t, t.m.y)
            pe.wait_ge(t.s["a_freed"], t.a.at)
            yield 8
            for c in range(NB):
                bank = t.a.open()
                for k in range(KC):
                    ins = pe.matmul(bank, w_conv[:, k, c * P:(c + 1) * P], t.m.xT[:, k:k + T],
                                    start=(k == 0), stop=(k == KC - 1))
                ins.then_inc(t.s["a_filled"], 1)
            u_at = t.a.at
            for c in range(NB):
                pe.matmul(t.a.open(), w_in[:, CH + c * P:CH + (c + 1) * P], t.m.xTn, start=True, stop=True)\
                    .then_inc(t.s["a_filled"], 1)
            yield 20
            pe.wait_ge(t.s["a_freed"], u_at)
            bank = t.a.open()
            for c in range(NB):
                ins = pe.matmul(bank[0:DTR, :], W("mamba", "x_dt", c=NB)[:, c, :], t.m.u[:, c, :],
                                start=(c == 0), stop=(c == NB - 1))
            ins.then_inc(t.s["a_filled"], 1)
            dt_at = t.a.at
            bank = t.v.open()
            for c in range(NB):
                ins = pe.matmul(bank[0:96, :], W("mamba", "x_bc", c=NB)[:, c, :], t.m.u[:, c, :],
                                start=(c == 0), stop=(c == NB - 1))
            ins.then_inc(t.s["v_filled"], 1)
            yield 26
            pe.wait_ge(t.s["a_freed"], dt_at)
            for c in range(NB):
                pe.matmul(t.a.open(), W("mamba", "w_dt")[0:DTR, c * P:(c + 1) * P], t.m.dtS[0:DTR, :],
                          start=True, stop=True).then_inc(t.s["a_filled"], 1)
            t.w(t.s["parts_ready"])
            pe.wait_ge(t.s["a_freed"], t.a.at)
            sum_banks = [t.a.banks[0], t.a.banks[1]]
            for n in range(NS + 1):
                yield STATES_AT + STATE_STEP * n
                if n < NS:
                    for which in (n, NS + n):
                        pe.matmul(t.v.open(), cbv["select"][0:96, which:which + 1].to_broadcast([96, P]), t.m.parts[0:96, :],
                                  start=True, stop=True).then_inc(t.s["v_filled"], 1)
                if n >= 1:
                    pe.wait_ge(t.s["v_freed"], t.v.at - (2 if n < NS else 0))
                    for c in range(NB):
                        ins = pe.matmul(sum_banks[c], ident, t.m.hC[:, 2 * ((n - 1) % 2) + c, :],
                                        start=(n == 1), stop=(n == NS))
                        if n == NS:
                            ins.then_inc(t.s["sum_filled"], 1)
                    if n < NS:
                        ins.then_inc(t.s["states_used"], 1)
            yield MAMBA_END - 11
            t.w(t.s["gated_ready"])
            t.v.use(1)
            bank = t.o.open()
            for i in range(NT):
                for c in range(NB):
                    ins = pe.matmul(tok(bank, i), tok(t.m.yg[:, c, :], i), W("mamba", "w_out", c=NB)[:, c, :],
                                    start=(i == 0 and c == 0), stop=(i == NT - 1 and c == NB - 1),
                                    skip_group_check=True)
            ins.then_inc(t.s["o_filled"], 1)

        def mamba_scalar(t):
            act = t.eng
            yield 0
            t.w(t.s["x_loaded"], 16)
            for i in range(NT):
                ins = act.activation(tok(t.m.rest, i), t.m.x[:, i, :], ACT.Square, scale=D ** -0.5,
                                     accum_out=t.m.small[:, 0, i:i + 1])
            ins.then_inc(t.s["squares_ready"], 1)
            yield 2
            plain_scalar(t)
            yield 8
            for c in range(NB):
                act.activation(t.m.u[:, c, :], t.a.take(), ACT.Silu, bias=W("mamba", "conv_b")[:, c:c + 1])\
                    .then_inc(t.s["a_freed"], 1)
            for c in range(NB):
                act.activation(t.m.zs[:, c, :], t.a.take(), ACT.Silu).then_inc(t.s["a_freed"], 1)
            yield 20
            act.activation(t.m.dtS[0:DTR, :], t.a.take()[0:DTR, :], ACT.Copy).then_inc(t.s["a_freed"], 1)
            yield 26
            for c in range(NB):
                bank = t.a.take()
                act.activation(t.m.sp1[:, c, :], bank, ACT.Abs, bias=W("mamba", "b_dt")[:, c:c + 1])
                act.activation(t.m.sp2[:, c, :], bank, ACT.Relu, bias=W("mamba", "b_dt")[:, c:c + 1])\
                    .then_inc(t.s["a_freed"], 1)
            act.wait_ge(t.s["a_freed"], t.a.at)
            act.activation(t.m.sp1[:, :, :], t.m.sp1[:, :, :], ACT.Exp, scale=-1.0).then_inc(t.s["soft_ready"], 1)
            act.wait_ge(t.s["soft_ready"], 1)
            act.activation(t.m.delta[:, :, :], t.m.sp1[:, :, :], ACT.Ln, bias=one).then_inc(t.s["soft_ready"], 1)
            yield STATES_AT
            t.w(t.s["delta_ready"])
            for n in range(NS):
                yield STATES_AT + STATE_STEP * n
                for c in range(NB):
                    i = NB * n + c
                    if i >= 4:
                        t.w(t.s["decay_used"])
                    act.activation(t.m.dA[:, i % 4, :], t.m.delta[:, c, :], ACT.Exp, scale=a_neg[:, c, n:n + 1])\
                        .then_inc(t.s["decay_ready"], 1)
            t.skip(v=1 + 2 * NS, o=1)
            t.v.use(1)

        def mamba_vector(t):
            dve = t.eng
            yield 0
            t.w(t.s["rstd_ready"])
            for i in range(NT):
                ins = dve.tensor_scalar(t.m.y[:, i, :], t.m.x[:, i, :], t.m.rstd[:, i:i + 1], None, ALU.mult)
            ins.then_inc(t.s["rms_ready"], 1)
            t.skip(a=8)
            yield 20
            bank = t.v.take()
            t.w.step(dve.tensor_copy(t.m.parts[0:96, :], bank[0:96, :]))
            dve.tensor_tensor(t.m.rest[0:96, :], bank[0:96, :], t.m.parts[0:96, :], ALU.subtract)\
                .then_inc(t.s["v_freed"], 1)
            dve.wait_ge(t.s["v_freed"], t.v.at)
            t.w.step(dve.tensor_copy(t.m.mid[0:96, :], t.m.rest[0:96, :]))
            dve.tensor_copy(t.m.parts[32:64, :], t.m.mid[32:64, :])
            t.w.step(dve.tensor_tensor(t.m.rest[64:96, :], t.m.rest[64:96, :], t.m.mid[64:96, :], ALU.subtract))
            dve.tensor_copy(t.m.parts[64:96, :], t.m.rest[64:96, :]).then_inc(t.s["parts_ready"], 1)
            yield 26
            t.w(t.s["soft_ready"])
            t.w.step(dve.tensor_scalar(t.m.du[:, :, :], t.m.sp1[:, :, :], 1.0, 1.0, ALU.add, ALU.subtract))
            t.w.step(dve.tensor_tensor(t.m.du[:, :, :], t.m.sp1[:, :, :], t.m.du[:, :, :], ALU.subtract))
            t.w(t.s["soft_ready"])
            t.w.step(dve.tensor_tensor(t.m.delta[:, :, :], t.m.delta[:, :, :], t.m.du[:, :, :], ALU.add))
            t.w.step(dve.tensor_tensor(t.m.delta[:, :, :], t.m.delta[:, :, :], t.m.sp2[:, :, :], ALU.add))
            dve.tensor_tensor(t.m.du[:, :, :], t.m.delta[:, :, :], t.m.u[:, :, :], ALU.mult).then_inc(t.s["delta_ready"], 1)
            t.w(t.s["delta_ready"])
            for n in range(NS):
                yield STATES_AT + STATE_STEP * n
                bank = t.v.take().rearrange("p (o z) -> p o z", o=1).to_broadcast([P, NB, T])
                dve.tensor_tensor(t.m.dBu[:, :, :], t.m.du[:, :, :], bank, ALU.mult).then_inc(t.s["v_freed"], 1)
                dve.wait_ge(t.s["v_freed"], t.v.at)
                for c in range(NB):
                    i = NB * n + c
                    t.w(t.s["decay_ready"])
                    dve.tensor_tensor_scan(t.m.hs[:, c, :], t.m.dA[:, i % 4, :], t.m.dBu[:, c, :], 0.0, ALU.mult, ALU.add)\
                        .then_inc(t.s["decay_used"], 1)
                bank = t.v.take().rearrange("p (o z) -> p o z", o=1).to_broadcast([P, NB, T])
                if n >= 2:
                    t.w(t.s["states_used"])
                dve.wait_ge(t.s["decay_used"], NB * (n + 1))
                dve.tensor_tensor(t.m.hC[:, 2 * (n % 2):2 * (n % 2) + 2, :], t.m.hs[:, :, :], bank, ALU.mult)\
                    .then_inc(t.s["v_freed"], 1)
            yield STATES_AT + STATE_STEP * NS
            t.w(t.s["sum_filled"], 2)
            for c in range(NB):
                bank = t.a.banks[c]
                dve.scalar_tensor_tensor(t.m.yg[:, c, :], t.m.u[:, c, :], W("mamba", "d_skip")[:, c:c + 1], bank,
                                         ALU.mult, ALU.add).then_inc(t.s["sums_read"], 1)
            t.w(t.s["sums_read"], 2)
            dve.tensor_tensor(t.m.yg[:, :, :], t.m.yg[:, :, :], t.m.zs[:, :, :], ALU.mult).then_inc(t.s["gated_ready"], 1)
            t.v.use(1)
            yield MAMBA_END - 8
            residual_vector(t, t.m.y_flat, 2.0)
            norm_vector(t, t.m.x, t.m.y, "norm_ready")

        def mamba_pool(t):
            yield 0
            t.w(t.s["squares_ready"])
            inverse_root(t, t.m.rstd[:, :], t.m.small[:, 0, 0:NT], ALU.add, EPS, "rstd_ready")
            yield MAMBA_END - 8
            norm_pool(t)
            t.skip(a=8, v=1 + 2 * NS, o=1)
            t.v.use(1)

        def cross_tensor(t, inner, bias):
            pe = t.eng
            yield 1
            t.w(t.s["norm_ready"], 2 if inner else 1)
            turn_tensor(t, t.m.y if inner else t.m.x)
            pe.wait_ge(t.s["a_freed"], t.a.at)
            t.w(t.s["score_loaded"], 16)
            out_bank = t.o.open()
            pe.matmul(out_bank, ones[0:1, :], bias, start=True, stop=False, skip_group_check=True)
            for i in range(NT + 2):
                yield 12 + CROSS_STEP * i
                if i < NT:
                    pe.matmul(t.v.open(), tok(t.m.xTn, i), t.m.score[:, :], start=True, stop=True)\
                        .then_inc(t.s["v_filled"], 1)
                if 1 <= i <= NT:
                    t.w(t.s["prob_ready"])
                    bank = t.a.open()
                    for j in range(4):
                        ins = pe.transpose(tok(bank, j), tok(t.m.e1[:, (i - 1) % 2, :], j), ident)
                    ins.then_inc(t.s["a_filled"], 1)
                if i >= 2:
                    pe.wait_ge(t.s["a_freed"], t.a.at - (1 if i <= NT else 0))
                    for j in range(4):
                        ins = pe.matmul(tok(out_bank, i - 2), t.m.pT1[:, i % 2, j, :], t.m.value[:, j, :],
                                        start=False, stop=(i == NT + 1 and j == 3), skip_group_check=True)
                    ins.then_inc(t.s["o_filled"] if i == NT + 1 else t.s["pT_used"], 1)

        def cross_scalar(t, scale, inner):
            act = t.eng
            yield 1
            if inner:
                act.activation(t.m.xTn, t.a.take(), ACT.Identity, scale=W("experts", "gamma"),
                               bias=W("experts", "beta")).then_inc(t.s["a_freed"], 1)
            else:
                plain_scalar(t)
            for i in range(NT + 1):
                yield 12 + CROSS_STEP * i
                if i < NT:
                    t.skip(v=1)
                    act.wait_ge(t.s["v_freed"], t.v.at)
                    act.activation(t.m.e1[:, i % 2, :], t.m.e1[:, i % 2, :], ACT.Exp, scale=scale)\
                        .then_inc(t.s["e_ready"], 1)
                if i >= 1:
                    if i >= 3:
                        t.w(t.s["pT_used"])
                    act.activation(t.m.pT1[:, (i - 1) % 2].rearrange("p j z -> p (j z)"), t.a.take(), ACT.Copy)\
                        .then_inc(t.s["a_freed"], 1)
            t.w(t.s["pT_used"], 1)
            t.skip(o=1)

        def cross_vector(t, inner):
            dve = t.eng
            yield 1
            if inner:
                norm_vector(t, t.m.y, t.m.x, "norm_ready")
            t.skip(a=1)
            heads = lambda v: v.rearrange("p (h k) -> p h k", h=H1)
            wide = lambda v: v.rearrange("p (h o) -> p h o", o=1).to_broadcast([P, H1, S])
            for i in range(NT + 1):
                yield 12 + CROSS_STEP * i
                if i < NT:
                    if i >= 2:
                        dve.wait_ge(t.s["a_freed"], t.a.at - 0)
                    bank = t.v.take()
                    t.w.step(dve.tensor_reduce(t.m.mx[:, i % 2, 0:H1], heads(bank), X, ALU.max, negate=True))
                    dve.tensor_tensor(heads(t.m.e1[:, i % 2, :]), heads(bank), wide(t.m.mx[:, i % 2, 0:H1]), ALU.add)\
                        .then_inc(t.s["v_freed"], 1)
                if i >= 1:
                    j = (i - 1) % 2
                    t.w(t.s["e_ready"])
                    t.w.step(dve.tensor_reduce(t.m.sums[:, j, 0:H1], heads(t.m.e1[:, j, :]), X, ALU.add))
                    dve.reciprocal(t.m.rinv[:, j, 0:H1], t.m.sums[:, j, 0:H1]).then_inc(t.s["rinv_ready"], 1)
                    t.skip(a=1)
            yield CROSS_END - 8
            residual_vector(t, t.m.y_flat)
            norm_vector(t, t.m.x, t.m.y, "norm_ready")

        def cross_pool(t, inner):
            if inner:
                yield 1
                norm_pool(t)
            for i in range(NT):
                yield 12 + CROSS_STEP * (i + 1)
                t.w(t.s["rinv_ready"])
                by = t.m.rinv[:, i % 2, 0:H1].rearrange("p (h o) -> p h o", o=1).to_broadcast([P, H1, S])
                v = t.m.e1[:, i % 2, :].rearrange("p (h k) -> p h k", h=H1)
                t.eng.tensor_tensor(v, v, by, ALU.mult).then_inc(t.s["prob_ready"], 1)
            yield CROSS_END - 8
            norm_pool(t)
            t.skip(a=1 + NT, v=NT, o=1)

        def experts_tensor(t):
            pe = t.eng
            yield 0
            t.w(t.s["norm_ready"])
            turn_tensor(t, t.m.x)
            pe.wait_ge(t.s["a_freed"], t.a.at)
            bank = t.v.open()
            pe.matmul(bank[:, 0:NT * E], ones[0:1, :],
                      W("rows", "router").rearrange("p (o z) -> p o z", o=1).to_broadcast([1, NT, E]),
                      start=True, stop=False, skip_group_check=True)
            for i in range(NT):
                ins = pe.matmul(bank[:, i * E:(i + 1) * E], tok(t.m.xTn, i), W("experts", "router"), start=False,
                                stop=(i == NT - 1), skip_group_check=True)
            ins.then_inc(t.s["v_filled"], 1)
            hid_at = {}
            for k in range(E + 2):
                yield 10 + EXPERT_STEP * k
                if 1 <= k <= E:
                    pe.matmul(t.a.open(), ident[0:E, k - 1:k].to_broadcast([E, P]), t.m.combT[0:E, :],
                              start=True, stop=True).then_inc(t.s["a_filled"], 1)
                if k <= E:
                    t.w(t.s[f"expert{k % NE}_loaded"], 16)
                    for f in range(NF):
                        pe.matmul(t.a.open(), we[:, k % NE, f * P:(f + 1) * P], t.m.xTn, start=True, stop=True)\
                            .then_inc(t.s["a_filled"], 1)
                    hid_at[k] = t.a.at
                if k == 0:
                    t.w(t.s["comb_ready"])
                    bank = t.a.open()
                    for i in range(NT):
                        ins = pe.transpose(tok(bank, i)[0:E, :], t.m.comb[:, i, :], ident)
                    ins.then_inc(t.s["a_filled"], 1)
                    pe.wait_ge(t.s["a_freed"], t.a.at)
                if k >= 1:
                    pe.wait_ge(t.s["a_freed"], hid_at[k - 1])
                    bank = t.v.open()
                    if k == 1:
                        pe.matmul(bank, W("experts", "b2e")[0:E, :], t.m.combT[0:E, :], start=True, stop=False)
                    for f in range(NF):
                        ins = pe.matmul(bank, we[:, (k - 1) % NE, FF + f * P:FF + (f + 1) * P], t.m.hid[:, (k - 1) % 2, f, :],
                                        start=(k > 1 and f == 0), stop=(f == NF - 1))
                    ins.then_inc(t.s["v_filled"], 1)
            yield EXPERTS_END - 22
            t.w(t.s["acc_ready"], E)
            bank = t.v.open()
            for i in range(NT):
                ins = pe.transpose(tok(bank, i), tok(t.m.acc, i), ident)
            ins.then_inc(t.s["v_filled"], 1)

        def experts_scalar(t):
            act = t.eng
            yield 0
            plain_scalar(t)
            t.skip(v=1)
            yield 10
            t.w(t.s["gap_ready"])
            act.activation(t.m.small[:, 1, 0:NT], t.m.small[:, 0, 0:NT], ACT.Exp).then_inc(t.s["ratio_ready"], 1)
            for k in range(E + 1):
                yield 10 + EXPERT_STEP * k
                if k >= 1:
                    act.activation(t.m.pickS[:, k - 1, :], t.a.take(), ACT.Copy).then_inc(t.s["a_freed"], 1)
                for f in range(NF):
                    if k >= 2 and f == 0:
                        act.wait_ge(t.s["v_filled"], t.v.at)
                    c = k * NF + f
                    act.activation(t.m.hid[:, k % 2, f, :], t.a.take(), ACT.Gelu_apprx_tanh,
                                   bias=W("experts", "b1")[:, c:c + 1]).then_inc(t.s["a_freed"], 1)
                if k == 0:
                    act.activation(t.m.combT[0:E, :], t.a.take()[0:E, :], ACT.Copy).then_inc(t.s["a_freed"], 1)
                if k >= 1:
                    t.skip(v=1)
            t.skip(v=2)

        def experts_vector(t):
            dve = t.eng
            yield 0
            bank = t.v.take()
            dve.tensor_copy(t.m.lg[:, :, :].rearrange("p t e -> p (t e)"), bank[:, 0:NT * E]).then_inc(t.s["v_freed"], 1)
            dve.wait_ge(t.s["v_freed"], t.v.at)
            for i in range(NT):
                ins = dve.max(t.m.m8[:, i, :], t.m.lg[:, i, :])
            t.w.step(ins)
            dve.tensor_tensor(t.m.small[:, 0, 0:NT], t.m.m8[:, :, 1], t.m.m8[:, :, 0], ALU.subtract).then_inc(t.s["gap_ready"], 1)
            for i in range(NT):
                ins = dve.max_index(t.m.i8[:, i, :], t.m.m8[:, i, :], t.m.lg[:, i, :])
            t.w.step(ins)
            top = t.m.small[:, 2, 0:2 * NT].rearrange("p (t e) -> p t e", e=2)
            dve.tensor_copy(top, t.m.i8[:, :, 0:2])
            yield 10
            t.w(t.s["ratio_ready"])
            t.w.step(dve.tensor_scalar(t.m.small[:, 3, 0:NT], t.m.small[:, 1, 0:NT], 1.0, None, ALU.add))
            t.w.step(dve.reciprocal(t.m.small[:, 4, 0:NT], t.m.small[:, 3, 0:NT]))
            t.w.step(dve.tensor_tensor(t.m.small[:, 5, 0:NT], t.m.small[:, 4, 0:NT], t.m.small[:, 1, 0:NT], ALU.mult))
            wide = lambda v: v.rearrange("p (t o) -> p t o", o=1).to_broadcast([P, NT, E])
            iota = W("const", "iota").rearrange("p (o e) -> p o e", o=1).to_broadcast([P, NT, E])
            for n, dst in ((0, t.m.comb), (1, t.m.eqt)):
                t.w.step(dve.tensor_tensor(dst[:, :, :], iota, top[:, :, n:n + 1].to_broadcast([P, NT, E]), ALU.is_equal))
                t.w.step(dve.tensor_tensor(dst[:, :, :], dst[:, :, :], wide(t.m.small[:, 4 + n, 0:NT]), ALU.mult))
            dve.tensor_tensor(t.m.comb[:, :, :], t.m.comb[:, :, :], t.m.eqt[:, :, :], ALU.add).then_inc(t.s["comb_ready"], 1)
            for k in range(E + 1):
                yield 10 + EXPERT_STEP * (k + 1)
                bank = t.v.take()
                if k == 0:
                    dve.tensor_scalar(t.m.acc, bank, W("experts", "b2s"), None, ALU.add).then_inc(t.s["v_freed"], 1)
                else:
                    if k >= 3:
                        t.w(t.s["acc_ready"])
                    dve.tensor_tensor(t.m.tmp[:, k % 2, :], bank, t.m.pickS[:, k - 1, :], ALU.mult).then_inc(t.s["v_freed"], 1)
            yield EXPERTS_END - 22
            t.w(t.s["acc_ready"], 2)
            dve.tensor_tensor(t.m.y_flat, t.v.take(), t.m.x_flat, ALU.add).then_inc(t.s["v_freed"], 1)
            dve.wait_ge(t.s["v_freed"], t.v.at)
            t.skip(a=2 + E + (E + 1) * NF)
            yield EXPERTS_END - 18
            norm_vector(t, t.m.x, t.m.y, "norm_ready")

        def experts_pool(t):
            yield 10
            t.eng.memset(t.m.vpad, 0.0)
            t.skip(v=2, a=2 + E + (E + 1) * NF)
            for k in range(1, E + 1):
                yield 10 + EXPERT_STEP * (k + 1)
                t.skip(v=1)
                t.eng.wait_ge(t.s["v_freed"], t.v.at)
                t.eng.tensor_tensor(t.m.acc, t.m.acc, t.m.tmp[:, k % 2, :], ALU.add).then_inc(t.s["acc_ready"], 1)
                t.w(t.s["acc_ready"])
            t.skip(v=1)
            yield EXPERTS_END - 18
            norm_pool(t)
            t.eng.memset(t.m.qpad, 0.0)
            t.eng.memset(t.m.kpad, 0.0).then_inc(t.s["pads_ready"], 1)

        class Band:

            def __init__(self, heads, mask, wide_values, step):
                self.heads, self.mask, self.wide, self.step = heads, mask, wide_values, step
                self.rows = 32 if wide_values == 32 else 64
                self.per = P // self.rows
                self.units = []
                for j in range(NT):
                    nk = 1 if j == 0 else 2
                    for i in range(self.per):
                        for g in range(0, heads // self.per, 4 // nk):
                            hh = [self.per * (g + a) + i for a in range(4 // nk)]
                            self.units.append((j, nk, hh))
                self.per_tile = [sum(1 for u in self.units if u[0] == j) for j in range(NT)]

            def last_of_tile(self, n):
                return n + 1 == len(self.units) or self.units[n + 1][0] != self.units[n][0]

            def cols(self, n):
                return sum(len(hh) for _, _, hh in self.units[:n]), len(self.units[n][2])

        def band_tensor(t, band, t0):
            pe, at = t.eng, {}
            pairs = lambda v, n, z: v.rearrange("p (o z) -> p o z", o=1).to_broadcast([P, n, z])
            U = len(band.units)
            for n in range(U + 3):
                yield t0 + band.step * n
                if n < U:
                    j, nk, hh = band.units[n]
                    bank = t.s_.open()
                    mask = cbv[band.mask][:, (2 - nk) * P:2 * P]
                    pe.matmul(bank, cbv["ident"], pairs(mask, len(hh), nk * P), start=True, stop=False,
                              skip_group_check=True)
                    for a, h in enumerate(hh):
                        g, r = h // band.per, band.rows * (h % band.per)
                        ins = pe.matmul(bank[:, a * nk * P:(a + 1) * nk * P],
                                        t.m.qT[r:r + band.rows, g, j * P:(j + 1) * P],
                                        t.m.kT[r:r + band.rows, g, (j + 1 - nk) * P:(j + 1) * P],
                                        start=False, stop=(a == len(hh) - 1), skip_group_check=True)
                    ins.then_inc(t.s["s_filled"], 1)
                if 2 <= n < U + 2:
                    t.w(t.s["prob_ready"])
                    bank = t.v.open()
                    for c in range(4):
                        ins = pe.transpose(tok(bank, c), tok(t.m.pr[:, (n - 2) % 3, :], c), ident)
                    ins.then_inc(t.s["v_filled"], 1)
                    at[n - 2] = t.v.at
                if n >= 3:
                    m = n - 3
                    j, nk, hh = band.units[m]
                    pe.wait_ge(t.s["v_freed"], at[m])
                    if hh[0] == 0:
                        heads_bank = t.o.open()
                    for a, h in enumerate(hh):
                        g, r = h // band.per, band.rows * (h % band.per)
                        for c in range(nk):
                            tile = j + 1 - nk + c
                            if band.wide == 32:
                                v, o = t.m.vpad[:, tile, h, :], heads_bank[r:r + 32, 0:P]
                            else:
                                v, o = t.m.vv[:, tile, h * 64:(h + 1) * 64], tok(heads_bank, g)[r:r + 64, :]
                            ins = pe.matmul(o, v, t.m.pT[:, m % 2, (a * nk + c) * P:(a * nk + c + 1) * P],
                                            start=(g == 0 and c == 0),
                                            stop=(h >= band.heads - band.per and c == nk - 1),
                                            skip_group_check=True)
                    ins.then_inc(t.s["pT_used"], 1)

        def band_scalar(t, band, t0):
            act = t.eng
            U = len(band.units)
            v0, p0 = t.v.at, t.w.asked.get("pT_used", 0)
            for n in range(U + 3):
                yield t0 + band.step * n
                if n < U:
                    j, nk, hh = band.units[n]
                    c0, k = band.cols(n)
                    t.skip(s=1)
                    bank = t.s_.bank()
                    t.w(t.s["max_ready"])
                    if n >= 3:
                        act.wait_ge(t.s["v_filled"], v0 + n - 2)
                    for a in range(k):
                        z = slice(a * nk * P, (a + 1) * nk * P)
                        ins = act.activation(t.m.pr[:, n % 3, z], bank[:, z], ACT.Exp, bias=t.m.mx2[:, c0 + a:c0 + a + 1],
                                             accum_out=t.m.sums2[:, c0 + a:c0 + a + 1])
                    ins.then_inc(t.s["s_freed"], 1)
                if 2 <= n < U + 2:
                    t.skip(v=1)
                    if n % 2:
                        if n >= 4:
                            act.wait_ge(t.s["pT_used"], p0 + n - 3)
                        act.wait_ge(t.s["v_filled"], t.v.at)
                        act.activation(t.m.pT[:, n % 2, :], t.v.bank(), ACT.Copy).then_inc(t.s["v_freed"], 1)
                if n >= 3 and band.last_of_tile(n - 3):
                    j = band.units[n - 3][0]
                    t.w(t.s["pT_used"], band.per_tile[j])
                    t.skip(o=1)
                    if band.wide == 32:
                        act.activation(tok(t.m.oT[:, 0, :], j), t.o.bank()[:, 0:P], ACT.Copy).then_inc(t.s["o_freed"], 1)
                    else:
                        act.activation(t.m.oT[:, :, j * P:(j + 1) * P], t.o.bank().rearrange("p (g z) -> p g z", g=4),
                                       ACT.Copy).then_inc(t.s["o_freed"], 1)

        def band_vector(t, band, t0):
            dve = t.eng
            U = len(band.units)
            s0 = t.s_.at
            for n in range(U + 3):
                yield t0 + band.step * n
                if n < U:
                    j, nk, hh = band.units[n]
                    c0, k = band.cols(n)
                    bank = t.s_.take()
                    dve.tensor_reduce(t.m.mx2[:, c0:c0 + k], bank.rearrange("p (a z) -> p a z", a=k), X, ALU.max,
                                      negate=True).then_inc(t.s["max_ready"], 1)
                if 1 <= n <= U:
                    c0, k = band.cols(n - 1)
                    dve.wait_ge(t.s["s_freed"], s0 + n)
                    t.w.step(dve.reciprocal(t.m.rinv2[:, c0:c0 + k], t.m.sums2[:, c0:c0 + k]))
                    nk = band.units[n - 1][1]
                    for a in range(k):
                        z = t.m.pr[:, (n - 1) % 3, a * nk * P:(a + 1) * nk * P]
                        ins = dve.tensor_scalar(z, z, t.m.rinv2[:, c0 + a:c0 + a + 1], None, ALU.mult)
                    ins.then_inc(t.s["prob_ready"], 1)
                if 2 <= n < U + 2:
                    if n >= 4:
                        t.w(t.s["pT_used"])
                    if n % 2 == 0:
                        dve.tensor_copy(t.m.pT[:, n % 2, :], t.v.take()).then_inc(t.s["v_freed"], 1)
                    else:
                        t.skip(v=1)
            t.w(t.s["pT_used"], 2)
            t.skip(o=NT)

        window, local = Band(H3, "band3", 32, WINDOW_STEP), Band(H5, "band5", 64, LOCAL_STEP)
        WINDOW_BAND, LOCAL_BAND = 10 + ROPE_STEP * NT, 10 + QKV_STEP * (NT + 0.5)
        WINDOW_END = WINDOW_BAND + window.step * (len(window.units) + 3)
        LOCAL_END = LOCAL_BAND + local.step * (len(local.units) + 3)

        def turn_qk(t, q, k):
            for src in (q, k):
                bank = t.a.open()
                for g in range(4):
                    ins = t.eng.transpose(tok(bank, g), tok(src, g), ident)
                ins.then_inc(t.s["a_filled"], 1)

        def take_qk(t, i):
            for dst in (t.m.qT, t.m.kT):
                t.eng.activation(dst[:, :, i * P:(i + 1) * P], t.a.take().rearrange("p (g z) -> p g z", g=4),
                                 ACT.Copy).then_inc(t.s["a_freed"], 1)

        def window_tensor(t):
            pe = t.eng
            yield 0
            t.w(t.s["norm_ready"])
            turn_tensor(t, t.m.x)
            pe.wait_ge(t.s["a_freed"], t.a.at)
            bank = t.v.open()
            for i in range(NT):
                ins = pe.matmul(tok(bank, i), tok(t.m.xTn, i), W("window", "w_v"), start=(i == 0), stop=(i == NT - 1),
                                skip_group_check=True)
            ins.then_inc(t.s["v_filled"], 1)
            for i in range(NT + 1):
                yield 4 + ROPE_STEP * i
                if i < NT:
                    pe.matmul(t.v.open(), tok(t.m.xTn, i), W("window", "w_qk"), start=True, stop=True)\
                        .then_inc(t.s["v_filled"], 1)
                if i >= 1:
                    t.w(t.s["rope_ready"])
                    turn_qk(t, t.m.qpad[:, (i - 1) % 2, :], t.m.kpad[:, (i - 1) % 2, :])
            pe.wait_ge(t.s["a_freed"], t.a.at)
            yield from band_tensor(t, window, WINDOW_BAND)
            yield WINDOW_END
            pe.wait_ge(t.s["o_freed"], t.o.at)
            bank = t.o.open()
            pe.matmul(bank, ones[0:1, :], row("b_win"), start=True, stop=False, skip_group_check=True)
            for i in range(NT):
                ins = pe.matmul(tok(bank, i), tok(t.m.oT[:, 0, :], i), W("window", "w_o"), start=False,
                                stop=(i == NT - 1), skip_group_check=True)
            ins.then_inc(t.s["o_filled"], 1)

        def window_scalar(t):
            yield 0
            plain_scalar(t)
            for i in range(NT):
                yield 4 + ROPE_STEP * (i + 1)
                take_qk(t, i)
            t.skip(v=1 + NT)
            yield from band_scalar(t, window, WINDOW_BAND)
            t.skip(o=1)

        def window_vector(t):
            dve = t.eng
            yield 0
            t.w(t.s["pads_ready"])
            t.skip(a=1)
            bank = t.v.take().rearrange("p (t h d) -> p t h d", t=NT, h=H3)
            for g in range(4):
                for i in range(NT):
                    ins = dve.tensor_copy(t.m.vpad[:, i, 4 * g:4 * g + 4, 8 * g:8 * g + 8],
                                          bank[:, i, 4 * g:4 * g + 4, :])
            ins.then_inc(t.s["v_freed"], 1)
            rope = W("const", "rope3", t=NT, f=2, q=2)
            for i in range(NT):
                yield 4 + ROPE_STEP * i
                bank = t.v.take().rearrange("p (f q h d) -> p f q h d", f=2, q=2, h=H3)
                for f, dst in ((0, t.m.ra3), (1, t.m.rb3)):
                    for q in range(2):
                        by = rope[:, i, f, q:q + 1, :].to_broadcast([P, H3, DH3])
                        ins = dve.tensor_tensor(dst[:, i % 2, q * P:(q + 1) * P].rearrange("p (h d) -> p h d", h=H3),
                                                bank[:, f, q], by, ALU.mult)
                ins.then_inc(t.s["v_freed"], 1)
                dve.wait_ge(t.s["v_freed"], t.v.at)
                if i >= 2:
                    dve.wait_ge(t.s["a_freed"], t.a.at - 2)
                for q, dst in ((0, t.m.qpad), (1, t.m.kpad)):
                    h = lambda v: v[:, i % 2, q * P:(q + 1) * P].rearrange("p (h d) -> p h d", h=H3)
                    ins = dve.tensor_tensor(dst[:, i % 2, :].rearrange("p (h z) -> p h z", h=H3)[:, :, 0:DH3],
                                            h(t.m.ra3), h(t.m.rb3), ALU.add)
                ins.then_inc(t.s["rope_ready"], 1)
                t.skip(a=2)
            yield from band_vector(t, window, WINDOW_BAND)
            yield WINDOW_END + 4
            residual_vector(t, t.m.y_flat)
            norm_vector(t, t.m.x, t.m.y, "norm_ready")

        def window_pool(t):
            yield WINDOW_END + 4
            norm_pool(t)
            t.skip(a=1 + 2 * NT, v=1 + NT + len(window.units), s=len(window.units), o=NT + 1)

        def shift_scalar(t):
            bank = t.a.take()
            t.eng.activation(t.m.hT[0:64, :], bank[0:64, :], ACT.Copy)
            t.eng.activation(t.m.hT[64:P, 1:T], bank[64:P, 0:T - 1], ACT.Copy).then_inc(t.s["a_freed"], 1)

        def local_tensor(t, l):
            pe = t.eng
            w_qkv = W("local", "w_qkv", l=DEPTH)[:, l]
            yield 0
            if l == 0:
                t.w(t.s["norm_ready"])
            else:
                pe.wait_ge(t.s["o_freed"], t.o.at)
            turn_tensor(t, t.m.x)
            pe.wait_ge(t.s["a_freed"], t.a.at)
            for i in range(NT + 1):
                yield 4 + QKV_STEP * i
                if i < NT:
                    for c, ring, sig in ((0, t.a, "a_filled"), (1, t.a, "a_filled"), (2, t.v, "v_filled")):
                        pe.matmul(ring.open(), tok(t.m.hT, i), w_qkv[:, c * 512:(c + 1) * 512],
                                  start=True, stop=True).then_inc(t.s[sig], 1)
                if i >= 1:
                    t.w(t.s["rope_ready"])
                    turn_qk(t, t.m.ra[:, (i - 1) % 2, 0:512], t.m.ra[:, (i - 1) % 2, 512:1024])
            pe.wait_ge(t.s["a_freed"], t.a.at)
            yield from band_tensor(t, local, LOCAL_BAND)
            yield LOCAL_END
            pe.wait_ge(t.s["o_freed"], t.o.at)
            bank = t.o.open()
            w_o = W("local", "w_o", l=DEPTH, g=4)
            for i in range(NT):
                for g in range(4):
                    ins = pe.matmul(tok(bank, i), tok(t.m.oT[:, g, :], i), w_o[:, l, g, :],
                                    start=(i == 0 and g == 0), stop=(i == NT - 1 and g == 3), skip_group_check=True)
            ins.then_inc(t.s["o_filled"], 1)
            yield LOCAL_END + 4
            pe.wait_ge(t.s["o_freed"], t.o.at)
            turn_tensor(t, t.m.x)
            pe.wait_ge(t.s["a_freed"], t.a.at)
            pe.matmul(t.v.open(), mean_w, t.m.hT[:, :], start=True, stop=True).then_inc(t.s["v_filled"], 1)
            yield LOCAL_END + 10
            t.w(t.s["sq_ready"])
            pe.matmul(t.a.open(), mean_w, t.m.sq, start=True, stop=True).then_inc(t.s["a_filled"], 1)
            yield LOCAL_END + 18
            t.w(t.s["hn_ready"])
            w1 = W("local", "w1", l=DEPTH)[:, l]
            for c in range(NH):
                m = HC[c]
                pe.matmul(t.a.open()[0:m, :], w1[:, HID + c * P:HID + c * P + m], t.m.hc, start=True, stop=True)\
                    .then_inc(t.s["a_filled"], 1)
                pe.matmul(t.v.open()[0:m, :], w1[:, c * P:c * P + m], t.m.hc, start=True, stop=True)\
                    .then_inc(t.s["v_filled"], 1)
            bank = t.o.open()
            pe.matmul(bank, ones[0:1, :], row(f"b2_{l}"), start=True, stop=False, skip_group_check=True)
            w2 = W("local", "w2", l=DEPTH, c=NH)
            yield LOCAL_END + 28
            pe.wait_ge(t.s["v_freed"], t.v.at)
            for c in range(NH):
                for i in range(NT):
                    ins = pe.matmul(tok(bank, i), tok(t.m.uu[0:HC[c], c, :], i), w2[0:HC[c], l, c, :], start=False,
                                    stop=(i == NT - 1 and c == NH - 1), skip_group_check=True)
            ins.then_inc(t.s["o_filled"], 1)

        def local_scalar(t, l):
            act = t.eng
            yield 0
            shift_scalar(t)
            for i in range(NT + 1):
                yield 4 + QKV_STEP * i
                if i < NT:
                    if i >= 2:
                        t.w(t.s["rope_ready"])
                    for c in range(2):
                        bank, z = t.a.take(), slice(512 * c, 512 * c + 512)
                        act.activation(t.m.rb[:, i % 2, z], bank, ACT.Square)
                        act.activation(t.m.qk[:, i % 2, z], bank, ACT.Copy).then_inc(t.s["a_freed"], 1)
                    t.skip(v=1)
                if i >= 1:
                    take_qk(t, i - 1)
            t.w(t.s["rope_ready"], 2)
            yield from band_scalar(t, local, LOCAL_BAND)
            t.skip(o=1)
            yield LOCAL_END + 4
            shift_scalar(t)
            t.skip(v=1)
            yield LOCAL_END + 10
            act.wait_ge(t.s["v_freed"], t.v.at)
            act.activation(t.m.sq, t.m.hc, ACT.Square).then_inc(t.s["sq_ready"], 1)
            act.activation(t.m.rst, t.a.take(), ACT.Ln, bias=eps).then_inc(t.s["a_freed"], 1)
            act.wait_ge(t.s["a_freed"], t.a.at)
            act.activation(t.m.rst, t.m.rst, ACT.Exp, scale=-0.5).then_inc(t.s["rst_ready"], 1)
            b1 = W("local", "b1", l=DEPTH, f=2)
            yield LOCAL_END + 18
            for c in range(NH):
                m = HC[c]
                act.activation(t.m.gg[0:m, c, :], t.a.take()[0:m, :], ACT.Gelu, bias=b1[0:m, l, 1, c:c + 1])\
                    .then_inc(t.s["a_freed"], 1)
            t.skip(v=NH, o=1)

        def local_vector(t, l):
            dve = t.eng
            yield 0
            t.skip(a=1)
            if l == 0:
                t.w.step(dve.tensor_copy(t.m.y_flat, t.m.x_flat))
            for i in range(NT):
                yield 4 + QKV_STEP * i
                j = i % 2
                t.skip(a=2)
                dve.tensor_copy(t.m.vv[:, i, :], t.v.take()).then_inc(t.s["v_freed"], 1)
                dve.wait_ge(t.s["a_freed"], t.a.at)
                ss = t.m.small[:, 2 * j, 0:16]
                h = lambda v: v[:, j, :].rearrange("p (h d) -> p h d", h=2 * H5)
                dve.tensor_reduce(ss, h(t.m.rb), X, ALU.add).then_inc(t.s["ss_ready"], 1)
                t.w(t.s["rn_ready"])
                rn = t.m.small[:, 2 * j + 1, 0:16].rearrange("p (h o) -> p h o", o=1).to_broadcast([P, 2 * H5, DH5])
                dve.tensor_tensor(h(t.m.qk), h(t.m.qk), rn, ALU.mult).then_inc(t.s["qn_ready"], 1)
                dve.wait_ge(t.s["qn_ready"], l * NT + i + 1)
                if i >= 2:
                    dve.wait_ge(t.s["a_freed"], ra_at)
                for q in range(2):
                    z = lambda v: v[:, j, q * 512:(q + 1) * 512].rearrange("p (h d) -> p h d", h=H5)
                    ins = dve.tensor_tensor(z(t.m.ra), z(t.m.qk), tab5[:, l, 2 * q, i:i + 1, :].to_broadcast([P, H5, DH5]), ALU.mult)
                t.w.step(ins)
                t.w(t.s["rot_ready"])
                dve.tensor_tensor(t.m.ra[:, j, :], t.m.ra[:, j, :], t.m.rb[:, j, :], ALU.add).then_inc(t.s["rope_ready"], 1)
                if i >= 1:
                    t.skip(a=2)
                ra_at = t.a.at
            t.skip(a=2)
            yield from band_vector(t, local, LOCAL_BAND)
            yield LOCAL_END + 4
            residual_vector(t, t.m.x_flat)
            t.skip(a=1)
            dve.tensor_tensor(t.m.hc, t.m.hT[:, :], t.v.take(), ALU.subtract).then_inc(t.s["v_freed"], 1)
            t.skip(a=1)
            yield LOCAL_END + 14
            t.w(t.s["rst_ready"])
            t.w.step(dve.tensor_tensor(t.m.hc, t.m.hc, t.m.rst, ALU.mult))
            dve.tensor_scalar(t.m.hc, t.m.hc, W("local", "ln_g")[:, l:l + 1], W("local", "ln_b")[:, l:l + 1],
                              ALU.mult, ALU.add).then_inc(t.s["hn_ready"], 1)
            yield LOCAL_END + 18
            b1 = W("local", "b1", l=DEPTH, f=2)
            for c in range(NH):
                m = HC[c]
                t.skip(a=1)
                bank = t.v.take()
                dve.wait_ge(t.s["a_freed"], t.a.at)
                dve.scalar_tensor_tensor(t.m.uu[0:m, c, :], bank[0:m, :], b1[0:m, l, 0, c:c + 1], t.m.gg[0:m, c, :],
                                         ALU.add, ALU.mult).then_inc(t.s["v_freed"], 1)
            yield LOCAL_END + 32
            residual_vector(t, t.m.x_flat)
            if l == DEPTH - 1:
                t.w.step(dve.tensor_tensor(t.m.y_flat, t.m.y_flat, t.m.x_flat, ALU.add))
                norm_vector(t, t.m.x, t.m.y, "y_ready")

        def local_pool(t, l):
            for i in range(NT):
                yield 4 + QKV_STEP * i
                t.w(t.s["ss_ready"])
                inverse_root(t, t.m.small[:, 2 * (i % 2) + 1, 0:16], t.m.small[:, 2 * (i % 2), 0:16], ALU.max, 1e-24,
                             "rn_ready")
                t.w(t.s["qn_ready"])
                for q in range(2):
                    z = lambda v: v[:, i % 2, q * 512:(q + 1) * 512].rearrange("p (h a d) -> p h a d", h=H5, a=2)
                    for a in range(2):
                        by = tab5[:, l, 2 * q + 1, i:i + 1, 32 * a:32 * a + 32].to_broadcast([P, H5, 32])
                        ins = t.eng.tensor_tensor(z(t.m.rb)[:, :, a, :], z(t.m.qk)[:, :, 1 - a, :], by, ALU.mult)
                ins.then_inc(t.s["rot_ready"], 1)
            if l == DEPTH - 1:
                yield LOCAL_END + 32
                norm_pool(t)
            t.skip(a=1 + 4 * NT + 2 + NH, v=NT + len(local.units) + 1 + NH, s=len(local.units), o=NT + 2)

        def turn(first, second):
            STAGES = ("mamba", "cross0", "experts", "window", "cross1", "local0", "local1")
            spans = dict(mamba=MAMBA_END, cross0=CROSS_END, experts=EXPERTS_END, window=WINDOW_END + 12,
                         cross1=CROSS_END, local0=LOCAL_END + GEGLU, local1=LOCAL_END + GEGLU)
            starts = {n: sum(spans[k] for k in STAGES[:i]) for i, n in enumerate(STAGES)}
            logs = []

            def both(eng, name, stages):
                lanes = [Lane(eng, sems_of[i], None if name == "pe" else name + "_step", ps[i], rows[i]) for i in (0, 1)]
                interleave(*(run(t, [(starts[n] + i * LAG, g) for n, g in zip(STAGES, stages(t))])
                             for i, t in enumerate(lanes)))
                logs.append([t.log for t in lanes])

            with nc.Block() as block:
                @block.sync
                def _(sp):
                    batches = (first, second)
                    tokens = lambda v: v.rearrange("(t p) d -> p t d", p=P)
                    for b, m, d in zip(batches, rows, sems_of):
                        sp.dma_start(m.x[:, :, :], tokens(x_in[b])).then_inc(d["x_loaded"], 16)
                        sp.dma_start(m.folded[:, :], folded_dram[b]).then_inc(d["score_loaded"], 16)
                    for k in range(E + 1):
                        if k == NE:
                            for b, m, d in zip(batches, rows, sems_of):
                                sp.wait_ge(d["norm_ready"], 3)
                                sp.dma_start(m.folded[:, :], folded_dram[B + b]).then_inc(d["score_loaded"], 16)
                        if k >= NE:
                            for d in sems_of:
                                sp.wait_ge(d["acc_ready"], max(k - NE, 1))
                        sp.dma_start(we[:, k % NE, :], experts_in[k]).then_inc(shared[f"expert{k % NE}_loaded"], 16)
                    for b, m, d in zip(batches, rows, sems_of):
                        sp.wait_ge(d["y_ready"], 1)
                        sp.dma_start(tokens(out[b]), m.x[:, :, :]).then_inc(d["stored"], 16)
                    for d in sems_of:
                        sp.wait_ge(d["stored"], 16)

                @block.gpsimd
                def _(pool):
                    both(pool, "pool",
                         lambda t: [mamba_pool(t), cross_pool(t, True), experts_pool(t), window_pool(t),
                                    cross_pool(t, False), local_pool(t, 0), local_pool(t, 1)])

                @block.scalar
                def _(act):
                    both(act, "act",
                         lambda t: [mamba_scalar(t), cross_scalar(t, DH1 ** -0.5, True), experts_scalar(t),
                                    window_scalar(t), cross_scalar(t, DH3 ** -0.5, False), local_scalar(t, 0),
                                    local_scalar(t, 1)])

                @block.vector
                def _(dve):
                    both(dve, "dve",
                         lambda t: [mamba_vector(t), cross_vector(t, True), experts_vector(t), window_vector(t),
                                    cross_vector(t, False), local_vector(t, 0), local_vector(t, 1)])

                @block.tensor
                def _(pe):
                    both(pe, "pe",
                         lambda t: [mamba_tensor(t), cross_tensor(t, True, row_x0), experts_tensor(t),
                                    window_tensor(t), cross_tensor(t, False, row("b_x1")), local_tensor(t, 0),
                                    local_tensor(t, 1)])
            assert all(v == logs[0] for v in logs), logs
            nc.sync.sem_clear(sems)
            nc.all_engine_barrier()

        with nc.Fori(0, B // 2) as b:
            turn(b, b + B // 2)


def shape_constants(group):
    c, f = {}, np.float32
    c["ident"] = np.eye(P, dtype=f)
    c["mean"] = np.full((P, P), 1.0 / P, f)
    t = np.arange(T, dtype=np.float64)
    inv = 1.0 / 10000.0 ** (np.arange(0, DH3, 2) / DH3)
    ang = (t[:, None] * inv[None]).astype(f).astype(np.float64)
    cos, sin = np.tile(np.cos(ang), 2), np.tile(np.sin(ang), 2)
    sin[:, :DH3 // 2] *= -1
    r = np.stack([np.stack([cos * DH3 ** -0.5, cos], 1), np.stack([sin * DH3 ** -0.5, sin], 1)], 1)
    c["rope3"] = r.reshape(NT, P, 2 * 2 * DH3).transpose(1, 0, 2).reshape(P, -1)
    half = np.arange(0, DH5, 2)
    inv = 1.0 / 10000.0 ** (half / DH5)
    ang = (t[:, None] * inv[None]).astype(f).astype(np.float64)
    cos, sin = np.tile(np.cos(ang), 2), np.tile(np.sin(ang), 2)
    sin[:, :DH5 // 2] *= -1
    base = (half + 0.4 * DH5) / (1.4 * DH5)
    scale = np.tile(base[None] ** ((t - T // 2) / 32.0)[:, None], 2)
    r = np.stack([cos * scale * 8.0, sin * scale * 8.0, cos / scale, sin / scale])
    c["tables"] = r.reshape(4, NT, P, DH5).transpose(2, 0, 1, 3).reshape(P, -1)
    p = np.arange(P)
    c["pair"] = (p[:, None] // 64 == np.arange(2)[None]).astype(f)
    c["head"] = (p[:, None] // DH3 == np.arange(H3)[None]).astype(f)
    c["iota"] = np.tile(np.arange(E, dtype=f), (P, 1))
    c["eps"] = np.full((P, 1), EPS, f)
    c["neg_half"] = np.full((P, 1), -0.5, f)
    c["one"] = np.ones((P, 1), f)
    return np.concatenate([np.asarray(c[n], f) for n in GROUPS[group]], axis=1)


def bf16_constants(bf16):
    q, k = np.arange(P)[:, None], np.arange(P)[None]
    band = lambda prev, cur: np.where(np.concatenate([prev, cur], 1), 0.0, NEG)
    sel = (np.arange(P)[:, None] % 32 == np.arange(2 * NS)[None]).astype(np.float32)
    parts = [np.eye(P), band(k >= q + 1, k <= q), band(k >= q + 64, (k <= q) & (q - k <= 64)), sel]
    return np.concatenate(parts, axis=1).astype(bf16)


def blocks(a, rows=P):
    n = a.shape[0] // rows
    return a.reshape(n, rows, -1).transpose(1, 0, 2).reshape(rows, -1)


def fill(a, rows=P):
    out = np.zeros((rows,) + a.shape[1:], a.dtype)
    out[:a.shape[0]] = a
    return out


def col(a):
    return np.asarray(a).reshape(-1, P).T


def spread(a):
    return np.broadcast_to(np.asarray(a).reshape(1, -1), (P, a.size))


def pack(w):
    g = {n: {} for n in GROUPS}
    m = g["mamba"]
    m["w_in"] = w["L0_attn_in_proj_w"].T
    m["w_conv"] = spread(np.ascontiguousarray(w["L0_attn_conv_w"][:, 0, :].T))
    m["norm_w"] = w["L0_attn_norm_w"][:, None]
    m["conv_b"] = col(w["L0_attn_conv_b"])
    xp = w["L0_attn_x_proj_w"]
    bc = xp[DTR:]
    m["x_bc"] = blocks(np.ascontiguousarray(np.concatenate([bc, bc, bc], 0).T))
    m["x_dt"] = blocks(np.ascontiguousarray(xp[:DTR].T))
    m["w_dt"] = fill(w["L0_attn_dt_proj_w"].T)
    m["b_dt"] = col(w["L0_attn_dt_proj_b"])
    m["a_log"] = blocks(w["L0_attn_A_log"])
    m["d_skip"] = col(w["L0_attn_D"])
    m["w_out"] = blocks(np.ascontiguousarray(w["L0_attn_out_proj_w"].T))
    c = g["cross0"]
    c["ctx"] = w["ctx_1024"].reshape(B * S, D).T
    c["w_qT"] = blocks(np.ascontiguousarray(w["L0_xattn_w_q"].T))
    c["w_k"] = w["L0_xattn_w_kv"][:, :1024]
    c["w_v"] = w["L0_xattn_w_kv"][:, 1024:]
    c["w_o"] = blocks(w["L0_xattn_w_out"])
    g["experts"]["gamma"] = col(w["L0_xattn_ln_gamma"])
    g["experts"]["beta"] = col(w["L0_xattn_ln_beta"])
    c["gate"] = spread(w["L0_xattn_gate"])
    c["w4_q"] = w["L1_xattn_Wq"]
    c["w4_k"] = w["L1_xattn_Wkv"][:D].T
    c["w4_v"] = w["L1_xattn_Wkv"][D:].T
    c["w4_o"] = w["L1_xattn_Wout"].T
    e = g["experts"]
    w1 = np.concatenate([w["L0_ffn_shared_w1"][None], w["L0_ffn_spec_w1"]], 0)
    b1 = np.concatenate([w["L0_ffn_shared_b1"][None], w["L0_ffn_spec_b1"]], 0)
    e["b1"] = col(b1)
    w2 = np.concatenate([w["L0_ffn_shared_w2"][None], w["L0_ffn_spec_w2"]], 0)
    w2 = w2.reshape(E + 1, D, NF, P).transpose(0, 3, 2, 1).reshape(E + 1, P, FF)
    experts = np.ascontiguousarray(np.concatenate([w1.transpose(0, 2, 1), w2], axis=2))
    e["b2s"] = col(w["L0_ffn_shared_b2"])
    e["router"] = w["L0_ffn_router_w"].T
    e["b2e"] = fill(w["L0_ffn_spec_b2"])
    h = DH3 // 2
    turned = lambda a: np.concatenate([a.reshape(H3, 2, h, D)[:, 1:], a.reshape(H3, 2, h, D)[:, :1]], 1).reshape(D, D)
    wq, wk = w["L1_attn_Wq"], w["L1_attn_Wk"]
    g["window"]["w_qk"] = np.concatenate([wq, wk, turned(wq), turned(wk)], 0).T
    g["window"]["w_v"] = w["L1_attn_Wv"].T
    g["window"]["w_o"] = w["L1_attn_Wo"].T.reshape(4, 4, DH3, D).transpose(1, 0, 2, 3).reshape(D, D)
    f = g["local"]
    f["w_qkv"] = w["L1_ffn_wqkv"].transpose(1, 0, 2).reshape(P, -1)
    qs, ks = w["L1_ffn_q_scale"], w["L1_ffn_k_scale"]
    swap = lambda a: np.concatenate([a[:, 32:], a[:, :32]], 1)
    c["scales"] = spread(np.stack([qs, swap(qs), ks, swap(ks)], 1))
    f["w_o"] = w["L1_ffn_wo"].reshape(DEPTH, 4, P, D).transpose(2, 0, 1, 3).reshape(P, -1)
    f["ln_g"], f["ln_b"] = w["L1_ffn_ln_g"].T, w["L1_ffn_ln_b"].T
    f["w1"] = w["L1_ffn_w1"].transpose(1, 0, 2).reshape(P, -1)
    b1 = np.zeros((DEPTH, 2, NH * P), np.float32)
    b1[:, :, :HID] = w["L1_ffn_b1"].reshape(DEPTH, 2, HID)
    f["b1"] = b1.reshape(DEPTH * 2 * NH, P).T
    w2 = np.zeros((DEPTH, NH * P, D), np.float32)
    w2[:, :HID] = w["L1_ffn_w2"]
    f["w2"] = w2.reshape(DEPTH * NH, P, D).transpose(1, 0, 2).reshape(P, -1)
    r = g["rows"]
    r["b_x0"], r["b_win"], r["b_x1"] = w["L0_xattn_b_out"][None], w["L1_attn_bo"][None], w["L1_xattn_bout"][None]
    r["b2_0"], r["b2_1"] = w["L1_ffn_b2"][0:1], w["L1_ffn_b2"][1:2]
    r["ones"] = np.ones((1, P), np.float32)
    r["router"] = w["L0_ffn_router_b"][None]
    out = {}
    for n, cols in GROUPS.items():
        if n in ("const", "rope5"):
            out[n] = shape_constants(n)
            continue
        for k, width in cols.items():
            assert g[n][k].shape == (ROWS.get(n, P), width), (n, k, g[n][k].shape, width)
        out[n] = np.ascontiguousarray(np.concatenate([g[n][k] for k in cols], axis=1))
    return out, experts


def kernel(**inputs):
    import concourse.bacc as bacc
    from concourse.bass_utils import run_bass_kernel_spmd

    w = {n: np.asarray(v) for n, v in inputs.items()}
    groups, experts = pack(w)
    arrays = {"in_" + n: v for n, v in groups.items()}
    arrays["in_expert_weights"] = experts
    arrays["in_x"] = np.ascontiguousarray(w["x"])
    arrays["in_bf16"] = bf16_constants(mybir.dt.np(BF16))
    nc = bacc.Bacc("TRN2", target_bir_lowering=False, num_devices=1)
    aps = {n: nc.dram_tensor(n, a.shape, mybir.dt.from_np(a.dtype), kind="ExternalInput").ap()
           for n, a in arrays.items()}
    out = nc.dram_tensor("out", (B, T, D), F32, kind="ExternalOutput").ap()
    folded_dram = nc.dram_tensor("folded_products", (2 * B, P, 1024), F32, kind="Internal").ap()
    decoder_kernel(nc, aps["in_x"], {g: aps["in_" + g] for g in GROUPS}, aps["in_bf16"],
                   aps["in_expert_weights"], folded_dram, out)
    r = run_bass_kernel_spmd(nc, [arrays], core_ids=[0])
    return r.results[0]["out"]
```

```python
from contextlib import ExitStack

import numpy as np

import concourse.bass as bass
from concourse import mybir

F32 = mybir.dt.float32
BF16 = mybir.dt.bfloat16
U32 = mybir.dt.uint32
ACT = mybir.ActivationFunctionType
ALU = mybir.AluOpType
X = mybir.AxisListType.X

B, T, D = 4, 512, 128
P = 128
NT = T // P
S = 32
CH, NS, KC, DTR = 256, 16, 4, 8
NB = CH // P
H1, DH1 = 16, 64
E, FF = 8, 512
NF = FF // P
H3, DH3 = 16, 8
H5, DH5 = 8, 64
HID = 341
NH = 3
HC = [min(P, HID - P * c) for c in range(NH)]
DEPTH = 2
EPS = 1e-5
SCRATCH = 12288
NEG = -1e30

GROUPS = {
    "mamba": dict(w_in=512, conv_w=NB * KC, norm_w=1, conv_b=NB, x_bc=NB * 96, x_dt=NB * DTR,
                  w_dt=CH, b_dt=NB, a_log=NB * NS, d_skip=NB, w_out=NB * D),
    "cross0": dict(ctx=B * S, w_qT=8 * P, w_k=1024, w_v=1024, w_o=8 * P, gate=1,
                   w4_q=D, w4_k=D, w4_v=D, w4_o=D,
                   scales=DEPTH * 4 * DH5),
    "rope5": dict(tables=NT * 4 * DH5),
    "experts": dict(b1=(E + 1) * NF, router=E, b2=D, gamma=1, beta=1),
    "window": dict(w_qk=4 * D, w_v=D, w_o=D),
    "local": dict(w_qkv=DEPTH * 1536, w_o=DEPTH * 4 * D, ln_g=DEPTH, ln_b=DEPTH,
                  w1=DEPTH * 2 * HID, b1=DEPTH * 2 * NH, w2=DEPTH * NH * D),
    "rows": dict(b_x0=D, b_win=D, b_x1=D, b2_0=D, b2_1=D, router=E, ones=P),
    "const": dict(ident=P, mean=P, rope3=NT * 2 * 2 * DH3,
                  pair=2, head=H3, iota=E, eps=1, neg_half=1, one=1),
}
FIRST, REST = ["cross0", "const"], [g for g in GROUPS if g not in ("cross0", "const")]
WIDTH = {g: sum(c.values()) for g, c in GROUPS.items()}
ROWS = {"rows": 1}
CB = dict(ident=P, band3=2 * P, band5=2 * P, select=2 * NS)

STATES_AT, STATE_STEP = 40, 4
CROSS_STEP, EXPERT_STEP, ROPE_STEP, QKV_STEP, WINDOW_STEP, LOCAL_STEP, GEGLU = 5, 6, 4, 11.5, 3.5, 4.3, 45
LAGS = dict(zip("mamba cross0 experts window cross1 local0 local1".split(), (0, 1, 1, 1, 1, 12.5, 11)))
MAMBA_END = STATES_AT + STATE_STEP * NS + 16
CROSS_END = 12 + CROSS_STEP * (NT + 2) + 8
EXPERTS_END = 10 + EXPERT_STEP * (E + 1) + 28


class Waits:

    def __init__(self, eng, own):
        self.eng, self.own, self.asked, self.steps = eng, own, {}, 0

    def __call__(self, sem, k=1):
        n = self.asked.get(sem.name, 0) + k
        self.asked[sem.name] = n
        if n > 0:
            self.eng.wait_ge(sem, n)

    def step(self, ins):
        self.steps += 1
        ins.then_inc(self.own, 1)
        self.eng.wait_ge(self.own, self.steps)


class Ring:

    def __init__(self, eng, banks, filled, freed):
        self.eng, self.banks, self.n, self.filled, self.freed, self.at = eng, banks, len(banks), filled, freed, 0

    def use(self, n):
        self.n = n

    def bank(self):
        return self.banks[(self.at - 1) % self.n]

    def open(self):
        if self.at >= self.n:
            self.eng.wait_ge(self.freed, self.at - self.n + 1)
        self.at += 1
        return self.bank()

    def take(self):
        self.at += 1
        self.eng.wait_ge(self.filled, self.at)
        return self.bank()


class Lane:

    def __init__(self, eng, s, own, ps, m=None):
        self.eng, self.s, self.m, self.w = eng, s, m, Waits(eng, s[own] if own else None)
        self.a = Ring(eng, ps["a"], s["a_filled"], s["a_freed"])
        self.v = Ring(eng, ps["v"], s["v_filled"], s["v_freed"])
        self.o = Ring(eng, ps["o"], s["o_filled"], s["o_freed"])
        self.s_ = Ring(eng, ps["s"], s["s_filled"], s["s_freed"])
        self.log = []

    def counts(self):
        return self.a.at, self.v.at, self.o.at, self.s_.at

    def skip(self, a=0, v=0, s=0, o=0):
        self.a.at += a
        self.v.at += v
        self.o.at += o
        self.s_.at += s


class Row:
    pass


def run(lane, stages):
    for start, stage in stages:
        for at in stage:
            yield start + at
        lane.log.append(lane.counts())


def interleave(first, second):
    now = [next(first, None), next(second, None)]
    while now[0] is not None or now[1] is not None:
        if now[1] is None or (now[0] is not None and now[0] <= now[1]):
            now[0] = next(first, None)
        else:
            now[1] = next(second, None)


def decoder_kernel(nc, x_in, packed, cb_in, experts_in, folded_dram, out):
    with ExitStack() as ctx:
        def sb(name, shape, dt=F32):
            return ctx.enter_context(nc.sbuf_tensor(name, shape, dt))

        def sem(name):
            return ctx.enter_context(nc.semaphore(name))

        psum = ctx.enter_context(nc.psum_tensor("psum", [P, 8, 512], F32))
        bank = [psum[:, i] for i in range(8)]
        ps = [dict(a=bank[i:i + 2], s=bank[i:i + 2], v=bank[i + 2:i + 4], o=bank[i + 3:i + 4]) for i in (0, 4)]

        scratch = [sb("scratch_0", [P, SCRATCH]), sb("scratch_1", [P, SCRATCH])]
        used = [0, 0]

        def carve(of, *shape):
            n = int(np.prod(shape))
            v = scratch[of][:, used[of]:used[of] + n]
            used[of] += n
            assert used[of] <= SCRATCH, used
            names = "abcde"[:len(shape)]
            if len(shape) == 1:
                return v
            return v.rearrange(f"p ({' '.join(names)}) -> p {' '.join(names)}",
                               **dict(zip(names[:-1], shape[:-1])))

        def again(of, at=0):
            used[of] = at

        wt, cols = {}, {}
        for g, c in GROUPS.items():
            if g in ("cross0", "rope5"):
                wt[g] = carve(1, WIDTH[g])
            else:
                wt[g] = sb("w_" + g, [ROWS.get(g, P), WIDTH[g]])
            at = 0
            for n, w in c.items():
                cols[g, n] = (at, at + w)
                at += w

        def W(group, name, **dims):
            a, b = cols[group, name]
            v = wt[group][:, a:b]
            if dims:
                v = v.rearrange(f"p ({' '.join(dims)} z) -> p {' '.join(dims)} z", **dims)
            return v

        cb = sb("cb", [P, sum(CB.values())], BF16)
        cbv, at = {}, 0
        for n, w in CB.items():
            cbv[n] = cb[:, at:at + w]
            at += w
        ident, mean_w, ones = W("const", "ident"), W("const", "mean"), W("rows", "ones")
        eps, one = W("const", "eps"), W("const", "one")
        row = lambda n: W("rows", n).rearrange("p (o z) -> p o z", o=1).to_broadcast([1, NT, D])

        w_in = W("mamba", "w_in")
        a_neg = sb("a_neg", [P, NB, NS])
        gate = sb("gate", [P, 1])
        b_x0 = W("rows", "b_x0")
        tab5 = sb("tab5", [P, DEPTH, 4, NT, DH5])

        NE = 3
        we = sb("expert_weights", [P, NE, 2 * FF])

        kbd, vbd = carve(0, B, 512), carve(0, B, 512)
        folded = carve(0, 2 * B, 1024)
        kbd1, vbd1 = carve(1, B, 512), carve(1, B, 512)
        row_x0 = b_x0.rearrange("p (o z) -> p o z", o=1).to_broadcast([1, NT, D])

        def row_buffers(i):
            m = Row()
            own = lambda name, shape, dt=F32: sb(f"{name}_{i}", shape, dt)
            m.x = own("x", [P, NT, D])
            m.y = own("y", [P, NT, D])
            m.xT = own("xT", [P, T])
            m.x_flat = m.x[:, :, :].rearrange("p t d -> p (t d)")
            m.y_flat = m.y[:, :, :].rearrange("p t d -> p (t d)")
            m.hT = own("hT", [P, T])
            m.rowstat = own("rowstat", [P, NT, 6])
            m.mv, m.rstd = own("mv", [P, NT, 2]), own("rstd", [P, NT])
            m.small = own("small", [P, 6, 16])
            m.mx, m.sums, m.rinv = (own(n, [P, 2, H1]) for n in ("mx", "sums", "rinv"))
            m.mx2, m.sums2, m.rinv2 = (own(n, [P, 64]) for n in ("mx2", "sums2", "rinv2"))
            m.m8, m.i8 = own("m8", [P, NT, 8]), own("i8", [P, NT, 8], U32)
            m.lg, m.eqt = own("lg", [P, NT, E]), own("eqt", [P, NT, E])
            m.comb = own("comb", [P, NT, E + 1])
            m.folded = own("folded", [P, 1024])
            m.score = m.folded[:, 0:512]
            m.value = m.folded[:, 512:1024].rearrange("p (j d) -> p j d", j=4)
            again(i)
            m.u, m.zs, m.delta, m.du = (carve(i, NB, T) for _ in range(4))
            m.dA = carve(i, 4, T)
            early = used[i]
            m.dBu, m.hs, m.hC = carve(i, 2, T), carve(i, 2, T), carve(i, 4, T)
            m.mid = carve(i, T // 2).bitcast(BF16)
            m.parts = carve(i, T // 2).bitcast(BF16)
            again(i, early)
            m.rest, m.dtS = carve(i, T), carve(i, T)
            again(i, early + 4 * T)
            m.sp1, m.sp2 = carve(i, NB, T), carve(i, NB, T)
            m.yg = m.delta
            again(i)
            m.e1, m.pT1 = carve(i, 2, T), carve(i, 2, 4, P)
            again(i)
            m.hid, m.combT = carve(i, 2, NF, T), carve(i, T)
            again(i)
            m.qk, m.ra, m.rb = carve(i, 2, 1024), carve(i, 2, 1024), carve(i, 2, 1024)
            after = used[i]
            m.qT, m.kT, m.vv = carve(i, 4, T), carve(i, 4, T), carve(i, NT, 512)
            again(i)
            m.pr, m.pT, m.oT = carve(i, 3, 512), carve(i, 2, 512), carve(i, 4, T)
            assert used[i] <= after
            again(i, used[i] - 3 * T)
            m.qpad, m.kpad = carve(i, 2, 512), carve(i, 2, 512)
            m.ra3, m.rb3 = carve(i, 2, 256), carve(i, 2, 256)
            assert used[i] <= after
            again(i, SCRATCH - NT * H3 * 32)
            m.vpad = carve(i, NT, H3, 32)
            again(i)
            m.hc, m.sq, m.rst, m.gg, m.uu = carve(i, T), carve(i, T), carve(i, T), carve(i, NH, T), carve(i, NH, T)
            return m

        rows = [row_buffers(0), row_buffers(1)]

        own_names = ("act_step dve_step pool_step a_filled a_freed v_filled v_freed o_filled o_freed s_filled s_freed "
                     "stats_ready rstd_ready norm_ready score_loaded e_ready prob_ready pT_used x_loaded "
                     "squares_ready rms_ready u_ready soft_ready delta_ready parts_ready decay_ready decay_used states_used "
                     "sum_filled sums_read gated_ready gap_ready ratio_ready comb_ready expert_done pads_ready "
                     "max_ready ss_ready root_ready rope_ready sq_ready rst_ready hn_ready "
                     "y_ready stored ")
        shared_names = ("first_loaded loaded cb_loaded setup_act folded_stored "
                        "expert0_loaded expert1_loaded expert2_loaded ")
        shared = {n: sem(n) for n in shared_names.split()}
        sems_of = [dict(shared, **{n: sem(f"row{i}_{n}") for n in own_names.split()}) for i in (0, 1)]
        s = sems_of[0]
        every = {v.num for d in sems_of for v in d.values()}
        sems = range(min(every), max(every) + 1)
        assert len(sems) == len(every)

        KV_BANKS = 18
        with nc.Block() as block:
            @block.sync
            def _(sp):
                for g in FIRST + REST:
                    sp.dma_start(wt[g][:, :], packed[g]).then_inc(s["first_loaded" if g in FIRST else "loaded"], 16)
                sp.dma_start(cb[:, :], cb_in).then_inc(s["cb_loaded"], 16)
                sp.wait_ge(s["cb_loaded"], 16)
                for i in range(2 * B):
                    sp.wait_ge(s["v_freed"], KV_BANKS + 2 * (i + 1))
                    sp.dma_start(folded_dram[i], folded[:, i, :]).then_inc(s["folded_stored"], 16)
                sp.wait_ge(s["folded_stored"], 16 * 2 * B)

            @block.gpsimd
            def _(pool):
                for m in rows:
                    nc.gpsimd.memset(m.hT[:, :], 0.0)
                    nc.gpsimd.memset(m.comb[:, :, E:E + 1], 1.0)

            @block.scalar
            def _(act):
                act.wait_ge(s["first_loaded"], 16 * len(FIRST))
                act.activation(gate[:, :], W("cross0", "gate"), ACT.Tanh).then_inc(s["setup_act"], 1)
                act.wait_ge(s["loaded"], 16 * len(REST))
                act.activation(a_neg[:, :, :], W("mamba", "a_log", b=NB), ACT.Exp).then_inc(s["setup_act"], 1)

            @block.vector
            def _(dve):
                t = Lane(dve, s, "dve_step", dict(ps[0], v=bank))
                w, v = t.w, t.v
                w(s["first_loaded"], 16 * len(FIRST))
                pair = W("const", "pair").rearrange("p (a i b) -> p a i b", a=1, b=1).to_broadcast([P, B, 2, S])
                for p in range(8):
                    for dst in (kbd, vbd):
                        src = v.take()[:, 0:B * S].rearrange("p (b o k) -> p b o k", b=B, o=1)
                        dve.tensor_tensor(dst[:, :, p * 2 * S:(p + 1) * 2 * S].rearrange("p b (i k) -> p b i k", i=2),
                                          src.to_broadcast([P, B, 2, S]), pair, ALU.mult).then_inc(s["v_freed"], 1)
                head = W("const", "head").rearrange("p (a i b) -> p a i b", a=1, b=1).to_broadcast([P, B, H3, S])
                for dst in (kbd1, vbd1):
                    src = v.take()[:, 0:B * S].rearrange("p (b o k) -> p b o k", b=B, o=1)
                    for b in range(B):
                        ins = dve.tensor_tensor(dst[:, b].rearrange("p (i k) -> p i k", i=H3),
                                                src[:, b].to_broadcast([P, H3, S]), head[:, b], ALU.mult)
                    ins.then_inc(s["v_freed"], 1)
                w(s["setup_act"])
                for b in range(B):
                    dve.tensor_copy(folded[:, b, 0:512], v.take()).then_inc(s["v_freed"], 1)
                    dve.tensor_scalar(folded[:, b, 512:1024], v.take(), gate[:, :], None, ALU.mult)\
                        .then_inc(s["v_freed"], 1)
                w(s["loaded"], 16 * len(REST))
                dve.tensor_scalar(w_in[:, :], W("mamba", "w_in"), W("mamba", "norm_w"), None, ALU.mult)
                w(s["setup_act"])
                dve.tensor_scalar(a_neg[:, :, :], a_neg[:, :, :], -1.0, None, ALU.mult)
                dve.tensor_scalar(b_x0, b_x0, gate[0:1, :], None, ALU.mult)
                rope = W("rope5", "tables", f=4, t=NT)
                for l in range(DEPTH):
                    sc = W("cross0", "scales", l=DEPTH, f=4)
                    for f in range(4):
                        by = sc[:, l, f, :].rearrange("p (o z) -> p o z", o=1).to_broadcast([P, NT, DH5])
                        dve.tensor_tensor(tab5[:, l, f], rope[:, f], by, ALU.mult)
                for b in range(B):
                    for half in (0, 512):
                        dve.tensor_copy(folded[:, B + b, half:half + 512], v.take()).then_inc(s["v_freed"], 1)

            @block.tensor
            def _(pe):
                t = Lane(pe, s, None, dict(ps[0], v=bank))
                w, v = t.w, t.v
                w(s["first_loaded"], 16 * len(FIRST))
                ctxT = W("cross0", "ctx")
                for p in range(8):
                    for n in ("w_k", "w_v"):
                        pe.matmul(v.open()[:, 0:B * S], W("cross0", n)[:, p * P:(p + 1) * P], ctxT,
                                  start=True, stop=True).then_inc(s["v_filled"], 1)
                for n in ("w4_k", "w4_v"):
                    pe.matmul(v.open()[:, 0:B * S], W("cross0", n), ctxT, start=True, stop=True).then_inc(s["v_filled"], 1)
                pe.wait_ge(s["v_freed"], 16)
                for b in range(B):
                    own = v.open()
                    for p in range(8):
                        ins = pe.matmul(own[:, p * 64:(p + 1) * 64], W("cross0", "w_qT")[:, p * P:(p + 1) * P],
                                        kbd[:, b, p * 64:(p + 1) * 64], start=(p == 0), stop=(p == 7),
                                        skip_group_check=True)
                    ins.then_inc(s["v_filled"], 1)
                    own = v.open()
                    for j in range(4):
                        for i in range(2):
                            p = 2 * j + i
                            ins = pe.matmul(own[64 * i:64 * i + 64, j * D:(j + 1) * D],
                                            vbd[:, b, p * 64:(p + 1) * 64], W("cross0", "w_o")[:, p * P:(p + 1) * P],
                                            start=(j == 0), stop=(j == 3), skip_group_check=True)
                    ins.then_inc(s["v_filled"], 1)
                pe.wait_ge(s["v_freed"], KV_BANKS)
                for b in range(B):
                    pe.matmul(v.open()[:, :], W("cross0", "w4_q"), kbd1[:, b], start=True, stop=True)\
                        .then_inc(s["v_filled"], 1)
                    own = v.open()
                    for j in range(4):
                        ins = pe.matmul(own[:, j * D:(j + 1) * D], vbd1[:, b, j * P:(j + 1) * P], W("cross0", "w4_o"),
                                        start=(j == 0), stop=(j == 3), skip_group_check=True)
                    ins.then_inc(s["v_filled"], 1)
        nc.sync.sem_clear(sems)
        nc.all_engine_barrier()

        def tok(v, t):
            return v[:, t * P:(t + 1) * P]

        def norm_vector(t, dst, src, done):
            for i in range(NT):
                ins = t.eng.bn_stats(t.m.rowstat[:, i, :], src[:, i, :])
            t.w.step(ins)
            for i in range(NT):
                ins = t.eng.bn_aggr(t.m.mv[:, i, :], t.m.rowstat[:, i, :])
            ins.then_inc(t.s["stats_ready"], 1)
            t.w(t.s["rstd_ready"])
            for i in range(NT):
                ins = t.eng.tensor_scalar(dst[:, i, :], src[:, i, :], t.m.mv[:, i, 0:1], t.m.rstd[:, i:i + 1],
                                          ALU.subtract, ALU.mult)
            ins.then_inc(t.s[done], 1)
            t.w(t.s[done])

        def inverse_root(t, dst, src, op, by, done):
            t.w.step(t.eng.tensor_scalar(dst, src, by, None, op))
            t.eng.tensor_tensor(dst, dst, W("const", "neg_half").to_broadcast([P, dst.shape[1]]), ALU.pow)\
                .then_inc(t.s[done], 1)

        def norm_pool(t):
            t.w(t.s["stats_ready"])
            inverse_root(t, t.m.rstd[:, :], t.m.mv[:, :, 1], ALU.add, EPS, "rstd_ready")

        def turn_tensor(t, src):
            bank = t.a.open()
            for i in range(NT):
                ins = t.eng.transpose(tok(bank, i), src[:, i, :], ident)
            ins.then_inc(t.s["a_filled"], 1)
            return t.a.at

        def plain_scalar(t):
            t.eng.activation(t.m.xT[:, :], t.a.take(), ACT.Copy).then_inc(t.s["a_freed"], 1)

        def residual_vector(t, dst, times=None):
            t.w(t.s["o_filled"])
            t.skip(o=1)
            bank = t.o.bank()
            if times:
                ins = t.eng.scalar_tensor_tensor(dst, t.m.x_flat, times, bank, ALU.mult, ALU.add)
            else:
                ins = t.eng.tensor_tensor(dst, bank, t.m.x_flat, ALU.add)
            ins.then_inc(t.s["o_freed"], 1)
            t.eng.wait_ge(t.s["o_freed"], t.o.at)

        def mamba_tensor(t):
            pe = t.eng
            yield 2
            t.w(t.s["rms_ready"])
            turn_tensor(t, t.m.y)
            pe.wait_ge(t.s["a_freed"], t.a.at)
            yield 8
            for c in range(NB):
                pe.matmul(t.v.open(), w_in[:, c * P:(c + 1) * P], t.m.xT[:, :], start=True, stop=True)\
                    .then_inc(t.s["v_filled"], 1)
            for c in range(NB):
                pe.matmul(t.a.open(), w_in[:, CH + c * P:CH + (c + 1) * P], t.m.xT[:, :], start=True, stop=True)\
                    .then_inc(t.s["a_filled"], 1)
            yield 20
            t.w(t.s["u_ready"])
            bank = t.a.open()
            for c in range(NB):
                ins = pe.matmul(bank[0:DTR, :], W("mamba", "x_dt", c=NB)[:, c, :], t.m.u[:, c, :],
                                start=(c == 0), stop=(c == NB - 1))
            ins.then_inc(t.s["a_filled"], 1)
            dt_at = t.a.at
            bank = t.v.open()
            for c in range(NB):
                ins = pe.matmul(bank[0:96, :], W("mamba", "x_bc", c=NB)[:, c, :], t.m.u[:, c, :],
                                start=(c == 0), stop=(c == NB - 1))
            ins.then_inc(t.s["v_filled"], 1)
            yield 26
            pe.wait_ge(t.s["a_freed"], dt_at)
            for c in range(NB):
                pe.matmul(t.a.open(), W("mamba", "w_dt")[0:DTR, c * P:(c + 1) * P], t.m.dtS[0:DTR, :],
                          start=True, stop=True).then_inc(t.s["a_filled"], 1)
            t.w(t.s["parts_ready"])
            pe.wait_ge(t.s["a_freed"], t.a.at)
            sum_banks = [t.a.banks[0], t.a.banks[1]]
            for n in range(NS + 1):
                yield STATES_AT + STATE_STEP * n
                if n < NS:
                    for which in (n, NS + n):
                        pe.matmul(t.v.open(), cbv["select"][0:96, which:which + 1].to_broadcast([96, P]), t.m.parts[0:96, :],
                                  start=True, stop=True).then_inc(t.s["v_filled"], 1)
                if n >= 1:
                    pe.wait_ge(t.s["v_freed"], t.v.at - (2 if n < NS else 0))
                    for c in range(NB):
                        ins = pe.matmul(sum_banks[c], ident, t.m.hC[:, 2 * ((n - 1) % 2) + c, :],
                                        start=(n == 1), stop=(n == NS))
                        if n == NS:
                            ins.then_inc(t.s["sum_filled"], 1)
                    if n < NS:
                        ins.then_inc(t.s["states_used"], 1)
            yield MAMBA_END - 11
            t.w(t.s["gated_ready"])
            t.v.use(1)
            bank = t.o.open()
            for i in range(NT):
                for c in range(NB):
                    ins = pe.matmul(tok(bank, i), tok(t.m.yg[:, c, :], i), W("mamba", "w_out", c=NB)[:, c, :],
                                    start=(i == 0 and c == 0), stop=(i == NT - 1 and c == NB - 1),
                                    skip_group_check=True)
            ins.then_inc(t.s["o_filled"], 1)

        def mamba_scalar(t):
            act = t.eng
            yield 0
            t.w(t.s["x_loaded"], 16)
            for i in range(NT):
                ins = act.activation(tok(t.m.rest, i), t.m.x[:, i, :], ACT.Square, scale=D ** -0.5,
                                     accum_out=t.m.small[:, 0, i:i + 1])
            ins.then_inc(t.s["squares_ready"], 1)
            yield 2
            plain_scalar(t)
            yield 8
            for c in range(NB):
                act.activation(t.m.zs[:, c, :], t.a.take(), ACT.Silu).then_inc(t.s["a_freed"], 1)
            yield 12
            t.skip(v=NB)
            act.wait_ge(t.s["v_freed"], t.v.at)
            for c in range(NB):
                ins = act.activation(t.m.u[:, c, :], t.m.du[:, c, :], ACT.Silu, bias=W("mamba", "conv_b")[:, c:c + 1])
            ins.then_inc(t.s["u_ready"], 1)
            yield 20
            act.activation(t.m.dtS[0:DTR, :], t.a.take()[0:DTR, :], ACT.Copy).then_inc(t.s["a_freed"], 1)
            yield 26
            for c in range(NB):
                bank = t.a.take()
                act.activation(t.m.sp1[:, c, :], bank, ACT.Abs, bias=W("mamba", "b_dt")[:, c:c + 1])
                act.activation(t.m.sp2[:, c, :], bank, ACT.Relu, bias=W("mamba", "b_dt")[:, c:c + 1])\
                    .then_inc(t.s["a_freed"], 1)
            act.wait_ge(t.s["a_freed"], t.a.at)
            act.activation(t.m.sp1[:, :, :], t.m.sp1[:, :, :], ACT.Exp, scale=-1.0).then_inc(t.s["soft_ready"], 1)
            act.wait_ge(t.s["soft_ready"], 1)
            act.activation(t.m.delta[:, :, :], t.m.sp1[:, :, :], ACT.Ln, bias=one).then_inc(t.s["soft_ready"], 1)
            yield STATES_AT
            t.w(t.s["delta_ready"])
            for n in range(NS):
                yield STATES_AT + STATE_STEP * n
                for c in range(NB):
                    i = NB * n + c
                    if i >= 4:
                        t.w(t.s["decay_used"])
                    act.activation(t.m.dA[:, i % 4, :], t.m.delta[:, c, :], ACT.Exp, scale=a_neg[:, c, n:n + 1])\
                        .then_inc(t.s["decay_ready"], 1)
            t.skip(v=1 + 2 * NS, o=1)
            t.v.use(1)

        def mamba_vector(t):
            dve = t.eng
            yield 0
            t.w(t.s["rstd_ready"])
            for i in range(NT):
                ins = dve.tensor_scalar(t.m.y[:, i, :], t.m.x[:, i, :], t.m.rstd[:, i:i + 1], None, ALU.mult)
            ins.then_inc(t.s["rms_ready"], 1)
            t.skip(a=6)
            yield 8
            taps = W("mamba", "conv_w", c=NB)
            banks = [t.v.take() for c in range(NB)]
            for k in range(KC):
                for c in range(NB):
                    w, dst, src = taps[:, c, KC - 1 - k:KC - k], t.m.du[:, c, k:T], banks[c][:, 0:T - k]
                    if k == 0:
                        ins = dve.tensor_scalar(dst, src, w, None, ALU.mult)
                    else:
                        ins = dve.scalar_tensor_tensor(dst, src, w, dst, ALU.mult, ALU.add)
                        if k == KC - 1:
                            ins.then_inc(t.s["v_freed"], 1)
                if k < KC - 1:
                    t.w.step(ins)
            yield 20
            bank = t.v.take()
            t.w.step(dve.tensor_copy(t.m.parts[0:96, :], bank[0:96, :]))
            dve.tensor_tensor(t.m.rest[0:96, :], bank[0:96, :], t.m.parts[0:96, :], ALU.subtract)\
                .then_inc(t.s["v_freed"], 1)
            dve.wait_ge(t.s["v_freed"], t.v.at)
            t.w.step(dve.tensor_copy(t.m.mid[0:96, :], t.m.rest[0:96, :]))
            dve.tensor_copy(t.m.parts[32:64, :], t.m.mid[32:64, :])
            t.w.step(dve.tensor_tensor(t.m.rest[64:96, :], t.m.rest[64:96, :], t.m.mid[64:96, :], ALU.subtract))
            dve.tensor_copy(t.m.parts[64:96, :], t.m.rest[64:96, :]).then_inc(t.s["parts_ready"], 1)
            yield 26
            t.w(t.s["soft_ready"])
            t.w.step(dve.tensor_scalar(t.m.du[:, :, :], t.m.sp1[:, :, :], 1.0, 1.0, ALU.add, ALU.subtract))
            t.w.step(dve.tensor_tensor(t.m.du[:, :, :], t.m.sp1[:, :, :], t.m.du[:, :, :], ALU.subtract))
            t.w(t.s["soft_ready"])
            t.w.step(dve.tensor_tensor(t.m.delta[:, :, :], t.m.delta[:, :, :], t.m.du[:, :, :], ALU.add))
            t.w.step(dve.tensor_tensor(t.m.delta[:, :, :], t.m.delta[:, :, :], t.m.sp2[:, :, :], ALU.add))
            dve.tensor_tensor(t.m.du[:, :, :], t.m.delta[:, :, :], t.m.u[:, :, :], ALU.mult).then_inc(t.s["delta_ready"], 1)
            t.w(t.s["delta_ready"])
            for n in range(NS):
                yield STATES_AT + STATE_STEP * n
                bank = t.v.take().rearrange("p (o z) -> p o z", o=1).to_broadcast([P, NB, T])
                dve.tensor_tensor(t.m.dBu[:, :, :], t.m.du[:, :, :], bank, ALU.mult).then_inc(t.s["v_freed"], 1)
                dve.wait_ge(t.s["v_freed"], t.v.at)
                for c in range(NB):
                    i = NB * n + c
                    t.w(t.s["decay_ready"])
                    dve.tensor_tensor_scan(t.m.hs[:, c, :], t.m.dA[:, i % 4, :], t.m.dBu[:, c, :], 0.0, ALU.mult, ALU.add)\
                        .then_inc(t.s["decay_used"], 1)
                bank = t.v.take().rearrange("p (o z) -> p o z", o=1).to_broadcast([P, NB, T])
                if n >= 2:
                    t.w(t.s["states_used"])
                dve.wait_ge(t.s["decay_used"], NB * (n + 1))
                dve.tensor_tensor(t.m.hC[:, 2 * (n % 2):2 * (n % 2) + 2, :], t.m.hs[:, :, :], bank, ALU.mult)\
                    .then_inc(t.s["v_freed"], 1)
            yield STATES_AT + STATE_STEP * NS
            t.w(t.s["sum_filled"], 2)
            for c in range(NB):
                bank = t.a.banks[c]
                dve.scalar_tensor_tensor(t.m.yg[:, c, :], t.m.u[:, c, :], W("mamba", "d_skip")[:, c:c + 1], bank,
                                         ALU.mult, ALU.add).then_inc(t.s["sums_read"], 1)
            t.w(t.s["sums_read"], 2)
            dve.tensor_tensor(t.m.yg[:, :, :], t.m.yg[:, :, :], t.m.zs[:, :, :], ALU.mult).then_inc(t.s["gated_ready"], 1)
            t.v.use(1)
            yield MAMBA_END - 8
            residual_vector(t, t.m.y_flat, 2.0)
            norm_vector(t, t.m.x, t.m.y, "norm_ready")

        def mamba_pool(t):
            yield 0
            t.w(t.s["squares_ready"])
            inverse_root(t, t.m.rstd[:, :], t.m.small[:, 0, 0:NT], ALU.add, EPS, "rstd_ready")
            yield MAMBA_END - 8
            norm_pool(t)
            t.skip(a=6, v=NB + 1 + 2 * NS, o=1)
            t.v.use(1)

        def cross_tensor(t, inner, bias):
            pe = t.eng
            yield 1
            t.w(t.s["norm_ready"], 2 if inner else 1)
            turn_tensor(t, t.m.y if inner else t.m.x)
            pe.wait_ge(t.s["a_freed"], t.a.at)
            t.w(t.s["score_loaded"], 16)
            out_bank = t.o.open()
            pe.matmul(out_bank, ones[0:1, :], bias, start=True, stop=False, skip_group_check=True)
            for i in range(NT + 2):
                yield 12 + CROSS_STEP * i
                if i < NT:
                    pe.matmul(t.v.open(), tok(t.m.xT[:, :], i), t.m.score[:, :], start=True, stop=True)\
                        .then_inc(t.s["v_filled"], 1)
                if i >= 2:
                    pe.wait_ge(t.s["a_freed"], t.a.at)
                    for j in range(4):
                        ins = pe.matmul(tok(out_bank, i - 2), t.m.pT1[:, i % 2, j, :], t.m.value[:, j, :],
                                        start=False, stop=(i == NT + 1 and j == 3), skip_group_check=True)
                    ins.then_inc(t.s["o_filled"] if i == NT + 1 else t.s["pT_used"], 1)
                if 1 <= i <= NT:
                    t.w(t.s["prob_ready"])
                    bank = t.a.open()
                    for j in range(4):
                        ins = pe.transpose(tok(bank, j), tok(t.m.e1[:, (i - 1) % 2, :], j), ident)
                    ins.then_inc(t.s["a_filled"], 1)

        def cross_scalar(t, scale, inner):
            act = t.eng
            yield 1
            if inner:
                act.activation(t.m.xT[:, :], t.a.take(), ACT.Identity, scale=W("experts", "gamma"),
                               bias=W("experts", "beta")).then_inc(t.s["a_freed"], 1)
            else:
                plain_scalar(t)
            for i in range(NT + 1):
                yield 12 + CROSS_STEP * i
                if i < NT:
                    t.skip(v=1)
                    act.wait_ge(t.s["v_freed"], t.v.at)
                    act.activation(t.m.e1[:, i % 2, :], t.m.e1[:, i % 2, :], ACT.Exp, scale=scale)\
                        .then_inc(t.s["e_ready"], 1)
                if i >= 1:
                    if i >= 3:
                        t.w(t.s["pT_used"])
                    act.activation(t.m.pT1[:, (i - 1) % 2].rearrange("p j z -> p (j z)"), t.a.take(), ACT.Copy)\
                        .then_inc(t.s["a_freed"], 1)
            t.w(t.s["pT_used"], 1)
            t.skip(o=1)

        def cross_vector(t, inner):
            dve = t.eng
            yield 1
            if inner:
                norm_vector(t, t.m.y, t.m.x, "norm_ready")
            t.skip(a=1)
            heads = lambda v: v.rearrange("p (h k) -> p h k", h=H1)
            wide = lambda v: v.rearrange("p (h o) -> p h o", o=1).to_broadcast([P, H1, S])
            for i in range(NT + 1):
                yield 12 + CROSS_STEP * i
                if i >= 1:
                    j = (i - 1) % 2
                    t.w(t.s["e_ready"])
                    t.w.step(dve.tensor_reduce(t.m.sums[:, j, 0:H1], heads(t.m.e1[:, j, :]), X, ALU.add))
                    t.w.step(dve.reciprocal(t.m.rinv[:, j, 0:H1], t.m.sums[:, j, 0:H1]))
                    e = heads(t.m.e1[:, j, :])
                    dve.tensor_tensor(e, e, wide(t.m.rinv[:, j, 0:H1]), ALU.mult).then_inc(t.s["prob_ready"], 1)
                    t.skip(a=1)
                if i < NT:
                    if i >= 2:
                        dve.wait_ge(t.s["a_freed"], t.a.at - 1)
                    bank = t.v.take()
                    t.w.step(dve.tensor_reduce(t.m.mx[:, i % 2, 0:H1], heads(bank), X, ALU.max, negate=True))
                    dve.tensor_tensor(heads(t.m.e1[:, i % 2, :]), heads(bank), wide(t.m.mx[:, i % 2, 0:H1]), ALU.add)\
                        .then_inc(t.s["v_freed"], 1)
            yield CROSS_END - 8
            residual_vector(t, t.m.y_flat)
            norm_vector(t, t.m.x, t.m.y, "norm_ready")

        def cross_pool(t, inner):
            if inner:
                yield 1
                norm_pool(t)
            yield CROSS_END - 8
            norm_pool(t)
            t.skip(a=1 + NT, v=NT, o=1)

        def experts_tensor(t):
            pe = t.eng
            yield 0
            t.w(t.s["norm_ready"])
            turn_tensor(t, t.m.x)
            pe.wait_ge(t.s["a_freed"], t.a.at)
            bank = t.v.open()
            pe.matmul(bank[:, 0:NT * E], ones[0:1, :],
                      W("rows", "router").rearrange("p (o z) -> p o z", o=1).to_broadcast([1, NT, E]),
                      start=True, stop=False, skip_group_check=True)
            for i in range(NT):
                ins = pe.matmul(bank[:, i * E:(i + 1) * E], tok(t.m.xT[:, :], i), W("experts", "router"), start=False,
                                stop=(i == NT - 1), skip_group_check=True)
            ins.then_inc(t.s["v_filled"], 1)
            hid_at = {}
            for k in range(E + 2):
                yield 10 + EXPERT_STEP * k
                if k <= E:
                    t.w(t.s[f"expert{k % NE}_loaded"], 16)
                    for f in range(NF):
                        pe.matmul(t.a.open(), we[:, k % NE, f * P:(f + 1) * P], t.m.xT[:, :], start=True, stop=True)\
                            .then_inc(t.s["a_filled"], 1)
                    hid_at[k] = t.a.at
                if k == 0:
                    t.w(t.s["comb_ready"])
                    bank = t.a.open()
                    for i in range(NT):
                        ins = pe.transpose(tok(bank, i)[0:E + 1, :], t.m.comb[:, i, :], ident)
                    ins.then_inc(t.s["a_filled"], 1)
                    comb_at = t.a.at
                if k >= 1:
                    pe.wait_ge(t.s["a_freed"], hid_at[k - 1])
                    bank = t.v.open()
                    if k == 1:
                        pe.wait_ge(t.s["a_freed"], comb_at)
                        for i in range(NT):
                            pe.matmul(tok(bank, i), tok(t.m.combT[0:E + 1, :], i), W("experts", "b2")[0:E + 1, :],
                                      start=(i == 0), stop=False, skip_group_check=True)
                    for i in range(NT):
                        for f in range(NF):
                            ins = pe.matmul(tok(bank, i), tok(t.m.hid[:, (k - 1) % 2, f, :], i),
                                            we[:, (k - 1) % NE, FF + f * P:FF + (f + 1) * P],
                                            start=(k > 1 and i == 0 and f == 0), stop=(i == NT - 1 and f == NF - 1),
                                            skip_group_check=True)
                    ins.then_inc(t.s["v_filled"], 1)

        def experts_scalar(t):
            act = t.eng
            yield 0
            plain_scalar(t)
            t.skip(v=1)
            yield 6
            t.w(t.s["gap_ready"])
            act.activation(t.m.small[:, 1, 0:NT], t.m.small[:, 0, 0:NT], ACT.Exp).then_inc(t.s["ratio_ready"], 1)
            for k in range(E + 1):
                yield 10 + EXPERT_STEP * k
                for f in range(NF):
                    if k >= 2 and f == 0:
                        act.wait_ge(t.s["v_filled"], t.v.at)
                    c = k * NF + f
                    act.activation(t.m.hid[:, k % 2, f, :], t.a.take(), ACT.Gelu_apprx_tanh,
                                   bias=W("experts", "b1")[:, c:c + 1]).then_inc(t.s["a_freed"], 1)
                if k == 0:
                    act.activation(t.m.combT[0:E + 1, :], t.a.take()[0:E + 1, :], ACT.Copy).then_inc(t.s["a_freed"], 1)
                if k >= 1:
                    t.skip(v=1)
            t.skip(v=1)

        def experts_vector(t):
            dve = t.eng
            yield 0
            bank = t.v.take()
            dve.tensor_copy(t.m.lg[:, :, :].rearrange("p t e -> p (t e)"), bank[:, 0:NT * E]).then_inc(t.s["v_freed"], 1)
            dve.wait_ge(t.s["v_freed"], t.v.at)
            for i in range(NT):
                ins = dve.max(t.m.m8[:, i, :], t.m.lg[:, i, :])
            t.w.step(ins)
            dve.tensor_tensor(t.m.small[:, 0, 0:NT], t.m.m8[:, :, 1], t.m.m8[:, :, 0], ALU.subtract).then_inc(t.s["gap_ready"], 1)
            for i in range(NT):
                ins = dve.max_index(t.m.i8[:, i, :], t.m.m8[:, i, :], t.m.lg[:, i, :])
            t.w.step(ins)
            top = t.m.small[:, 2, 0:2 * NT].rearrange("p (t e) -> p t e", e=2)
            dve.tensor_copy(top, t.m.i8[:, :, 0:2])
            yield 10
            t.w(t.s["ratio_ready"])
            t.w.step(dve.tensor_scalar(t.m.small[:, 3, 0:NT], t.m.small[:, 1, 0:NT], 1.0, None, ALU.add))
            t.w.step(dve.reciprocal(t.m.small[:, 4, 0:NT], t.m.small[:, 3, 0:NT]))
            t.w.step(dve.tensor_tensor(t.m.small[:, 5, 0:NT], t.m.small[:, 4, 0:NT], t.m.small[:, 1, 0:NT], ALU.mult))
            wide = lambda v: v.rearrange("p (t o) -> p t o", o=1).to_broadcast([P, NT, E])
            iota = W("const", "iota").rearrange("p (o e) -> p o e", o=1).to_broadcast([P, NT, E])
            for n, dst in ((0, t.m.comb[:, :, 0:E]), (1, t.m.eqt[:, :, :])):
                t.w.step(dve.tensor_tensor(dst, iota, top[:, :, n:n + 1].to_broadcast([P, NT, E]), ALU.is_equal))
                t.w.step(dve.tensor_tensor(dst, dst, wide(t.m.small[:, 4 + n, 0:NT]), ALU.mult))
            dve.tensor_tensor(t.m.comb[:, :, 0:E], t.m.comb[:, :, 0:E], t.m.eqt[:, :, :], ALU.add).then_inc(t.s["comb_ready"], 1)
            for k in range(E + 1):
                yield 10 + EXPERT_STEP * (k + 1)
                bank = t.v.take()
                for i in range(NT):
                    if k == 0:
                        ins = dve.tensor_tensor(t.m.y[:, i, :], tok(bank, i), t.m.x[:, i, :], ALU.add)
                    else:
                        if i == 0:
                            dve.wait_ge(t.s["v_freed"], t.v.at - 1)
                        ins = dve.scalar_tensor_tensor(t.m.y[:, i, :], tok(bank, i), t.m.comb[:, i, k - 1:k],
                                                       t.m.y[:, i, :], ALU.mult, ALU.add)
                    if i == 0:
                        ins.then_inc(t.s["expert_done"], 1)
                ins.then_inc(t.s["v_freed"], 1)
            dve.wait_ge(t.s["v_freed"], t.v.at)
            t.skip(a=2 + (E + 1) * NF)
            yield EXPERTS_END - 18
            norm_vector(t, t.m.x, t.m.y, "norm_ready")

        def experts_pool(t):
            t.skip(v=1 + E + 1, a=2 + (E + 1) * NF)
            yield EXPERTS_END - 18
            norm_pool(t)
            t.eng.memset(t.m.vpad, 0.0)
            t.eng.memset(t.m.qpad, 0.0)
            t.eng.memset(t.m.kpad, 0.0).then_inc(t.s["pads_ready"], 1)

        class Band:

            def __init__(self, heads, mask, wide_values, step):
                self.heads, self.mask, self.wide, self.step = heads, mask, wide_values, step
                self.rows = 32 if wide_values == 32 else 64
                self.per = P // self.rows
                self.units = []
                for j in range(NT):
                    nk = 1 if j == 0 else 2
                    for i in range(self.per):
                        for g in range(0, heads // self.per, 4 // nk):
                            hh = [self.per * (g + a) + i for a in range(4 // nk)]
                            self.units.append((j, nk, hh))
                self.per_tile = [sum(1 for u in self.units if u[0] == j) for j in range(NT)]

            def last_of_tile(self, n):
                return n + 1 == len(self.units) or self.units[n + 1][0] != self.units[n][0]

            def cols(self, n):
                return sum(len(hh) for _, _, hh in self.units[:n]), len(self.units[n][2])

        def band_tensor(t, band, t0):
            pe, at = t.eng, {}
            pairs = lambda v, n, z: v.rearrange("p (o z) -> p o z", o=1).to_broadcast([P, n, z])
            U = len(band.units)
            for n in range(U + 3):
                yield t0 + band.step * n
                if n < U:
                    j, nk, hh = band.units[n]
                    bank = t.s_.open()
                    mask = cbv[band.mask][:, (2 - nk) * P:2 * P]
                    pe.matmul(bank, cbv["ident"], pairs(mask, len(hh), nk * P), start=True, stop=False,
                              skip_group_check=True)
                    for a, h in enumerate(hh):
                        g, r = h // band.per, band.rows * (h % band.per)
                        ins = pe.matmul(bank[:, a * nk * P:(a + 1) * nk * P],
                                        t.m.qT[r:r + band.rows, g, j * P:(j + 1) * P],
                                        t.m.kT[r:r + band.rows, g, (j + 1 - nk) * P:(j + 1) * P],
                                        start=False, stop=(a == len(hh) - 1), skip_group_check=True)
                    ins.then_inc(t.s["s_filled"], 1)
                if n >= 3:
                    m = n - 3
                    j, nk, hh = band.units[m]
                    pe.wait_ge(t.s["v_freed"], at[m])
                    if hh[0] == 0:
                        heads_bank = t.o.open()
                    for a, h in enumerate(hh):
                        g, r = h // band.per, band.rows * (h % band.per)
                        for c in range(nk):
                            tile = j + 1 - nk + c
                            if band.wide == 32:
                                v, o = t.m.vpad[:, tile, h, :], heads_bank[r:r + 32, 0:P]
                            else:
                                v, o = t.m.vv[:, tile, h * 64:(h + 1) * 64], tok(heads_bank, g)[r:r + 64, :]
                            ins = pe.matmul(o, v, t.m.pT[:, m % 2, (a * nk + c) * P:(a * nk + c + 1) * P],
                                            start=(g == 0 and c == 0),
                                            stop=(h >= band.heads - band.per and c == nk - 1),
                                            skip_group_check=True)
                    ins.then_inc(t.s["pT_used"], 1)
                if 2 <= n < U + 2:
                    t.w(t.s["prob_ready"])
                    bank = t.v.open()
                    for c in range(4):
                        ins = pe.transpose(tok(bank, c), tok(t.m.pr[:, (n - 2) % 3, :], c), ident)
                    ins.then_inc(t.s["v_filled"], 1)
                    at[n - 2] = t.v.at

        def band_scalar(t, band, t0):
            act = t.eng
            U = len(band.units)
            v0, p0 = t.v.at, t.w.asked.get(t.s["pT_used"].name, 0)
            for n in range(U + 3):
                yield t0 + band.step * n
                if n < U:
                    j, nk, hh = band.units[n]
                    c0, k = band.cols(n)
                    t.skip(s=1)
                    bank = t.s_.bank()
                    t.w(t.s["max_ready"])
                    if n >= 3:
                        act.wait_ge(t.s["v_filled"], v0 + n - 2)
                    for a in range(k):
                        z = slice(a * nk * P, (a + 1) * nk * P)
                        ins = act.activation(t.m.pr[:, n % 3, z], bank[:, z], ACT.Exp, bias=t.m.mx2[:, c0 + a:c0 + a + 1],
                                             accum_out=t.m.sums2[:, c0 + a:c0 + a + 1])
                    ins.then_inc(t.s["s_freed"], 1)
                if 2 <= n < U + 2:
                    t.skip(v=1)
                    if n % 2:
                        if n >= 4:
                            act.wait_ge(t.s["pT_used"], p0 + n - 3)
                        act.wait_ge(t.s["v_filled"], t.v.at)
                        act.activation(t.m.pT[:, n % 2, :], t.v.bank(), ACT.Copy).then_inc(t.s["v_freed"], 1)
                if n >= 3 and band.last_of_tile(n - 3):
                    j = band.units[n - 3][0]
                    t.w(t.s["pT_used"], band.per_tile[j])
                    t.skip(o=1)
                    if band.wide == 32:
                        act.activation(tok(t.m.oT[:, 0, :], j), t.o.bank()[:, 0:P], ACT.Copy).then_inc(t.s["o_freed"], 1)
                    else:
                        act.activation(t.m.oT[:, :, j * P:(j + 1) * P], t.o.bank().rearrange("p (g z) -> p g z", g=4),
                                       ACT.Copy).then_inc(t.s["o_freed"], 1)

        def band_vector(t, band, t0):
            dve = t.eng
            U = len(band.units)
            s0 = t.s_.at
            for n in range(U + 3):
                yield t0 + band.step * n
                if 1 <= n <= U:
                    c0, k = band.cols(n - 1)
                    dve.wait_ge(t.s["s_freed"], s0 + n)
                    t.w.step(dve.reciprocal(t.m.rinv2[:, c0:c0 + k], t.m.sums2[:, c0:c0 + k]))
                    nk = band.units[n - 1][1]
                    for a in range(k):
                        z = t.m.pr[:, (n - 1) % 3, a * nk * P:(a + 1) * nk * P]
                        ins = dve.tensor_scalar(z, z, t.m.rinv2[:, c0 + a:c0 + a + 1], None, ALU.mult)
                    ins.then_inc(t.s["prob_ready"], 1)
                if n < U:
                    j, nk, hh = band.units[n]
                    c0, k = band.cols(n)
                    bank = t.s_.take()
                    dve.tensor_reduce(t.m.mx2[:, c0:c0 + k], bank.rearrange("p (a z) -> p a z", a=k), X, ALU.max,
                                      negate=True).then_inc(t.s["max_ready"], 1)
                if 2 <= n < U + 2:
                    if n >= 4:
                        t.w(t.s["pT_used"])
                    if n % 2 == 0:
                        dve.tensor_copy(t.m.pT[:, n % 2, :], t.v.take()).then_inc(t.s["v_freed"], 1)
                    else:
                        t.skip(v=1)
            t.w(t.s["pT_used"], 2)
            t.skip(o=NT)

        window, local = Band(H3, "band3", 32, WINDOW_STEP), Band(H5, "band5", 64, LOCAL_STEP)
        WINDOW_BAND, LOCAL_BAND = 10 + ROPE_STEP * NT, 10 + QKV_STEP * (NT + 0.5)
        WINDOW_END = WINDOW_BAND + window.step * (len(window.units) + 3)
        LOCAL_END = LOCAL_BAND + local.step * (len(local.units) + 3)

        def turn_qk(t, q, k):
            for src in (q, k):
                bank = t.a.open()
                for g in range(4):
                    ins = t.eng.transpose(tok(bank, g), tok(src, g), ident)
                ins.then_inc(t.s["a_filled"], 1)

        def take_qk(t, i):
            for dst in (t.m.qT, t.m.kT):
                t.eng.activation(dst[:, :, i * P:(i + 1) * P], t.a.take().rearrange("p (g z) -> p g z", g=4),
                                 ACT.Copy).then_inc(t.s["a_freed"], 1)

        def window_tensor(t):
            pe = t.eng
            yield 0
            t.w(t.s["norm_ready"])
            turn_tensor(t, t.m.x)
            pe.wait_ge(t.s["a_freed"], t.a.at)
            bank = t.v.open()
            for i in range(NT):
                ins = pe.matmul(tok(bank, i), tok(t.m.xT[:, :], i), W("window", "w_v"), start=(i == 0), stop=(i == NT - 1),
                                skip_group_check=True)
            ins.then_inc(t.s["v_filled"], 1)
            for i in range(NT + 1):
                yield 4 + ROPE_STEP * i
                if i < NT:
                    pe.matmul(t.v.open(), tok(t.m.xT[:, :], i), W("window", "w_qk"), start=True, stop=True)\
                        .then_inc(t.s["v_filled"], 1)
                if i >= 1:
                    t.w(t.s["rope_ready"])
                    turn_qk(t, t.m.qpad[:, (i - 1) % 2, :], t.m.kpad[:, (i - 1) % 2, :])
            pe.wait_ge(t.s["a_freed"], t.a.at)
            yield from band_tensor(t, window, WINDOW_BAND)
            yield WINDOW_END
            pe.wait_ge(t.s["o_freed"], t.o.at)
            bank = t.o.open()
            pe.matmul(bank, ones[0:1, :], row("b_win"), start=True, stop=False, skip_group_check=True)
            for i in range(NT):
                ins = pe.matmul(tok(bank, i), tok(t.m.oT[:, 0, :], i), W("window", "w_o"), start=False,
                                stop=(i == NT - 1), skip_group_check=True)
            ins.then_inc(t.s["o_filled"], 1)

        def window_scalar(t):
            yield 0
            plain_scalar(t)
            for i in range(NT):
                yield 4 + ROPE_STEP * (i + 1)
                take_qk(t, i)
            t.skip(v=1 + NT)
            yield from band_scalar(t, window, WINDOW_BAND)
            t.skip(o=1)

        def window_vector(t):
            dve = t.eng
            yield 0
            t.w(t.s["pads_ready"])
            t.skip(a=1)
            bank = t.v.take().rearrange("p (t h d) -> p t h d", t=NT, h=H3)
            for g in range(4):
                for i in range(NT):
                    ins = dve.tensor_copy(t.m.vpad[:, i, 4 * g:4 * g + 4, 8 * g:8 * g + 8],
                                          bank[:, i, 4 * g:4 * g + 4, :])
            ins.then_inc(t.s["v_freed"], 1)
            rope = W("const", "rope3", t=NT, f=2, q=2)
            for i in range(NT):
                yield 4 + ROPE_STEP * i
                bank = t.v.take().rearrange("p (f q h d) -> p f q h d", f=2, q=2, h=H3)
                for f, dst in ((0, t.m.ra3), (1, t.m.rb3)):
                    for q in range(2):
                        by = rope[:, i, f, q:q + 1, :].to_broadcast([P, H3, DH3])
                        ins = dve.tensor_tensor(dst[:, i % 2, q * P:(q + 1) * P].rearrange("p (h d) -> p h d", h=H3),
                                                bank[:, f, q], by, ALU.mult)
                ins.then_inc(t.s["v_freed"], 1)
                dve.wait_ge(t.s["v_freed"], t.v.at)
                if i >= 2:
                    dve.wait_ge(t.s["a_freed"], t.a.at - 2)
                for q, dst in ((0, t.m.qpad), (1, t.m.kpad)):
                    h = lambda v: v[:, i % 2, q * P:(q + 1) * P].rearrange("p (h d) -> p h d", h=H3)
                    ins = dve.tensor_tensor(dst[:, i % 2, :].rearrange("p (h z) -> p h z", h=H3)[:, :, 0:DH3],
                                            h(t.m.ra3), h(t.m.rb3), ALU.add)
                ins.then_inc(t.s["rope_ready"], 1)
                t.skip(a=2)
            yield from band_vector(t, window, WINDOW_BAND)
            yield WINDOW_END + 4
            residual_vector(t, t.m.y_flat)
            norm_vector(t, t.m.x, t.m.y, "norm_ready")

        def window_pool(t):
            yield WINDOW_END + 4
            norm_pool(t)
            t.skip(a=1 + 2 * NT, v=1 + NT + len(window.units), s=len(window.units), o=NT + 1)

        def shift_scalar(t):
            bank = t.a.take()
            t.eng.activation(t.m.hT[0:64, :], bank[0:64, :], ACT.Copy)
            t.eng.activation(t.m.hT[64:P, 1:T], bank[64:P, 0:T - 1], ACT.Copy).then_inc(t.s["a_freed"], 1)

        def local_tensor(t, l):
            pe = t.eng
            w_qkv = W("local", "w_qkv", l=DEPTH)[:, l]
            yield 0
            if l == 0:
                t.w(t.s["norm_ready"])
            else:
                pe.wait_ge(t.s["o_freed"], t.o.at)
            turn_tensor(t, t.m.x)
            pe.wait_ge(t.s["a_freed"], t.a.at)
            for i in range(NT + 1):
                yield 4 + QKV_STEP * i
                if i < NT:
                    for c, ring, sig in ((0, t.a, "a_filled"), (1, t.a, "a_filled"), (2, t.v, "v_filled")):
                        pe.matmul(ring.open(), tok(t.m.hT, i), w_qkv[:, c * 512:(c + 1) * 512],
                                  start=True, stop=True).then_inc(t.s[sig], 1)
                if i >= 1:
                    t.w(t.s["rope_ready"])
                    turn_qk(t, t.m.ra[:, (i - 1) % 2, 0:512], t.m.ra[:, (i - 1) % 2, 512:1024])
            pe.wait_ge(t.s["a_freed"], t.a.at)
            yield from band_tensor(t, local, LOCAL_BAND)
            yield LOCAL_END
            pe.wait_ge(t.s["o_freed"], t.o.at)
            bank = t.o.open()
            w_o = W("local", "w_o", l=DEPTH, g=4)
            for i in range(NT):
                for g in range(4):
                    ins = pe.matmul(tok(bank, i), tok(t.m.oT[:, g, :], i), w_o[:, l, g, :],
                                    start=(i == 0 and g == 0), stop=(i == NT - 1 and g == 3), skip_group_check=True)
            ins.then_inc(t.s["o_filled"], 1)
            yield LOCAL_END + 4
            pe.wait_ge(t.s["o_freed"], t.o.at)
            turn_tensor(t, t.m.x)
            pe.wait_ge(t.s["a_freed"], t.a.at)
            pe.matmul(t.v.open(), mean_w, t.m.hT[:, :], start=True, stop=True).then_inc(t.s["v_filled"], 1)
            yield LOCAL_END + 10
            t.w(t.s["sq_ready"])
            pe.matmul(t.a.open(), mean_w, t.m.sq, start=True, stop=True).then_inc(t.s["a_filled"], 1)
            yield LOCAL_END + 18
            t.w(t.s["hn_ready"])
            w1 = W("local", "w1", l=DEPTH)[:, l]
            for c in range(NH):
                m = HC[c]
                pe.matmul(t.a.open()[0:m, :], w1[:, HID + c * P:HID + c * P + m], t.m.hc, start=True, stop=True)\
                    .then_inc(t.s["a_filled"], 1)
                pe.matmul(t.v.open()[0:m, :], w1[:, c * P:c * P + m], t.m.hc, start=True, stop=True)\
                    .then_inc(t.s["v_filled"], 1)
            bank = t.o.open()
            pe.matmul(bank, ones[0:1, :], row(f"b2_{l}"), start=True, stop=False, skip_group_check=True)
            w2 = W("local", "w2", l=DEPTH, c=NH)
            yield LOCAL_END + 28
            pe.wait_ge(t.s["v_freed"], t.v.at)
            for c in range(NH):
                for i in range(NT):
                    ins = pe.matmul(tok(bank, i), tok(t.m.uu[0:HC[c], c, :], i), w2[0:HC[c], l, c, :], start=False,
                                    stop=(i == NT - 1 and c == NH - 1), skip_group_check=True)
            ins.then_inc(t.s["o_filled"], 1)

        def local_scalar(t, l):
            act = t.eng
            yield 0
            shift_scalar(t)
            for i in range(NT + 1):
                yield 4 + QKV_STEP * i
                if i < NT:
                    if i >= 2:
                        t.w(t.s["rope_ready"])
                    for c in range(2):
                        bank, z = t.a.take(), slice(512 * c, 512 * c + 512)
                        act.activation(t.m.rb[:, i % 2, z], bank, ACT.Square)
                        act.activation(t.m.qk[:, i % 2, z], bank, ACT.Copy).then_inc(t.s["a_freed"], 1)
                    act.activation(t.m.vv[:, i, :], t.v.take(), ACT.Copy).then_inc(t.s["v_freed"], 1)
                    t.w(t.s["ss_ready"])
                    act.activation(t.m.small[:, 2 * (i % 2) + 1, 0:16], t.m.small[:, 2 * (i % 2), 0:16], ACT.Sqrt)\
                        .then_inc(t.s["root_ready"], 1)
                if i >= 1:
                    take_qk(t, i - 1)
            t.w(t.s["rope_ready"], 2)
            yield from band_scalar(t, local, LOCAL_BAND)
            t.skip(o=1)
            yield LOCAL_END + 4
            shift_scalar(t)
            t.skip(v=1)
            yield LOCAL_END + 10
            act.wait_ge(t.s["v_freed"], t.v.at)
            act.activation(t.m.sq, t.m.hc, ACT.Square).then_inc(t.s["sq_ready"], 1)
            act.activation(t.m.rst, t.a.take(), ACT.Ln, bias=eps).then_inc(t.s["a_freed"], 1)
            yield LOCAL_END + 13
            act.wait_ge(t.s["a_freed"], t.a.at)
            act.activation(t.m.rst, t.m.rst, ACT.Exp, scale=-0.5).then_inc(t.s["rst_ready"], 1)
            b1 = W("local", "b1", l=DEPTH, f=2)
            yield LOCAL_END + 18
            for c in range(NH):
                m = HC[c]
                act.activation(t.m.gg[0:m, c, :], t.a.take()[0:m, :], ACT.Gelu, bias=b1[0:m, l, 1, c:c + 1])\
                    .then_inc(t.s["a_freed"], 1)
            t.skip(v=NH, o=1)

        def local_vector(t, l):
            dve = t.eng
            yield 0
            t.skip(a=1)
            if l == 0:
                t.w.step(dve.tensor_copy(t.m.y_flat, t.m.x_flat))
            for i in range(NT):
                yield 4 + QKV_STEP * i
                j = i % 2
                t.skip(a=2, v=1)
                dve.wait_ge(t.s["a_freed"], t.a.at)
                ss = t.m.small[:, 2 * j, 0:16]
                h = lambda v: v[:, j, :].rearrange("p (h d) -> p h d", h=2 * H5)
                dve.tensor_reduce(ss, h(t.m.rb), X, ALU.add).then_inc(t.s["ss_ready"], 1)
                t.w(t.s["root_ready"])
                rn = t.m.small[:, 2 * j + 1, 0:16]
                t.w.step(dve.tensor_scalar(rn, rn, 1e-12, None, ALU.max))
                t.w.step(dve.reciprocal(rn, rn))
                rn = rn.rearrange("p (h o) -> p h o", o=1).to_broadcast([P, 2 * H5, DH5])
                t.w.step(dve.tensor_tensor(h(t.m.qk), h(t.m.qk), rn, ALU.mult))
                if i >= 2:
                    dve.wait_ge(t.s["a_freed"], ra_at)
                for q in range(2):
                    z = lambda v: v[:, j, q * 512:(q + 1) * 512].rearrange("p (h d) -> p h d", h=H5)
                    ins = dve.tensor_tensor(z(t.m.ra), z(t.m.qk), tab5[:, l, 2 * q, i:i + 1, :].to_broadcast([P, H5, DH5]), ALU.mult)
                    z = lambda v: v[:, j, q * 512:(q + 1) * 512].rearrange("p (h a d) -> p h a d", h=H5, a=2)
                    for a in range(2):
                        by = tab5[:, l, 2 * q + 1, i:i + 1, 32 * a:32 * a + 32].to_broadcast([P, H5, 32])
                        ins = dve.tensor_tensor(z(t.m.rb)[:, :, a, :], z(t.m.qk)[:, :, 1 - a, :], by, ALU.mult)
                t.w.step(ins)
                dve.tensor_tensor(t.m.ra[:, j, :], t.m.ra[:, j, :], t.m.rb[:, j, :], ALU.add).then_inc(t.s["rope_ready"], 1)
                if i >= 1:
                    t.skip(a=2)
                ra_at = t.a.at
            t.skip(a=2)
            yield from band_vector(t, local, LOCAL_BAND)
            yield LOCAL_END + 4
            residual_vector(t, t.m.x_flat)
            t.skip(a=1)
            dve.tensor_tensor(t.m.hc, t.m.hT[:, :], t.v.take(), ALU.subtract).then_inc(t.s["v_freed"], 1)
            t.skip(a=1)
            yield LOCAL_END + 14
            t.w(t.s["rst_ready"])
            t.w.step(dve.tensor_tensor(t.m.hc, t.m.hc, t.m.rst, ALU.mult))
            dve.tensor_scalar(t.m.hc, t.m.hc, W("local", "ln_g")[:, l:l + 1], W("local", "ln_b")[:, l:l + 1],
                              ALU.mult, ALU.add).then_inc(t.s["hn_ready"], 1)
            yield LOCAL_END + 18
            b1 = W("local", "b1", l=DEPTH, f=2)
            for c in range(NH):
                m = HC[c]
                t.skip(a=1)
                bank = t.v.take()
                dve.wait_ge(t.s["a_freed"], t.a.at)
                dve.scalar_tensor_tensor(t.m.uu[0:m, c, :], bank[0:m, :], b1[0:m, l, 0, c:c + 1], t.m.gg[0:m, c, :],
                                         ALU.add, ALU.mult).then_inc(t.s["v_freed"], 1)
            yield LOCAL_END + 32
            residual_vector(t, t.m.x_flat)
            if l == DEPTH - 1:
                t.w.step(dve.tensor_tensor(t.m.y_flat, t.m.y_flat, t.m.x_flat, ALU.add))
                norm_vector(t, t.m.x, t.m.y, "y_ready")

        def local_pool(t, l):
            yield 0
            if l == DEPTH - 1:
                yield LOCAL_END + 32
                norm_pool(t)
            t.skip(a=1 + 4 * NT + 2 + NH, v=NT + len(local.units) + 1 + NH, s=len(local.units), o=NT + 2)

        def turn(first, second):
            STAGES = list(LAGS)
            spans = dict(mamba=MAMBA_END, cross0=CROSS_END, experts=EXPERTS_END, window=WINDOW_END + 12,
                         cross1=CROSS_END, local0=LOCAL_END + GEGLU, local1=LOCAL_END + GEGLU)
            starts = {n: sum(spans[k] for k in STAGES[:i]) for i, n in enumerate(STAGES)}
            logs = []

            def both(eng, name, stages):
                lanes = [Lane(eng, sems_of[i], None if name == "pe" else name + "_step", ps[i], rows[i]) for i in (0, 1)]
                interleave(*(run(t, [(starts[n] + i * LAGS[n], g) for n, g in zip(STAGES, stages(t))])
                             for i, t in enumerate(lanes)))
                logs.append([t.log for t in lanes])

            with nc.Block() as block:
                @block.sync
                def _(sp):
                    batches = (first, second)
                    tokens = lambda v: v.rearrange("(t p) d -> p t d", p=P)
                    for b, m, d in zip(batches, rows, sems_of):
                        sp.dma_start(m.x[:, :, :], tokens(x_in[b])).then_inc(d["x_loaded"], 16)
                        sp.dma_start(m.folded[:, :], folded_dram[b]).then_inc(d["score_loaded"], 16)
                    for k in range(E + 1):
                        if k == NE:
                            for b, m, d in zip(batches, rows, sems_of):
                                sp.wait_ge(d["norm_ready"], 3)
                                sp.dma_start(m.folded[:, :], folded_dram[B + b]).then_inc(d["score_loaded"], 16)
                        if k >= NE:
                            for d in sems_of:
                                sp.wait_ge(d["expert_done"], k - NE + 1)
                        sp.dma_start(we[:, k % NE, :], experts_in[k]).then_inc(shared[f"expert{k % NE}_loaded"], 16)
                    for b, m, d in zip(batches, rows, sems_of):
                        sp.wait_ge(d["y_ready"], 1)
                        sp.dma_start(tokens(out[b]), m.x[:, :, :]).then_inc(d["stored"], 16)
                    for d in sems_of:
                        sp.wait_ge(d["stored"], 16)

                @block.gpsimd
                def _(pool):
                    both(pool, "pool",
                         lambda t: [mamba_pool(t), cross_pool(t, True), experts_pool(t), window_pool(t),
                                    cross_pool(t, False), local_pool(t, 0), local_pool(t, 1)])

                @block.scalar
                def _(act):
                    both(act, "act",
                         lambda t: [mamba_scalar(t), cross_scalar(t, DH1 ** -0.5, True), experts_scalar(t),
                                    window_scalar(t), cross_scalar(t, DH3 ** -0.5, False), local_scalar(t, 0),
                                    local_scalar(t, 1)])

                @block.vector
                def _(dve):
                    both(dve, "dve",
                         lambda t: [mamba_vector(t), cross_vector(t, True), experts_vector(t), window_vector(t),
                                    cross_vector(t, False), local_vector(t, 0), local_vector(t, 1)])

                @block.tensor
                def _(pe):
                    both(pe, "pe",
                         lambda t: [mamba_tensor(t), cross_tensor(t, True, row_x0), experts_tensor(t),
                                    window_tensor(t), cross_tensor(t, False, row("b_x1")), local_tensor(t, 0),
                                    local_tensor(t, 1)])
            assert all(v == logs[0] for v in logs), logs
            nc.sync.sem_clear(sems)
            nc.all_engine_barrier()

        with nc.Fori(0, B // 2) as b:
            turn(b, b + B // 2)


def shape_constants(group):
    c, f = {}, np.float32
    c["ident"] = np.eye(P, dtype=f)
    c["mean"] = np.full((P, P), 1.0 / P, f)
    t = np.arange(T, dtype=np.float64)
    inv = 1.0 / 10000.0 ** (np.arange(0, DH3, 2) / DH3)
    ang = (t[:, None] * inv[None]).astype(f).astype(np.float64)
    cos, sin = np.tile(np.cos(ang), 2), np.tile(np.sin(ang), 2)
    sin[:, :DH3 // 2] *= -1
    r = np.stack([np.stack([cos * DH3 ** -0.5, cos], 1), np.stack([sin * DH3 ** -0.5, sin], 1)], 1)
    c["rope3"] = r.reshape(NT, P, 2 * 2 * DH3).transpose(1, 0, 2).reshape(P, -1)
    half = np.arange(0, DH5, 2)
    inv = 1.0 / 10000.0 ** (half / DH5)
    ang = (t[:, None] * inv[None]).astype(f).astype(np.float64)
    cos, sin = np.tile(np.cos(ang), 2), np.tile(np.sin(ang), 2)
    sin[:, :DH5 // 2] *= -1
    base = (half + 0.4 * DH5) / (1.4 * DH5)
    scale = np.tile(base[None] ** ((t - T // 2) / 32.0)[:, None], 2)
    r = np.stack([cos * scale * 8.0, sin * scale * 8.0, cos / scale, sin / scale])
    c["tables"] = r.reshape(4, NT, P, DH5).transpose(2, 0, 1, 3).reshape(P, -1)
    p = np.arange(P)
    c["pair"] = (p[:, None] // 64 == np.arange(2)[None]).astype(f)
    c["head"] = (p[:, None] // DH3 == np.arange(H3)[None]).astype(f)
    c["iota"] = np.tile(np.arange(E, dtype=f), (P, 1))
    c["eps"] = np.full((P, 1), EPS, f)
    c["neg_half"] = np.full((P, 1), -0.5, f)
    c["one"] = np.ones((P, 1), f)
    return np.concatenate([np.asarray(c[n], f) for n in GROUPS[group]], axis=1)


def bf16_constants(bf16):
    q, k = np.arange(P)[:, None], np.arange(P)[None]
    band = lambda prev, cur: np.where(np.concatenate([prev, cur], 1), 0.0, NEG)
    sel = (np.arange(P)[:, None] % 32 == np.arange(2 * NS)[None]).astype(np.float32)
    parts = [np.eye(P), band(k >= q + 1, k <= q), band(k >= q + 64, (k <= q) & (q - k <= 64)), sel]
    return np.concatenate(parts, axis=1).astype(bf16)


def blocks(a, rows=P):
    n = a.shape[0] // rows
    return a.reshape(n, rows, -1).transpose(1, 0, 2).reshape(rows, -1)


def fill(a, rows=P):
    out = np.zeros((rows,) + a.shape[1:], a.dtype)
    out[:a.shape[0]] = a
    return out


def col(a):
    return np.asarray(a).reshape(-1, P).T


def spread(a):
    return np.broadcast_to(np.asarray(a).reshape(1, -1), (P, a.size))


def pack(w):
    g = {n: {} for n in GROUPS}
    m = g["mamba"]
    m["w_in"] = w["L0_attn_in_proj_w"].T
    m["conv_w"] = blocks(w["L0_attn_conv_w"][:, 0, :])
    m["norm_w"] = w["L0_attn_norm_w"][:, None]
    m["conv_b"] = col(w["L0_attn_conv_b"])
    xp = w["L0_attn_x_proj_w"]
    bc = xp[DTR:]
    m["x_bc"] = blocks(np.ascontiguousarray(np.concatenate([bc, bc, bc], 0).T))
    m["x_dt"] = blocks(np.ascontiguousarray(xp[:DTR].T))
    m["w_dt"] = fill(w["L0_attn_dt_proj_w"].T)
    m["b_dt"] = col(w["L0_attn_dt_proj_b"])
    m["a_log"] = blocks(w["L0_attn_A_log"])
    m["d_skip"] = col(w["L0_attn_D"])
    m["w_out"] = blocks(np.ascontiguousarray(w["L0_attn_out_proj_w"].T))
    c = g["cross0"]
    c["ctx"] = w["ctx_1024"].reshape(B * S, D).T
    c["w_qT"] = blocks(np.ascontiguousarray(w["L0_xattn_w_q"].T))
    c["w_k"] = w["L0_xattn_w_kv"][:, :1024]
    c["w_v"] = w["L0_xattn_w_kv"][:, 1024:]
    c["w_o"] = blocks(w["L0_xattn_w_out"])
    g["experts"]["gamma"] = col(w["L0_xattn_ln_gamma"])
    g["experts"]["beta"] = col(w["L0_xattn_ln_beta"])
    c["gate"] = spread(w["L0_xattn_gate"])
    c["w4_q"] = w["L1_xattn_Wq"]
    c["w4_k"] = w["L1_xattn_Wkv"][:D].T
    c["w4_v"] = w["L1_xattn_Wkv"][D:].T
    c["w4_o"] = w["L1_xattn_Wout"].T
    e = g["experts"]
    w1 = np.concatenate([w["L0_ffn_shared_w1"][None], w["L0_ffn_spec_w1"]], 0)
    b1 = np.concatenate([w["L0_ffn_shared_b1"][None], w["L0_ffn_spec_b1"]], 0)
    e["b1"] = col(b1)
    w2 = np.concatenate([w["L0_ffn_shared_w2"][None], w["L0_ffn_spec_w2"]], 0)
    w2 = w2.reshape(E + 1, D, NF, P).transpose(0, 3, 2, 1).reshape(E + 1, P, FF)
    experts = np.ascontiguousarray(np.concatenate([w1.transpose(0, 2, 1), w2], axis=2))
    e["router"] = w["L0_ffn_router_w"].T
    e["b2"] = fill(np.concatenate([w["L0_ffn_spec_b2"], w["L0_ffn_shared_b2"][None]], 0))
    h = DH3 // 2
    turned = lambda a: np.concatenate([a.reshape(H3, 2, h, D)[:, 1:], a.reshape(H3, 2, h, D)[:, :1]], 1).reshape(D, D)
    wq, wk = w["L1_attn_Wq"], w["L1_attn_Wk"]
    g["window"]["w_qk"] = np.concatenate([wq, wk, turned(wq), turned(wk)], 0).T
    g["window"]["w_v"] = w["L1_attn_Wv"].T
    g["window"]["w_o"] = w["L1_attn_Wo"].T.reshape(4, 4, DH3, D).transpose(1, 0, 2, 3).reshape(D, D)
    f = g["local"]
    f["w_qkv"] = w["L1_ffn_wqkv"].transpose(1, 0, 2).reshape(P, -1)
    qs, ks = w["L1_ffn_q_scale"], w["L1_ffn_k_scale"]
    swap = lambda a: np.concatenate([a[:, 32:], a[:, :32]], 1)
    c["scales"] = spread(np.stack([qs, swap(qs), ks, swap(ks)], 1))
    f["w_o"] = w["L1_ffn_wo"].reshape(DEPTH, 4, P, D).transpose(2, 0, 1, 3).reshape(P, -1)
    f["ln_g"], f["ln_b"] = w["L1_ffn_ln_g"].T, w["L1_ffn_ln_b"].T
    f["w1"] = w["L1_ffn_w1"].transpose(1, 0, 2).reshape(P, -1)
    b1 = np.zeros((DEPTH, 2, NH * P), np.float32)
    b1[:, :, :HID] = w["L1_ffn_b1"].reshape(DEPTH, 2, HID)
    f["b1"] = b1.reshape(DEPTH * 2 * NH, P).T
    w2 = np.zeros((DEPTH, NH * P, D), np.float32)
    w2[:, :HID] = w["L1_ffn_w2"]
    f["w2"] = w2.reshape(DEPTH * NH, P, D).transpose(1, 0, 2).reshape(P, -1)
    r = g["rows"]
    r["b_x0"], r["b_win"], r["b_x1"] = w["L0_xattn_b_out"][None], w["L1_attn_bo"][None], w["L1_xattn_bout"][None]
    r["b2_0"], r["b2_1"] = w["L1_ffn_b2"][0:1], w["L1_ffn_b2"][1:2]
    r["ones"] = np.ones((1, P), np.float32)
    r["router"] = w["L0_ffn_router_b"][None]
    out = {}
    for n, cols in GROUPS.items():
        if n in ("const", "rope5"):
            out[n] = shape_constants(n)
            continue
        for k, width in cols.items():
            assert g[n][k].shape == (ROWS.get(n, P), width), (n, k, g[n][k].shape, width)
        out[n] = np.ascontiguousarray(np.concatenate([g[n][k] for k in cols], axis=1))
    return out, experts


def kernel(**inputs):
    import concourse.bacc as bacc
    from concourse.bass_utils import run_bass_kernel_spmd

    w = {n: np.asarray(v) for n, v in inputs.items()}
    groups, experts = pack(w)
    arrays = {"in_" + n: v for n, v in groups.items()}
    arrays["in_expert_weights"] = experts
    arrays["in_x"] = np.ascontiguousarray(w["x"])
    arrays["in_bf16"] = bf16_constants(mybir.dt.np(BF16))
    nc = bacc.Bacc("TRN2", target_bir_lowering=False, num_devices=1)
    aps = {n: nc.dram_tensor(n, a.shape, mybir.dt.from_np(a.dtype), kind="ExternalInput").ap()
           for n, a in arrays.items()}
    out = nc.dram_tensor("out", (B, T, D), F32, kind="ExternalOutput").ap()
    folded_dram = nc.dram_tensor("folded_products", (2 * B, P, 1024), F32, kind="Internal").ap()
    decoder_kernel(nc, aps["in_x"], {g: aps["in_" + g] for g in GROUPS}, aps["in_bf16"],
                   aps["in_expert_weights"], folded_dram, out)
    r = run_bass_kernel_spmd(nc, [arrays], core_ids=[0])
    return r.results[0]["out"]
```
